# Optimizing a Trainium2 kernel written in Bass

```python
import numpy as np
import jax
import jax.numpy as jnp

def _softmax(x, axis=-1):
    return jax.nn.softmax(x, axis=axis)

def _gelu(x):
    return jax.nn.gelu(x, approximate=True)

def _silu(x):
    return jax.nn.silu(x)

def _sigmoid(x):
    return jax.nn.sigmoid(x)

def _layernorm(x, axis=-1, eps=1e-05):
    m = jnp.mean(x, axis=axis, keepdims=True)
    v = jnp.var(x, axis=axis, keepdims=True)
    return (x - m) / jnp.sqrt(v + eps)

def _scatter_add(tgt, idx, src, axis=0):
    return tgt.at[idx].add(src)

def _segment_sum(src, seg, n):
    return jax.ops.segment_sum(src, seg, n)
kernel_name = 'mk_adaln_d2_jaxref_r8_8eaafe'

def setup_inputs(seed: int=0):
    np.random.seed(seed)
    _w = jnp.asarray

    def _L0_attn_setup():
        import jax, jax.numpy as jnp
        import numpy as np
        B, S, DM = (2, 256, 256)
        H, KVH, HD = (16, 4, 128)
        REP = H // KVH
        ROPE_BASE = 10000.0
        EPS = 1e-06

        def _rope_tables(seq_len, dim):
            inv_freq = 1.0 / ROPE_BASE ** (jnp.arange(0, dim, 2, dtype=jnp.float32) / dim)
            t = jnp.arange(seq_len, dtype=jnp.float32)
            freqs = jnp.outer(t, inv_freq)
            emb = jnp.concatenate([freqs, freqs], -1)
            return (jnp.cos(emb), jnp.sin(emb))

        def _rotate_half(x):
            d = x.shape[-1] // 2
            return jnp.concatenate([-x[..., d:], x[..., :d]], axis=-1)
        key = jax.random.key(seed)
        k0, k1, k2, k3, k4 = jax.random.split(key, 5)
        w = lambda k, o, i: jax.random.normal(k, (o, i), jnp.float32) * (1.0 / np.sqrt(i))
        return {'x': jax.random.normal(k0, (B, S, DM), jnp.float32), 'Wq': w(k1, H * HD, DM), 'Wk': w(k2, KVH * HD, DM), 'Wv': w(k3, KVH * HD, DM), 'Wo': w(k4, DM, H * HD)}
    _L0_attn_in = _L0_attn_setup()

    def _L0_ffn_setup():
        import jax, jax.numpy as jnp
        import numpy as np

        def _sparsify_2to4(h):
            B, S, I = h.shape
            g = h.reshape(B, S, I // 4, 4)
            a = jnp.abs(g)
            _, idx = jax.lax.top_k(a, 2)
            pos = jnp.arange(4)
            mask = (pos == idx[..., 0:1]) | (pos == idx[..., 1:2])
            return (g * mask.astype(g.dtype)).reshape(B, S, I)
        key = jax.random.key(seed)
        k1, k2, k3, k4 = jax.random.split(key, 4)
        B, S, H, I = (4, 256, 256, 1024)
        x = jax.random.normal(k1, (B, S, H), dtype=jnp.float32)
        w_gate = jax.random.normal(k2, (H, I), dtype=jnp.float32) / np.sqrt(H)
        w_up = jax.random.normal(k3, (H, I), dtype=jnp.float32) / np.sqrt(H)
        w_down = jax.random.normal(k4, (I, H), dtype=jnp.float32) / np.sqrt(I)
        return {'x': x, 'w_gate': w_gate, 'w_up': w_up, 'w_down': w_down}
    _L0_ffn_in = _L0_ffn_setup()
    _L0_c = _w((lambda *s: np.random.randn(*s).astype(np.float32) * 0.05)(2, 256))
    _L0_wmod = _w((lambda *s: np.random.randn(*s).astype(np.float32) * 0.05)(256, 6 * 256) * 256 ** (-0.5))

    def _L1_attn_setup():
        import jax, jax.numpy as jnp
        import numpy as np
        from jax import lax
        H = 16
        MB = 16
        LR = 1.0
        ROPE_BASE = 10000.0
        LN_EPS = 1e-05

        def _rotate_half(u):
            u1, u2 = jnp.split(u, 2, axis=-1)
            return jnp.concatenate([-u2, u1], axis=-1)
        key = jax.random.key(seed)
        ks = jax.random.split(key, 4)
        B, S, D = (4, 512, 256)
        x = jax.random.normal(ks[0], (B, S, D), dtype=jnp.float32)
        scale = 1.0 / np.sqrt(D)
        Wk = jax.random.normal(ks[1], (D, D), dtype=jnp.float32) * scale
        Wv = jax.random.normal(ks[2], (D, D), dtype=jnp.float32) * scale
        Wo = jax.random.normal(ks[3], (D, D), dtype=jnp.float32) * scale
        ln_gamma = jnp.ones((D,), dtype=jnp.float32)
        ln_beta = jnp.zeros((D,), dtype=jnp.float32)
        return {'x': x, 'Wk': Wk, 'Wv': Wv, 'Wo': Wo, 'ln_gamma': ln_gamma, 'ln_beta': ln_beta}
    _L1_attn_in = _L1_attn_setup()

    def _L1_ffn_setup():
        import jax, jax.numpy as jnp
        import numpy as np
        K = 2

        def gelu(v):
            return jax.nn.gelu(v, approximate=False)
        key = jax.random.key(seed)
        ks = jax.random.split(key, 10)
        B, S, D, H, E = (4, 256, 256, 128, 8)
        SH = 2 * H
        u = lambda k_, shape, b: jax.random.uniform(k_, shape, jnp.float32, -b, b)
        return {'x': jax.random.normal(ks[0], (B, S, D), jnp.float32), 'gate_w': u(ks[1], (D, E), 1.0 / D), 'w1': u(ks[2], (E, D, H), 1.0 / D), 'b1': u(ks[3], (E, H), 1.0 / np.sqrt(D)), 'w2': u(ks[4], (E, H, D), 1.0 / H), 'b2': u(ks[5], (E, D), 1.0 / np.sqrt(H)), 'shared_w1': u(ks[6], (D, SH), 1.0 / D), 'shared_b1': u(ks[7], (SH,), 1.0 / np.sqrt(D)), 'shared_w2': u(ks[8], (SH, D), 1.0 / SH), 'shared_b2': u(ks[9], (D,), 1.0 / np.sqrt(SH))}
    _L1_ffn_in = _L1_ffn_setup()
    _L1_c = _w((lambda *s: np.random.randn(*s).astype(np.float32) * 0.05)(2, 256))
    _L1_wmod = _w((lambda *s: np.random.randn(*s).astype(np.float32) * 0.05)(256, 6 * 256) * 256 ** (-0.5))
    _d = {'L0_attn_x': _L0_attn_in['x'], 'L0_attn_Wq': _L0_attn_in['Wq'], 'L0_attn_Wk': _L0_attn_in['Wk'], 'L0_attn_Wv': _L0_attn_in['Wv'], 'L0_attn_Wo': _L0_attn_in['Wo'], 'L0_ffn_w_gate': _L0_ffn_in['w_gate'], 'L0_ffn_w_up': _L0_ffn_in['w_up'], 'L0_ffn_w_down': _L0_ffn_in['w_down'], 'L0_c': _L0_c, 'L0_wmod': _L0_wmod, 'L1_attn_Wk': _L1_attn_in['Wk'], 'L1_attn_Wv': _L1_attn_in['Wv'], 'L1_attn_Wo': _L1_attn_in['Wo'], 'L1_attn_ln_gamma': _L1_attn_in['ln_gamma'], 'L1_attn_ln_beta': _L1_attn_in['ln_beta'], 'L1_ffn_gate_w': _L1_ffn_in['gate_w'], 'L1_ffn_w1': _L1_ffn_in['w1'], 'L1_ffn_b1': _L1_ffn_in['b1'], 'L1_ffn_w2': _L1_ffn_in['w2'], 'L1_ffn_b2': _L1_ffn_in['b2'], 'L1_ffn_shared_w1': _L1_ffn_in['shared_w1'], 'L1_ffn_shared_b1': _L1_ffn_in['shared_b1'], 'L1_ffn_shared_w2': _L1_ffn_in['shared_w2'], 'L1_ffn_shared_b2': _L1_ffn_in['shared_b2'], 'L1_c': _L1_c, 'L1_wmod': _L1_wmod}
    _x0 = _d['L0_attn_x']
    _d['L0_attn_x'] = jax.random.normal(jax.random.fold_in(jax.random.key(seed), 1), (2, 1024, 256), dtype=_x0.dtype)
    del _x0
    return _d

def reference(L0_attn_x, L0_attn_Wq, L0_attn_Wk, L0_attn_Wv, L0_attn_Wo, L0_ffn_w_gate, L0_ffn_w_up, L0_ffn_w_down, L0_c, L0_wmod, L1_attn_Wk, L1_attn_Wv, L1_attn_Wo, L1_attn_ln_gamma, L1_attn_ln_beta, L1_ffn_gate_w, L1_ffn_w1, L1_ffn_b1, L1_ffn_w2, L1_ffn_b2, L1_ffn_shared_w1, L1_ffn_shared_b1, L1_ffn_shared_w2, L1_ffn_shared_b2, L1_c, L1_wmod):

    def _L0_attn_ref(x, Wq, Wk, Wv, Wo):
        import jax, jax.numpy as jnp
        import numpy as np
        B, S, DM = (2, 256, 256)
        H, KVH, HD = (16, 4, 128)
        REP = H // KVH
        ROPE_BASE = 10000.0
        EPS = 1e-06

        def _rope_tables(seq_len, dim):
            inv_freq = 1.0 / ROPE_BASE ** (jnp.arange(0, dim, 2, dtype=jnp.float32) / dim)
            t = jnp.arange(seq_len, dtype=jnp.float32)
            freqs = jnp.outer(t, inv_freq)
            emb = jnp.concatenate([freqs, freqs], -1)
            return (jnp.cos(emb), jnp.sin(emb))

        def _rotate_half(x):
            d = x.shape[-1] // 2
            return jnp.concatenate([-x[..., d:], x[..., :d]], axis=-1)
        bsz, seq_len, _ = x.shape
        q = (x @ Wq.T).reshape(bsz, seq_len, H, HD).transpose(0, 2, 1, 3)
        k = (x @ Wk.T).reshape(bsz, seq_len, KVH, HD).transpose(0, 2, 1, 3)
        v = (x @ Wv.T).reshape(bsz, seq_len, KVH, HD).transpose(0, 2, 1, 3)
        cos, sin = _rope_tables(seq_len, HD)
        cos, sin = (cos[None, None], sin[None, None])
        q = q * cos + _rotate_half(q) * sin
        k = k * cos + _rotate_half(k) * sin
        k = jnp.repeat(k, REP, axis=1)
        v = jnp.repeat(v, REP, axis=1)
        qf = jax.nn.elu(q) + 1.0
        kf = jax.nn.elu(k) + 1.0
        qf_t = qf.transpose(2, 0, 1, 3)
        kf_t = kf.transpose(2, 0, 1, 3)
        v_t = v.transpose(2, 0, 1, 3)

        def step(carry, inp):
            state, z = carry
            q_s, k_s, v_s = inp
            state = state + k_s[..., :, None] * v_s[..., None, :]
            z = z + k_s
            num = jnp.einsum('bhe,bhed->bhd', q_s, state)
            den = jnp.einsum('bhe,bhe->bh', q_s, z)[..., None] + EPS
            return ((state, z), num / den)
        init = (jnp.zeros((bsz, H, HD, HD), x.dtype), jnp.zeros((bsz, H, HD), x.dtype))
        _, out = jax.lax.scan(step, init, (qf_t, kf_t, v_t))
        out = out.transpose(1, 0, 2, 3).reshape(bsz, seq_len, H * HD)
        return out @ Wo.T

    def _L0_ffn_ref(x, w_gate, w_up, w_down):
        import jax, jax.numpy as jnp
        import numpy as np

        def _sparsify_2to4(h):
            B, S, I = h.shape
            g = h.reshape(B, S, I // 4, 4)
            a = jnp.abs(g)
            _, idx = jax.lax.top_k(a, 2)
            pos = jnp.arange(4)
            mask = (pos == idx[..., 0:1]) | (pos == idx[..., 1:2])
            return (g * mask.astype(g.dtype)).reshape(B, S, I)
        h = jax.nn.silu(jnp.einsum('bsh,hi->bsi', x, w_gate)) * jnp.einsum('bsh,hi->bsi', x, w_up)
        h_sparse = _sparsify_2to4(h)
        return jnp.einsum('bsi,ih->bsh', h_sparse, w_down)

    def _L1_attn_ref(x, Wk, Wv, Wo, ln_gamma, ln_beta):
        import jax, jax.numpy as jnp
        import numpy as np
        from jax import lax
        H = 16
        MB = 16
        LR = 1.0
        ROPE_BASE = 10000.0
        LN_EPS = 1e-05

        def _rotate_half(u):
            u1, u2 = jnp.split(u, 2, axis=-1)
            return jnp.concatenate([-u2, u1], axis=-1)
        B, S, Dm = x.shape
        Dh = Dm // H
        k = (x @ Wk.T).reshape(B, S, H, Dh).transpose(0, 2, 1, 3)
        v = (x @ Wv.T).reshape(B, S, H, Dh).transpose(0, 2, 1, 3)
        inv_freq = 1.0 / ROPE_BASE ** (jnp.arange(0, Dh, 2, dtype=jnp.float32) / Dh)
        t = jnp.arange(S, dtype=jnp.float32)
        freqs = t[:, None] * inv_freq[None, :]
        emb = jnp.concatenate([freqs, freqs], axis=-1)
        cos, sin = (jnp.cos(emb), jnp.sin(emb))
        k = k * cos + _rotate_half(k) * sin
        nmb = S // MB
        k_c = k.reshape(B, H, nmb, MB, Dh).transpose(2, 0, 1, 3, 4)
        v_c = v.reshape(B, H, nmb, MB, Dh).transpose(2, 0, 1, 3, 4)
        W0 = jnp.broadcast_to(jnp.eye(Dh, dtype=x.dtype), (B, H, Dh, Dh))
        inv_n = 2.0 / (MB * Dh)

        def step(W, kv):
            kc, vc = kv
            z = jnp.einsum('bhsd,bhde->bhse', kc, W)
            grad = jnp.einsum('bhsd,bhse->bhde', kc, (z - vc) * inv_n)
            return (W - LR * grad, z)
        _, zs = lax.scan(step, W0, (k_c, v_c))
        out = zs.transpose(1, 2, 0, 3, 4).reshape(B, H, S, Dh)
        out = out.transpose(0, 2, 1, 3).reshape(B, S, Dm)
        mu = jnp.mean(out, axis=-1, keepdims=True)
        var = jnp.var(out, axis=-1, keepdims=True)
        out = (out - mu) * lax.rsqrt(var + LN_EPS) * ln_gamma + ln_beta
        return out @ Wo.T

    def _L1_ffn_ref(x, gate_w, w1, b1, w2, b2, shared_w1, shared_b1, shared_w2, shared_b2):
        import jax, jax.numpy as jnp
        import numpy as np
        K = 2

        def gelu(v):
            return jax.nn.gelu(v, approximate=False)
        B, S, D = x.shape
        E = gate_w.shape[1]
        xf = x.reshape(-1, D)
        logits = xf @ gate_w
        top_logits, top_idx = jax.lax.top_k(logits, K)
        top_gates = jax.nn.softmax(top_logits, axis=-1)
        gates = jnp.sum(jax.nn.one_hot(top_idx, E, dtype=xf.dtype) * top_gates[..., None], axis=1)
        h = gelu(jnp.einsum('nd,edh->neh', xf, w1) + b1)
        out_e = jnp.einsum('neh,ehd->ned', h, w2) + b2
        routed = jnp.einsum('ne,ned->nd', gates, out_e)
        shared = gelu(xf @ shared_w1 + shared_b1) @ shared_w2 + shared_b2
        return (routed + shared).reshape(B, S, D)
    x = L0_attn_x
    mod = (_silu(L0_c) @ L0_wmod).reshape(L0_c.shape[0], 6, 1, -1)
    sa, ca, ga, sb, cb, gb = (mod[:, 0], mod[:, 1], mod[:, 2], mod[:, 3], mod[:, 4], mod[:, 5])
    ga = (2 * (ga >= 0) - 1) * jnp.maximum(jnp.abs(ga), 0.25)
    gb = (2 * (gb >= 0) - 1) * jnp.maximum(jnp.abs(gb), 0.25)
    h = _layernorm(x, axis=-1) * (1 + ca) + sa
    x = x + ga * _L0_attn_ref(h, L0_attn_Wq, L0_attn_Wk, L0_attn_Wv, L0_attn_Wo)
    h = _layernorm(x, axis=-1) * (1 + cb) + sb
    x = x + gb * _L0_ffn_ref(h, L0_ffn_w_gate, L0_ffn_w_up, L0_ffn_w_down)
    mod = (_silu(L1_c) @ L1_wmod).reshape(L1_c.shape[0], 6, 1, -1)
    sa, ca, ga, sb, cb, gb = (mod[:, 0], mod[:, 1], mod[:, 2], mod[:, 3], mod[:, 4], mod[:, 5])
    ga = (2 * (ga >= 0) - 1) * jnp.maximum(jnp.abs(ga), 0.25)
    gb = (2 * (gb >= 0) - 1) * jnp.maximum(jnp.abs(gb), 0.25)
    h = _layernorm(x, axis=-1) * (1 + ca) + sa
    x = x + ga * _L1_attn_ref(h, L1_attn_Wk, L1_attn_Wv, L1_attn_Wo, L1_attn_ln_gamma, L1_attn_ln_beta)
    h = _layernorm(x, axis=-1) * (1 + cb) + sb
    x = x + gb * _L1_ffn_ref(h, L1_ffn_gate_w, L1_ffn_w1, L1_ffn_b1, L1_ffn_w2, L1_ffn_b2, L1_ffn_shared_w1, L1_ffn_shared_b1, L1_ffn_shared_w2, L1_ffn_shared_b2)
    return x

_drawn_inputs = setup_inputs


def setup_inputs(seed=0):
    import zlib

    import numpy as np

    out = dict(_drawn_inputs(seed))
    spreads = {'L1_attn_ln_gamma': (1.0, 0.2), 'L1_attn_ln_beta': (0.0, 0.345)}
    factors = {'L0_attn_Wq': 177.171,
     'L0_attn_Wk': 64.0,
     'L1_ffn_gate_w': 7.644,
     'L1_ffn_w1': 40.866,
     'L1_ffn_b1': 41.718,
     'L1_ffn_w2': 29.163,
     'L1_ffn_b2': 6.339,
     'L1_ffn_shared_w1': 41.481,
     'L1_ffn_shared_b1': 43.678,
     'L1_ffn_shared_w2': 30.255,
     'L1_ffn_shared_b2': 6.334}
    for name, (base, spread) in spreads.items():
        noise = np.random.default_rng([zlib.crc32(name.encode()), seed]).standard_normal(out[name].shape)
        drawn = base * np.exp(spread * noise) if base else spread * noise
        out[name] = jnp.asarray(drawn.astype(out[name].dtype))
    for name, factor in factors.items():
        out[name] = (out[name] * factor).astype(out[name].dtype)
    return out
```

```python
from contextlib import ExitStack

import numpy as np

import concourse.bass as bass
from concourse import mybir

F32 = mybir.dt.float32
F32R = mybir.dt.float32r
BF16 = mybir.dt.bfloat16
U32 = mybir.dt.uint32
ALU = mybir.AluOpType
ACT = mybir.ActivationFunctionType
AX = mybir.AxisListType

P = 128
B, S, D = 2, 1024, 256
KD = D // P
NC = S // P
NT = B * NC
LN_EPS = 1e-5

H, KVH, HD = 16, 4, 128
REP = H // KVH
GW = REP * HD
QKV = (H + 2 * KVH) * HD
DEN_EPS = 1e-6
VW = HD + 1

FI = 1024
NM = FI // P
TH = 16
TD = D // TH
MB = 16
NMB = P // MB
INV_N = 2.0 / (MB * TD)
E, EH = 8, 128
GT = 4
NG = NT // GT

SA, CA, GA, SB_, CB, GB = range(6)


def at(c, b, per, k):
    return c * (2 * per) + (per * b + k)


def build(nc, a, out):
    with ExitStack() as keep:
        Program(nc, a, out, keep).run()


class Program:
    def __init__(self, nc, a, out, keep):
        self.nc, self.a, self.out, self.keep = nc, a, out, keep

    def sem(self, name):
        return self.keep.enter_context(self.nc.semaphore(name))

    def run(self):
        nc = self.nc

        def sb(name, shape, dt=F32):
            return self.keep.enter_context(nc.sbuf_tensor(name, shape, dt))

        self.x = sb("x_sb", [P, NT, D])
        self.ident = sb("ident", [P, P])
        self.mod_t = sb("mod_t", [P, 2, 6 * KD, B])
        self.gate_b = sb("gate_b", [P, 2, 2, B, D])
        self.half = sb("minus_half", [P, 1])
        self.eps = sb("eps", [P, 1])
        self.setup_phase()
        self.attention_phase()
        self.ffn_phase()
        self.scan_phase()
        self.moe_phase()

    def setup_phase(self):
        nc, a = self.nc, self.a
        x, ident, mod_t, gate_b, half, eps = self.x, self.ident, self.mod_t, self.gate_b, self.half, self.eps
        with ExitStack() as ctx:
            def sb(name, shape, dt=F32):
                return ctx.enter_context(nc.sbuf_tensor(name, shape, dt))

            def ps(name, shape, dt=F32):
                return ctx.enter_context(nc.psum_tensor(name, shape, dt))

            wmod = sb("wmod_sb", [P, 2, KD, 6 * D])
            cond = sb("cond", [P, 2, KD, B])
            scond = sb("silu_cond", [P, 2, KD, B])
            sbro = sb("silu_cond_wide", [P, 2 * KD * B, P])
            gmag = sb("gate_magnitude", [P, 2 * B, D])
            gneg = sb("gate_sign", [P, 2 * B, D])
            pm = ps("mod_ps", [P, 2, 512])
            pg = ps("gate_ps", [P, 4, 512])

            x_in, cond_in, wmod_in = self.sem("x_in"), self.sem("cond_in"), self.sem("wmod_in")
            const_made, silu_done, wide_done = self.sem("const_made"), self.sem("silu_done"), self.sem("wide_done")
            mod_full, gate_full, gate_step = self.sem("mod_full"), self.sem("gate_full"), self.sem("gate_step")
            ident_zero = self.sem("ident_zero")
            gate_free = self.sem("gate_free")
            self.x_in, self.const_made, self.gate_step = x_in, const_made, gate_step

            block = ctx.enter_context(nc.Block())

            @block.sync
            def _(sp):
                sp.dma_start(cond[:], a["cond"]).then_inc(cond_in, 16)
                for l in range(2):
                    sp.dma_start(wmod[:, l], a["wmod"][l].rearrange("(k p) n -> p k n", p=P)).then_inc(wmod_in, 16)
                sp.dma_start(x[:], a["x"].rearrange("b (c p) d -> p (b c) d", p=P)).then_inc(x_in, 16)
                sp.wait_ge(x_in, 16)

            @block.gpsimd
            def _(pool):
                pool.memset(ident[:], 0.0).then_inc(ident_zero, 1)
                pool.memset(half[:], -0.5)
                pool.memset(eps[:], LN_EPS)
                pool.wait_ge(ident_zero, 1)
                pool.affine_select(out=ident[:], in_=ident[:], compare_op=ALU.not_equal, fill=1.0, base=0,
                                   pattern=[[-1, P]], channel_multiplier=1).then_inc(const_made, 1)

            @block.scalar
            def _(act):
                act.wait_ge(cond_in, 16)
                act.activation(scond[:], cond[:], ACT.Silu).then_inc(silu_done, 1)

            @block.vector
            def _(dve):
                dve.wait_ge(silu_done, 1)
                dve.tensor_copy(sbro[:], scond[:].rearrange("p l k b -> p (l k b)").unsqueeze(2)
                                .broadcast_to([P, 2 * KD * B, P])).then_inc(wide_done, 1)
                n = 0
                for l in range(2):
                    dve.wait_ge(mod_full, l + 1)
                    m = mod_t[:, l]
                    dve.tensor_copy(m, pm[:, l, 0:6 * KD * B].rearrange("p (m b) -> p m b", b=B)).then_inc(gate_step, 1)
                    n += 1
                    dve.wait_ge(gate_step, n)
                    for kind in (CA, CB):
                        v = mod_t[:, l, kind * KD:(kind + 1) * KD]
                        dve.tensor_scalar(v, v, 1.0, None, ALU.add).then_inc(gate_step, 1)
                        n += 1
                    dve.wait_ge(gate_full, l + 1)
                    g = pg[:, :, 0:D]
                    dve.tensor_scalar(gneg[:], g, 0.0, 2.0, ALU.is_ge, ALU.mult).then_inc(gate_step, 1)
                    dve.tensor_scalar(gmag[:], g, -1.0, None, ALU.mult).then_inc(gate_step, 1)
                    n += 2
                    dve.wait_ge(gate_step, n)
                    dve.tensor_tensor(gmag[:], g, gmag[:], ALU.max).then_inc(gate_step, 1)
                    n += 1
                    dve.wait_ge(gate_step, n)
                    dve.tensor_scalar(gmag[:], gmag[:], 0.25, None, ALU.max).then_inc(gate_step, 1)
                    n += 1
                    dve.wait_ge(gate_step, n)
                    dve.scalar_tensor_tensor(gate_b[:, l].rearrange("p g b d -> p (g b) d"), gneg[:], -1.0, gmag[:],
                                             ALU.add, ALU.mult).then_inc(gate_free, 1)
                    dve.wait_ge(gate_free, l + 1)

            @block.tensor
            def _(pe):
                pe.wait_ge(wide_done, 1)
                for l in range(2):
                    pe.wait_ge(wmod_in, 16 * 2)
                    for m in range(6 * KD):
                        for k in range(KD):
                            mm = pe.matmul(pm[:, l, m * B:(m + 1) * B], wmod[:, l, k, m * P:(m + 1) * P],
                                           scond[:, l, k, :], start=(m == 0 and k == 0), stop=(k == KD - 1),
                                           skip_group_check=True)
                    mm.then_inc(mod_full, 1)
                    if l:
                        pe.wait_ge(gate_free, l)
                    for i, kind in enumerate((GA, GB)):
                        for b in range(B):
                            for k in range(KD):
                                mm = pe.matmul(pg[:, i * B + b, 0:D], sbro[:, (l * KD + k) * B + b, :],
                                               wmod[:, l, k, kind * D:(kind + 1) * D], start=(k == 0), stop=(k == KD - 1))
                    mm.then_inc(gate_full, 1)

    def attention_phase(self):
        nc, a = self.nc, self.a
        x, ident, mod_t, gate_b, half, eps = self.x, self.ident, self.mod_t, self.gate_b, self.half, self.eps
        WCH = 512
        NW = QKV // WCH
        RI = 1 + KVH
        with ExitStack() as ctx:
            def sb(name, shape, dt=F32):
                return ctx.enter_context(nc.sbuf_tensor(name, shape, dt))

            def ps(name, shape, dt=F32):
                return ctx.enter_context(nc.psum_tensor(name, shape, dt))

            stage = sb("a_stage", [P, 2, KD, WCH])
            w_hi, w_lo = sb("wqkv_hi", [P, KD, QKV], F32R), sb("wqkv_lo", [P, KD, QKV], F32R)
            wo = sb("wo_sb", [P, H, D])
            cos, sin = sb("cos_sb", [P, NC, HD // 2]), sb("sin_sb", [P, NC, HD])
            causal = sb("causal", [P, P])
            stats, mv = sb("a_stats", [P, 2, 6]), sb("a_mv", [P, 2, 2])
            rstd, veps = sb("a_rstd", [P, 2]), sb("a_veps", [P, 2])
            xn = sb("a_xn", [P, 2, D])
            h = sb("a_h", [P, 2, KD, P])
            h_hi, h_lo = sb("a_h_hi", [P, 2, KD, P], F32R), sb("a_h_lo", [P, 2, KD, P], F32R)
            t1, t2 = sb("rope_cos", [P, 2, GW]), sb("rope_sin", [P, 2, GW])
            y, ex = sb("rope_sum", [P, 2, GW]), sb("rope_exp", [P, 2, GW])
            feat = sb("feat", [P, 2, RI, GW])
            k_t, q_t = sb("k_t", [P, KVH, P]), sb("q_t", [P, KVH, REP * P])
            v = sb("v_ones", [P, 2, KVH, VW])
            am = sb("score_masked", [P, 2, REP * P])
            on = sb("attn_out", [P, 2, GW])
            o_t = sb("attn_out_t", [P, H, P])
            state = sb("state", [P, 2, KVH, VW])
            den, rden = sb("den", [P, REP]), sb("rden", [P, REP])
            dx = sb("a_dx", [P, D])

            proj = ps("proj", [P, 2, 512])
            turn = ps("turn", [P, 2, 512])
            score = ps("score", [P, 2, 512])
            num = ps("num", [P, 2, 512])

            names = ("w_in wo_in tab_in w_split w_used causal_made stat_done aggr_done veps_done rstd_done xn_done "
                     "hi_done hl_done proj_full proj_free turn_full turn_free score_full score_free num_full num_free "
                     "y_done relu_done exp_done feat_done den_done rden_done dx_done x_done cos_done mask_one")
            s = {n: self.sem("a_" + n) for n in names.split()}
            w_inb = [self.sem(f"a_w_in{i}") for i in range(2)]
            block = ctx.enter_context(nc.Block())

            def proj_item(c, b, j):
                return at(c, b, 7, 6 + j)

            def turn_item(c, b, j):
                return at(c, b, 10, 2 + j - (1 if last(c, b) else 0))

            def last(c, b):
                return isinstance(c, int) and c == NC - 1 and b == 1

            def walk(engine, step):
                with engine.Fori(0, NC - 1) as c:
                    step(c, 0, True, True)
                    step(c, 1, True, True)
                step(NC - 1, 0, True, False)
                step(NC - 1, 1, False, False)

            @block.sync
            def _(sp):
                for i in range(NW):
                    if i >= 2:
                        sp.wait_ge(s["w_split"], 2 * (i - 1))
                    sp.dma_start(stage[:, i % 2], a["wqkv"][:, i * WCH:(i + 1) * WCH]
                                 .rearrange("(k p) n -> p k n", p=P)).then_inc(w_inb[i % 2], 16)
                    if i == 0:
                        sp.dma_start(cos[:], a["cos"].rearrange("(c p) d -> p c d", p=P)).then_inc(s["tab_in"], 16)
                        sp.dma_start(sin[:], a["sin"].rearrange("(c p) d -> p c d", p=P)).then_inc(s["tab_in"], 16)
                sp.dma_start(wo[:], a["wo"].rearrange("(h p) n -> p h n", p=P)).then_inc(s["wo_in"], 16)

            @block.gpsimd
            def _(pool):
                pool.memset(causal[:], 1.0).then_inc(s["mask_one"], 1)
                pool.wait_ge(s["mask_one"], 1)
                pool.affine_select(out=causal[:], in_=causal[:], compare_op=ALU.is_ge, fill=0.0, base=0,
                                   pattern=[[1, P]], channel_multiplier=-1).then_inc(s["causal_made"], 1)

                def rstd_of(n, b):
                    pool.wait_ge(s["aggr_done"], n)
                    pool.tensor_tensor(veps[:, b:b + 1], mv[:, b, 1:2], eps[:], ALU.add).then_inc(s["veps_done"], 1)
                    pool.wait_ge(s["veps_done"], n)
                    pool.tensor_tensor(rstd[:, b:b + 1], veps[:, b:b + 1], half[:], ALU.pow).then_inc(s["rstd_done"], 1)

                def add_rope(item, parity, drained, first=False):
                    pool.wait_ge(s["proj_free"], drained)
                    if not first:
                        pool.wait_ge(s["feat_done"], item - 1)
                    pool.tensor_tensor(y[:, parity], t1[:, parity], t2[:, parity], ALU.add).then_inc(s["y_done"], 1)

                rstd_of(1, 0)
                rstd_of(2, 1)
                for r in range(RI):
                    add_rope(r, r % 2, 2 + (r + 1 if r else 0) + 1, first=r < 2)

                def step(c, b, nxt, norm):
                    if norm:
                        rstd_of(at(c, b, 1, 3), b)
                    if nxt:
                        for r in range(RI):
                            j = r + 1 if r else 0
                            add_rope(at(c, b, RI, RI + r), (b + 1 + r) % 2, 2 + 1 + proj_item(c, b, j))

                walk(pool, step)

            @block.scalar
            def _(act):
                def drain_turn(c, b, j, dst, src):
                    n = turn_item(c, b, j)
                    act.wait_ge(s["turn_full"], n + 1)
                    act.activation(dst, src, ACT.Copy).then_inc(s["turn_free"], 1)

                def drain_norm(n, parity, bank, b):
                    act.wait_ge(s["turn_full"], n + 1)
                    for k in range(KD):
                        i = act.activation(h[:, parity, k, :], turn[:, bank, k * P:(k + 1) * P], ACT.Identity,
                                           bias=mod_t[:, 0, SA * KD + k, b:b + 1], scale=mod_t[:, 0, CA * KD + k, b:b + 1])
                    i.then_inc(s["turn_free"], 1)

                def exp_of(item, parity):
                    act.wait_ge(s["y_done"], item + 1)
                    act.activation(ex[:, parity], y[:, parity], ACT.Relu, scale=-1.0).then_inc(s["relu_done"], 1)
                    act.wait_ge(s["relu_done"], item + 1)
                    act.activation(ex[:, parity], ex[:, parity], ACT.Exp, scale=-1.0).then_inc(s["exp_done"], 1)

                drain_norm(0, 0, 0, 0)
                drain_norm(1, 1, 1, 1)
                for r in range(RI):
                    exp_of(r, r % 2)

                def step(c, b, nxt, norm):
                    tp = 1 if last(c, b) else 0

                    def bank(j):
                        return (j + tp) % 2

                    def e(r):
                        if nxt:
                            exp_of(at(c, b, RI, RI + r), (b + 1 + r) % 2)

                    drain_turn(c, b, 0, k_t[:], turn[:, bank(0), :].rearrange("p (g t) -> p g t", g=KVH))
                    for g in range(KVH):
                        drain_turn(c, b, 1 + g, q_t[:, g], turn[:, bank(1 + g), :])
                        if g == 2:
                            e(0)
                    for g in range(KVH):
                        drain_turn(c, b, 5 + g, o_t[:, g * REP:(g + 1) * REP, :],
                                   turn[:, bank(5 + g), :].rearrange("p (r t) -> p r t", r=REP))
                        e(1 + g)
                    if norm:
                        drain_norm(turn_item(c, b, 9), b, bank(9), b)

                walk(act, step)

            @block.vector
            def _(dve):
                dve.memset(state[:], 0.0)
                dve.memset(v[:, :, :, HD:VW], 1.0)
                dve.memset(dx[:], 0.0).then_inc(s["proj_free"], 2)
                dve.memset(den[:], 0.0).then_inc(s["score_free"], 2)
                dve.memset(rden[:], 0.0).then_inc(s["num_free"], 1)
                dve.memset(h[:], 0.0).then_inc(s["turn_free"], 2)

                def norm(t, b):
                    dve.bn_stats(stats[:, b, :], x[:, t, :]).then_inc(s["stat_done"], 1)

                def aggregate(b):
                    dve.bn_aggr(mv[:, b, :], stats[:, b, :]).then_inc(s["aggr_done"], 1)

                def centre(t, n, b):
                    dve.wait_ge(s["rstd_done"], n)
                    dve.tensor_scalar(xn[:, b, :], x[:, t, :], mv[:, b, 0:1], rstd[:, b:b + 1],
                                      ALU.subtract, ALU.mult).then_inc(s["xn_done"], 1)

                def split(n, parity, drained):
                    dve.wait_ge(s["turn_free"], drained)
                    dve.tensor_copy(h_hi[:, parity], h[:, parity]).then_inc(s["hi_done"], 1)
                    dve.wait_ge(s["hi_done"], n)
                    dve.tensor_tensor(h_lo[:, parity], h[:, parity], h_hi[:, parity].bitcast(F32),
                                      ALU.subtract).then_inc(s["hl_done"], 1)

                def rope(item, parity, bank, c, n, first=False):
                    heads = proj[:, bank, :].rearrange("p (g d) -> p g d", d=HD)
                    halves = heads.rearrange("p g (u d) -> p g u d", u=2)
                    cc = cos[:, bass.ds(c, 1), :].rearrange("p o d -> p (o d)").unsqueeze(1)
                    ss = sin[:, bass.ds(c, 1), :].rearrange("p o (u d) -> p (o u) d", u=2).unsqueeze(1)
                    dve.wait_ge(s["proj_full"], n + 1)
                    if not first:
                        dve.wait_ge(s["y_done"], item - 1)
                    dve.tensor_tensor(t1[:, parity].rearrange("p (g d) -> p g d", d=HD // 2),
                                      proj[:, bank, :].rearrange("p (g d) -> p g d", d=HD // 2),
                                      cc.broadcast_to([P, 2 * REP, HD // 2]), ALU.mult)
                    dve.tensor_tensor(t2[:, parity].rearrange("p (g u d) -> p g u d", u=2, d=HD // 2),
                                      halves[:, :, ::-1, :], ss.broadcast_to([P, REP, 2, HD // 2]),
                                      ALU.mult).then_inc(s["proj_free"], 1)

                def keep_v(parity, bank, n):
                    dve.wait_ge(s["proj_full"], n + 1)
                    dve.tensor_copy(v[:, parity, :, 0:HD], proj[:, bank, :].rearrange("p (g d) -> p g d", d=HD)
                                    ).then_inc(s["proj_free"], 1)

                def feature(item, parity, dst):
                    dve.wait_ge(s["exp_done"], item + 1)
                    dve.scalar_tensor_tensor(dst, y[:, parity], 0.0, ex[:, parity], ALU.max, ALU.add
                                             ).then_inc(s["feat_done"], 1)

                for b in range(B):
                    norm(b * NC, b)
                dve.wait_ge(s["stat_done"], B)
                for b in range(B):
                    aggregate(b)
                centre(0, 1, 0)
                centre(NC, 2, 1)
                dve.wait_ge(s["tab_in"], 32)
                for i in range(NW):
                    dve.wait_ge(w_inb[i % 2], 16 * (i // 2 + 1))
                    cols = slice(i * WCH, (i + 1) * WCH)
                    dve.tensor_copy(w_hi[:, :, cols], stage[:, i % 2]).then_inc(s["w_split"], 1)
                    dve.wait_ge(s["w_split"], 2 * i + 1)
                    dve.tensor_tensor(w_lo[:, :, cols], stage[:, i % 2], w_hi[:, :, cols].bitcast(F32),
                                      ALU.subtract).then_inc(s["w_split"], 1)
                split(1, 0, 2 + 1)
                dve.wait_ge(s["causal_made"], 1)
                rope(0, 0, 0, 0, 0, first=True)
                keep_v(0, 1, 1)
                for r in range(1, RI):
                    rope(r, r % 2, (r + 1) % 2, 0, r + 1, first=r < 2)
                    feature(r - 1, (r - 1) % 2, feat[:, 0, r - 1, :])
                feature(RI - 1, (RI - 1) % 2, feat[:, 0, RI - 1, :])

                def step(c, b, nxt, norm_on):
                    nb = 1 - b
                    nc_ = c + b

                    def masked(g):
                        dve.wait_ge(s["score_full"], at(c, b, KVH, g + 1))
                        dve.tensor_tensor(am[:, g % 2].rearrange("p (r t) -> p r t", r=REP),
                                          score[:, g % 2, :].rearrange("p (r t) -> p r t", r=REP),
                                          causal[:].unsqueeze(1).broadcast_to([P, REP, P]),
                                          ALU.mult).then_inc(s["score_free"], 1)

                    def normalise(g):
                        dve.wait_ge(s["num_full"], at(c, b, KVH + 1, g + 1))
                        pairs = num[:, :, 0:2 * VW].rearrange("p k (h w) -> p k h w", w=VW)
                        dve.tensor_scalar(den[:].rearrange("p (k h) -> p k h", k=2), pairs[:, :, :, HD], DEN_EPS, None,
                                          ALU.add).then_inc(s["den_done"], 1)
                        dve.wait_ge(s["den_done"], at(c, b, KVH, g + 1))
                        dve.reciprocal(rden[:], den[:]).then_inc(s["rden_done"], 1)
                        dve.wait_ge(s["rden_done"], at(c, b, KVH, g + 1))
                        dve.tensor_tensor(on[:, g % 2].rearrange("p (k h d) -> p k h d", k=2, h=2),
                                          pairs[:, :, :, 0:HD],
                                          rden[:].rearrange("p (k h) -> p k h", k=2).unsqueeze(3)
                                          .broadcast_to([P, 2, 2, HD]), ALU.mult).then_inc(s["num_free"], 1)

                    def q_rope(r):
                        if nxt:
                            rope(at(c, b, RI, RI + r), (b + 1 + r) % 2, (b + (r + 1 if r else 0)) % 2, nc_,
                                 proj_item(c, b, r + 1 if r else 0))

                    def f(r):
                        if nxt:
                            feature(at(c, b, RI, RI + r), (b + 1 + r) % 2, feat[:, nb, r, :])

                    if nxt:
                        split(at(c, b, 1, 2), nb, 2 + 1 + at(c, b, 10, 1))
                    if norm_on:
                        norm(bass.ds(c + (b * NC + 1), 1), b)
                        dve.wait_ge(s["stat_done"], at(c, b, 1, 3))
                    masked(0)
                    if norm_on:
                        aggregate(b)
                    q_rope(0)
                    normalise(0)
                    masked(1)
                    if nxt:
                        keep_v(nb, (b + 1) % 2, proj_item(c, b, 1))
                    f(0)
                    normalise(1)
                    if norm_on:
                        centre(bass.ds(c + (b * NC + 1), 1), at(c, b, 1, 3), b)
                    masked(2)
                    q_rope(1)
                    normalise(2)
                    masked(3)
                    q_rope(2)
                    f(1)
                    normalise(3)
                    q_rope(3)
                    f(2)
                    dve.wait_ge(s["num_full"], at(c, b, KVH + 1, KVH + 1))
                    dve.tensor_tensor(state[:, b].rearrange("p (k h) w -> p k (h w)", k=2),
                                      num[:, :, 0:2 * VW], state[:, b].rearrange("p (k h) w -> p k (h w)", k=2),
                                      ALU.add).then_inc(s["num_free"], 1)
                    q_rope(4)
                    f(3)
                    n = at(c, b, 7, 6) if last(c, b) else proj_item(c, b, 6)
                    dve.wait_ge(s["proj_full"], n + 1)
                    dve.tensor_tensor(dx[:], proj[:, b, 0:D],
                                      gate_b[:, 0, 0, b, :], ALU.mult).then_inc(s["proj_free"], 1)
                    dve.wait_ge(s["proj_free"], 2 + n + 1)
                    xt = x[:, bass.ds(c + b * NC, 1), :].rearrange("p o d -> p (o d)")
                    dve.tensor_tensor(xt, xt, dx[:], ALU.add).then_inc(s["x_done"], 1)
                    f(4)

                walk(dve, step)

            @block.tensor
            def _(pe):
                pe.wait_ge(s["wo_in"], 16)

                def norm_turn(n, parity, bank, norms):
                    pe.wait_ge(s["xn_done"], norms)
                    pe.wait_ge(s["turn_free"], n + 1)
                    for k in range(KD):
                        t = pe.transpose(turn[:, bank, k * P:(k + 1) * P], xn[:, parity, k * P:(k + 1) * P], ident[:])
                    t.then_inc(s["turn_full"], 1)

                def project(parity, j, bank, n):
                    pe.wait_ge(s["proj_free"], n + 1)
                    cols = slice(j * 512, (j + 1) * 512)
                    passes = [(h_hi, w_hi), (h_hi, w_lo), (h_lo, w_hi)]
                    for i, (hh, ww) in enumerate(passes):
                        for k in range(KD):
                            mm = pe.matmul(proj[:, bank, :], hh[:, parity, k, :], ww[:, k, cols],
                                           start=(i == 0 and k == 0), stop=(i == 2 and k == KD - 1))
                    mm.then_inc(s["proj_full"], 1)

                norm_turn(0, 0, 0, 1)
                norm_turn(1, 1, 1, 2)
                pe.wait_ge(s["w_split"], 2 * NW)
                pe.wait_ge(s["hl_done"], 1)
                for j in range(RI + 1):
                    project(0, j, j % 2, j)

                def step(c, b, nxt, norm_on):
                    tp = 1 if last(c, b) else 0

                    def bank(j):
                        return (j + tp) % 2

                    def turn4(j, src):
                        n = turn_item(c, b, j)
                        pe.wait_ge(s["turn_free"], n + 1)
                        for r in range(4):
                            t = pe.transpose(turn[:, bank(j), r * P:(r + 1) * P], src[:, r * P:(r + 1) * P], ident[:])
                        t.then_inc(s["turn_full"], 1)

                    def q_turn(g):
                        pe.wait_ge(s["feat_done"], at(c, b, RI, 2 + g))
                        turn4(1 + g, feat[:, b, 1 + g, :])

                    def scores(g):
                        pe.wait_ge(s["turn_free"], 2 + 1 + turn_item(c, b, 1 + g))
                        pe.wait_ge(s["score_free"], at(c, b, KVH, g + 1))
                        pe.matmul(score[:, g % 2, :], k_t[:, g, :], q_t[:, g, :], start=True, stop=True
                                  ).then_inc(s["score_full"], 1)

                    def numerators(g):
                        pe.wait_ge(s["score_free"], 2 + at(c, b, KVH, g + 1))
                        pe.wait_ge(s["num_free"], at(c, b, KVH + 1, g + 1))
                        for r in range(REP):
                            dst = num[:, r // 2, (r % 2) * VW:(r % 2 + 1) * VW]
                            pe.matmul(dst, am[:, g % 2, r * P:(r + 1) * P], v[:, b, g, :], start=True, stop=False)
                            mm = pe.matmul(dst, q_t[:, g, r * P:(r + 1) * P], state[:, b, g, :], start=False, stop=True)
                        mm.then_inc(s["num_full"], 1)

                    def out_turn(g):
                        pe.wait_ge(s["num_free"], 1 + at(c, b, KVH + 1, g + 1))
                        turn4(5 + g, on[:, g % 2, :])

                    def p(j):
                        if nxt:
                            project(1 - b, j, (b + j) % 2, proj_item(c, b, j))

                    pe.wait_ge(s["feat_done"], at(c, b, RI, 1))
                    turn4(0, feat[:, b, 0, :])
                    q_turn(0)
                    q_turn(1)
                    scores(0)
                    q_turn(2)
                    if nxt:
                        pe.wait_ge(s["hl_done"], at(c, b, 1, 2))
                    p(0)
                    numerators(0)
                    scores(1)
                    q_turn(3)
                    p(1)
                    numerators(1)
                    out_turn(0)
                    scores(2)
                    p(2)
                    numerators(2)
                    out_turn(1)
                    scores(3)
                    p(3)
                    numerators(3)
                    out_turn(2)
                    p(4)
                    pe.wait_ge(s["num_free"], at(c, b, KVH + 1, KVH + 1))
                    for g in range(KVH):
                        mm = pe.matmul(num[:, g // 2, (g % 2) * VW:(g % 2 + 1) * VW], feat[:, b, 0, g * P:(g + 1) * P],
                                       v[:, b, g, :], start=True, stop=True)
                    mm.then_inc(s["num_full"], 1)
                    out_turn(3)
                    p(5)
                    if norm_on:
                        norm_turn(turn_item(c, b, 9), b, bank(9), at(c, b, 1, 3))
                    n = at(c, b, 7, 6) if last(c, b) else proj_item(c, b, 6)
                    pe.wait_ge(s["proj_free"], n + 1)
                    pe.wait_ge(s["turn_free"], 2 + 1 + turn_item(c, b, 8))
                    for i in range(H):
                        mm = pe.matmul(proj[:, b, 0:D], o_t[:, i, :], wo[:, i, :],
                                       start=(i == 0), stop=(i == H - 1))
                    mm.then_inc(s["proj_full"], 1)

                walk(pe, step)

    def ffn_phase(self):
        nc, a = self.nc, self.a
        x, ident, mod_t, gate_b, half, eps = self.x, self.ident, self.mod_t, self.gate_b, self.half, self.eps
        TOK = GT * P
        NQ = NM // 4
        with ExitStack() as ctx:
            def sb(name, shape, dt=F32):
                return ctx.enter_context(nc.sbuf_tensor(name, shape, dt))

            def ps(name, shape, dt=F32):
                return ctx.enter_context(nc.psum_tensor(name, shape, dt))

            stage = sb("f_stage", [P, 2, KD, 512])
            w_hi, w_lo = sb("wgu_hi", [P, KD, 2 * FI], F32R), sb("wgu_lo", [P, KD, 2 * FI], F32R)
            wd = sb("wd_sb", [P, NM, D])
            stats, mv = sb("f_stats", [P, GT, 6]), sb("f_mv", [P, GT, 2])
            veps, rstd = sb("f_veps", [P, GT]), sb("f_rstd", [P, GT])
            xn = sb("f_xn", [P, GT, D])
            h = sb("f_h", [P, KD, TOK])
            h_hi, h_lo = sb("f_h_hi", [P, 2, KD, TOK], F32R), sb("f_h_lo", [P, 2, KD, TOK], F32R)
            sg = sb("silu_gate", [P, 2, TOK])
            hid = sb("hidden", [P, 2, NM, TOK])
            mag = sb("magnitude", [P, NM, TOK])
            beats = sb("beats", [P, 6, TOK], BF16)
            wins = sb("wins", [P, 4, TOK], BF16)
            part = sb("wins_part", [P, 4, TOK], BF16)
            dx = sb("f_dx", [P, 2, D])
            turn = ps("f_turn", [P, 2, 512])
            gate, up = ps("gate_ps2", [P, 2, 512]), ps("up_ps", [P, 2, 512])
            rows = ps("f_rows", [P, 2, 512])

            names = ("wd_in w_split stat_done aggr_done veps_done rstd_done xn_done h_done hi_done hl_done "
                     "turn_full gate_full up_full silu_done hid_done mag_done pick_step pick_done rows_full dx_done x_done")
            s = {n: self.sem("f_" + n) for n in names.split()}
            w_in = [self.sem(f"f_w_in{i}") for i in range(2)]
            block = ctx.enter_context(nc.Block())
            NW = 2 * FI // 512

            @block.sync
            def _(sp):
                for i in range(NW):
                    if i >= 2:
                        sp.wait_ge(s["w_split"], 2 * (i - 1))
                    sp.dma_start(stage[:, i % 2], a["wgu"][:, i * 512:(i + 1) * 512]
                                 .rearrange("(k p) n -> p k n", p=P)).then_inc(w_in[i % 2], 16)
                sp.dma_start(wd[:], a["wd"].rearrange("(m p) n -> p m n", p=P)).then_inc(s["wd_in"], 16)
                sp.wait_ge(s["wd_in"], 16)

            @block.gpsimd
            def _(pool):
                def rstd_of(g):
                    pool.wait_ge(s["aggr_done"], GT * (g + 1))
                    pool.tensor_tensor(veps[:], mv[:, :, 1], eps[:].broadcast_to([P, GT]), ALU.add).then_inc(s["veps_done"], 1)
                    pool.wait_ge(s["veps_done"], g + 1)
                    pool.tensor_tensor(rstd[:], veps[:], half[:].broadcast_to([P, GT]), ALU.pow).then_inc(s["rstd_done"], 1)

                def add_rows(g):
                    for i in range(GT):
                        n = g * GT + i
                        pool.wait_ge(s["dx_done"], n + 1)
                        pool.tensor_tensor(x[:, n, :], x[:, n, :], dx[:, n % 2], ALU.add).then_inc(s["x_done"], 1)

                rstd_of(0)
                for g in range(NG):
                    if g + 1 < NG:
                        rstd_of(g + 1)
                    if g:
                        add_rows(g - 1)
                add_rows(NG - 1)

            @block.scalar
            def _(act):
                def drain_norm(g):
                    b = g * GT // NC
                    for k in range(KD):
                        act.wait_ge(s["turn_full"], KD * g + k + 1)
                        if g:
                            act.wait_ge(s["hl_done"], g)
                        act.activation(h[:, k, :], turn[:, k, :], ACT.Identity,
                                       bias=mod_t[:, 0, SB_ * KD + k, b:b + 1],
                                       scale=mod_t[:, 0, CB * KD + k, b:b + 1]).then_inc(s["h_done"], 1)

                def magnitude(g, m):
                    n = g * NM + m
                    act.wait_ge(s["hid_done"], n + 1)
                    if g:
                        act.wait_ge(s["pick_done"], NQ * (g - 1) + m // 4 + 1)
                    act.activation(mag[:, m], hid[:, g % 2, m], ACT.Abs).then_inc(s["mag_done"], 1)

                drain_norm(0)
                for g in range(NG):
                    for m in range(NM):
                        n = g * NM + m
                        act.wait_ge(s["gate_full"], n + 1)
                        if n >= 2:
                            act.wait_ge(s["hid_done"], n - 1)
                        act.activation(sg[:, n % 2], gate[:, n % 2, :], ACT.Silu).then_inc(s["silu_done"], 1)
                        if n:
                            magnitude((n - 1) // NM, (n - 1) % NM)
                        if m == 5 and g + 1 < NG:
                            drain_norm(g + 1)
                magnitude(NG - 1, NM - 1)

            @block.vector
            def _(dve):
                def norms(g):
                    for i in range(GT):
                        dve.bn_stats(stats[:, i, :], x[:, g * GT + i, :]).then_inc(s["stat_done"], 1)
                    for i in range(GT):
                        dve.wait_ge(s["stat_done"], g * GT + i + 1)
                        dve.bn_aggr(mv[:, i, :], stats[:, i, :]).then_inc(s["aggr_done"], 1)

                def centre(g):
                    dve.wait_ge(s["rstd_done"], g + 1)
                    if g:
                        dve.wait_ge(s["turn_full"], KD * g)
                    for i in range(GT):
                        dve.tensor_scalar(xn[:, i, :], x[:, g * GT + i, :], mv[:, i, 0:1], rstd[:, i:i + 1],
                                          ALU.subtract, ALU.mult).then_inc(s["xn_done"], 1)

                def split(g):
                    dve.wait_ge(s["h_done"], KD * (g + 1))
                    dve.tensor_copy(h_hi[:, g % 2], h[:]).then_inc(s["hi_done"], 1)
                    dve.wait_ge(s["hi_done"], g + 1)
                    dve.tensor_tensor(h_lo[:, g % 2], h[:], h_hi[:, g % 2].bitcast(F32), ALU.subtract
                                      ).then_inc(s["hl_done"], 1)

                steps = [0]

                def pick(g, q):
                    m0 = 4 * q
                    pairs = [(0, 1), (0, 2), (0, 3), (1, 2), (1, 3), (2, 3)]
                    c = {pr: beats[:, i] for i, pr in enumerate(pairs)}

                    def op(f, need=0):
                        def go():
                            if need:
                                dve.wait_ge(s["pick_step"], base + need)
                            f().then_inc(s["pick_step"], 1)
                        return go

                    base = (g * NQ + q) * 14
                    ops = []
                    for i, (u, w) in enumerate(pairs):
                        def duel(i=i, u=u, w=w):
                            dve.wait_ge(s["mag_done"], g * NM + m0 + 4)
                            return dve.tensor_tensor(beats[:, i], mag[:, m0 + u], mag[:, m0 + w], ALU.is_ge)
                        ops.append(op(duel))
                    sums = [(0, c[0, 1], c[0, 2], ALU.add), (1, c[1, 2], c[0, 1], ALU.subtract),
                            (2, c[2, 3], c[0, 2], ALU.subtract), (3, c[0, 3], c[1, 3], ALU.add)]
                    for i, u, w, o in sums:
                        ops.append(op(lambda i=i, u=u, w=w, o=o: dve.tensor_tensor(part[:, i], u, w, o), 6))
                    ends = [(0, c[0, 3], ALU.add), (1, c[1, 3], ALU.add), (2, c[1, 2], ALU.subtract), (3, c[2, 3], ALU.add)]
                    for i, w, o in ends:
                        ops.append(op(lambda i=i, w=w, o=o: dve.tensor_tensor(wins[:, i], part[:, i], w, o), 7 + i))
                    tests = [(0, 2.0, ALU.is_ge), (1, 1.0, ALU.is_ge), (2, 0.0, ALU.is_ge), (3, 1.0, ALU.is_le)]
                    for i, bound, o in tests:
                        def keep(i=i, bound=bound, o=o):
                            dve.wait_ge(s["pick_step"], base + 11 + i)
                            t = hid[:, g % 2, m0 + i]
                            ins = dve.scalar_tensor_tensor(t, wins[:, i], bound, t, o, ALU.mult)
                            if i == 3:
                                ins.then_inc(s["pick_done"], 1)
                        ops.append(keep)
                    return ops

                def out_rows(g):
                    b = g * GT // NC
                    for i in range(GT):
                        n = g * GT + i
                        dve.wait_ge(s["rows_full"], n + 1)
                        if n >= 2:
                            dve.wait_ge(s["x_done"], n - 1)
                        dve.tensor_tensor(dx[:, n % 2], rows[:, n % 2, 0:D], gate_b[:, 0, 1, b, :], ALU.mult
                                          ).then_inc(s["dx_done"], 1)

                norms(0)
                centre(0)
                for i in range(NW):
                    dve.wait_ge(w_in[i % 2], 16 * (i // 2 + 1))
                    cols = slice(i * 512, (i + 1) * 512)
                    dve.tensor_copy(w_hi[:, :, cols], stage[:, i % 2]).then_inc(s["w_split"], 1)
                    dve.wait_ge(s["w_split"], 2 * i + 1)
                    dve.tensor_tensor(w_lo[:, :, cols], stage[:, i % 2], w_hi[:, :, cols].bitcast(F32),
                                      ALU.subtract).then_inc(s["w_split"], 1)
                    if i == 0:
                        split(0)
                ops = []
                for g in range(NG):
                    for m in range(NM):
                        n = g * NM + m
                        dve.wait_ge(s["up_full"], n + 1)
                        dve.wait_ge(s["silu_done"], n + 1)
                        if g >= 2 and m == 0:
                            dve.wait_ge(s["rows_full"], GT * (g - 1))
                        dve.tensor_tensor(hid[:, g % 2, m], up[:, n % 2, :], sg[:, n % 2], ALU.mult
                                          ).then_inc(s["hid_done"], 1)
                        if m % 4 == 0 and n:
                            ops = pick((n - 4) // NM, (n - 4) % NM // 4)
                        for o in ops[:5]:
                            o()
                        ops = ops[5:]
                        if g + 1 < NG:
                            if m == 1:
                                norms(g + 1)
                            if m == 3:
                                centre(g + 1)
                            if m == 6:
                                split(g + 1)
                        if m == 5 and g:
                            out_rows(g - 1)
                for o in pick(NG - 1, NQ - 1):
                    o()
                out_rows(NG - 1)

            @block.tensor
            def _(pe):
                def norm_turn(g):
                    pe.wait_ge(s["xn_done"], GT * (g + 1))
                    for k in range(KD):
                        if g:
                            pe.wait_ge(s["h_done"], KD * (g - 1) + k + 1)
                        for i in range(GT):
                            t = pe.transpose(turn[:, k, i * P:(i + 1) * P], xn[:, i, k * P:(k + 1) * P], ident[:])
                        t.then_inc(s["turn_full"], 1)

                def hidden(g, m):
                    n = g * NM + m
                    for dst, off, full, used in ((gate, 0, "gate_full", "silu_done"), (up, FI, "up_full", "hid_done")):
                        if n >= 2:
                            pe.wait_ge(s[used], n - 1)
                        cols = slice(off + m * P, off + (m + 1) * P)
                        for i, (ww, hh) in enumerate([(w_hi, h_hi), (w_lo, h_hi), (w_hi, h_lo)]):
                            for k in range(KD):
                                mm = pe.matmul(dst[:, n % 2, :], ww[:, k, cols], hh[:, g % 2, k, :],
                                               start=(i == 0 and k == 0), stop=(i == 2 and k == KD - 1))
                        mm.then_inc(s[full], 1)

                def down(g):
                    pe.wait_ge(s["pick_done"], NQ * (g + 1))
                    for i in range(GT):
                        n = g * GT + i
                        if n >= 2:
                            pe.wait_ge(s["dx_done"], n - 1)
                        for m in range(NM):
                            mm = pe.matmul(rows[:, n % 2, 0:D], hid[:, g % 2, m, i * P:(i + 1) * P], wd[:, m, :],
                                           start=(m == 0), stop=(m == NM - 1))
                        mm.then_inc(s["rows_full"], 1)

                norm_turn(0)
                pe.wait_ge(s["w_split"], 2 * NW)
                pe.wait_ge(s["wd_in"], 16)
                for g in range(NG):
                    pe.wait_ge(s["hl_done"], g + 1)
                    for m in range(NM):
                        hidden(g, m)
                        if m == 4 and g + 1 < NG:
                            norm_turn(g + 1)
                        if m == 5 and g:
                            down(g - 1)
                down(NG - 1)

    def scan_phase(self):
        nc, a = self.nc, self.a
        x, ident, mod_t, gate_b, half, eps = self.x, self.ident, self.mod_t, self.gate_b, self.half, self.eps
        with ExitStack() as ctx:
            def sb(name, shape, dt=F32):
                return ctx.enter_context(nc.sbuf_tensor(name, shape, dt))

            def ps(name, shape, dt=F32):
                return ctx.enter_context(nc.psum_tensor(name, shape, dt))

            stage = sb("t_stage", [P, KD, 2 * D])
            w_hi, w_lo = sb("wkv_hi", [P, KD, 2 * D], F32R), sb("wkv_lo", [P, KD, 2 * D], F32R)
            wo = sb("t_wo", [P, KD, D])
            ln_g, ln_b = sb("ln_gamma", [P, KD]), sb("ln_beta", [P, KD])
            cos, sin = sb("t_cos", [P, NC, TD // 2]), sb("t_sin", [P, NC, TD])
            blocks, ident_n = sb("head_blocks", [P, P]), sb("ident_n", [P, P])
            rows_of = sb("rows_of", [P, NMB])
            stats, mv = sb("t_stats", [P, 2, 2, 6]), sb("t_mv", [P, 2, 2, 2])
            veps, rstd = sb("t_veps", [P, 2, 2]), sb("t_rstd", [P, 2, 2])
            xn, zn = sb("t_xn", [P, B, D]), sb("t_zn", [P, B, D])
            h = sb("t_h", [P, B, KD, P])
            h_hi, h_lo = sb("t_h_hi", [P, B, KD, P], F32R), sb("t_h_lo", [P, B, KD, P], F32R)
            t1, t2 = sb("t_rope_cos", [P, B, D]), sb("t_rope_sin", [P, B, D])
            kr, v = sb("t_k", [P, B, D]), sb("t_v", [P, B, D])
            STEP = P + MB
            k_diag = sb("k_diag", [P, B, KD, NMB * STEP])
            k_rows = sb("k_rows", [P, B, NMB, D])
            u = sb("t_u", [P, B, D])
            w = sb("t_w", [P, B, KD, P])
            zs = sb("t_z", [P, B, D])
            o_t = sb("t_o", [P, B, KD, P])
            dx = sb("t_dx", [P, B, D])
            z_ps, g_ps = ps("z_ps", [P, B, 512]), ps("g_ps", [P, B, 512])
            proj, turn = ps("t_proj", [P, B, 512]), ps("t_turn", [P, B, 512])

            def sems(name):
                return self.sem("t_" + name)

            def nth(b, n):
                return n * B + (b + 1 - B)

            w_in, wo_in, w_split, const_step, const_made = (self.sem("t_" + n) for n in (
                "w_in", "wo_in", "w_split", "const_step", "const_made"))
            zeroed, blocks_made = self.sem("t_zeroed"), self.sem("t_blocks_made")
            z_full, u_done, g_full, w_done = sems("z_full"), sems("u_done"), sems("g_full"), sems("w_done")
            z_kept, v_kept, k_diag_done, k_rows_done = sems("z_kept"), sems("v_kept"), sems("kdiag"), sems("krows")
            x_stat, x_aggr, x_rstd, xn_done = sems("x_stat"), sems("x_aggr"), sems("x_rstd"), sems("xn_done")
            z_stat, z_aggr, z_rstd, zn_done = sems("z_stat"), sems("z_aggr"), sems("z_rstd"), sems("zn_done")
            xv_done, zv_done = sems("x_veps"), sems("z_veps")
            xn_turned, zn_turned, k_turned = sems("xn_turned"), sems("zn_turned"), sems("k_turned")
            h_done, hi_done, hl_done, o_done = sems("h_done"), sems("hi_done"), sems("hl_done"), sems("o_done")
            proj_full, rope_done, kr_done = sems("proj_full"), sems("rope_done"), sems("kr_done")
            rows_full, dx_done, x_done = sems("rows_full"), sems("dx_done"), sems("x_done")
            block = ctx.enter_context(nc.Block())

            def tile(c, b):
                return bass.ds(c + b * NC, 1)

            def flat(ap):
                return ap.rearrange("p o d -> p (o d)")

            def walk(engine, step):
                step(0, False, True)
                with engine.Fori(1, NC - 1) as c:
                    step(c, True, True)
                step(NC - 1, True, False)

            @block.sync
            def _(sp):
                sp.dma_start(stage[:], a["wkv1"].rearrange("(k p) n -> p k n", p=P)).then_inc(w_in, 16)
                sp.dma_start(cos[:], a["cos1"].rearrange("(c p) d -> p c d", p=P)).then_inc(wo_in, 16)
                sp.dma_start(sin[:], a["sin1"].rearrange("(c p) d -> p c d", p=P)).then_inc(wo_in, 16)
                sp.dma_start(wo[:], a["wo1"].rearrange("(k p) n -> p k n", p=P)).then_inc(wo_in, 16)
                with nc.allow_non_contiguous_dma(reason="two vectors of 256"):
                    sp.dma_start(ln_g[:], a["ln_g"].rearrange("(k p) -> p k", p=P)).then_inc(wo_in, 16)
                    sp.dma_start(ln_b[:], a["ln_b"].rearrange("(k p) -> p k", p=P)).then_inc(wo_in, 16)
                sp.wait_ge(wo_in, 16 * 5)

            @block.gpsimd
            def _(pool):
                pool.memset(blocks[:], INV_N).then_inc(const_step, 1)
                pool.memset(rows_of[:], 1.0).then_inc(const_step, 1)
                pool.wait_ge(const_step, 2)
                n = 2
                for base, sign in ((0, 1), (MB - 1, -1)):
                    for dst, pattern in ((blocks[:].rearrange("p (h e) -> p h e", e=TD), [[-sign * TD, P // TD], [0, TD]]),
                                         (rows_of[:], [[-sign * MB, NMB]])):
                        pool.affine_select(out=dst, in_=dst, compare_op=ALU.is_ge, fill=0.0, base=base,
                                           pattern=pattern, channel_multiplier=sign).then_inc(const_step, 1)
                    n += 2
                    pool.wait_ge(const_step, n)
                pool.memset(veps[:], 0.0).then_inc(blocks_made, 1)

                def rstd_of(i, b, n, aggr, stepped, done):
                    pool.wait_ge(aggr, nth(b, n))
                    pool.tensor_tensor(veps[:, i, b:b + 1], mv[:, i, b, 1:2], eps[:], ALU.add).then_inc(stepped, 1)
                    pool.wait_ge(stepped, nth(b, n))
                    pool.tensor_tensor(rstd[:, i, b:b + 1], veps[:, i, b:b + 1], half[:], ALU.pow).then_inc(done, 1)

                def add_rope(b, n):
                    pool.wait_ge(rope_done, nth(b, n))
                    pool.tensor_tensor(kr[:, b], t1[:, b], t2[:, b], ALU.add).then_inc(kr_done, 1)

                def add_rows(c, b, n):
                    pool.wait_ge(dx_done, nth(b, n))
                    xt = flat(x[:, tile(c, b), :])
                    pool.tensor_tensor(xt, xt, dx[:, b], ALU.add).then_inc(x_done, 1)

                pool.wait_ge(blocks_made, 1)
                for b in range(B):
                    rstd_of(0, b, 1, x_aggr, xv_done, x_rstd)
                for b in range(B):
                    add_rope(b, 1)

                def step(c, prev, nxt):
                    if prev:
                        for b in range(B):
                            rstd_of(1, b, c, z_aggr, zv_done, z_rstd)
                    if nxt:
                        for b in range(B):
                            rstd_of(0, b, c + 2, x_aggr, xv_done, x_rstd)
                    if prev:
                        for b in range(B):
                            add_rows(c - 1, b, c)
                    if nxt:
                        for b in range(B):
                            pool.wait_ge(k_rows_done, nth(b, (c + 1) * NMB))
                            add_rope(b, c + 2)

                walk(pool, step)
                for b in range(B):
                    rstd_of(1, b, NC, z_aggr, zv_done, z_rstd)
                for b in range(B):
                    add_rows(NC - 1, b, NC)

            @block.scalar
            def _(act):
                def spread(c, b, j, waited=True):
                    if waited:
                        act.wait_ge(g_full, nth(b, c * NMB + (j - NMB + 2)))
                    act.activation(k_rows[:, b, j], kr[:, b], ACT.Copy, scale=rows_of[:, j:j + 1]
                                   ).then_inc(k_rows_done, 1)

                def drain_norm(b, n):
                    act.wait_ge(xn_turned, nth(b, n))
                    for k in range(KD):
                        i = act.activation(h[:, b, k], turn[:, b, k * P:(k + 1) * P], ACT.Identity,
                                           bias=mod_t[:, 1, SA * KD + k, b:b + 1], scale=mod_t[:, 1, CA * KD + k, b:b + 1])
                    i.then_inc(h_done, 1)

                def drain_out(b, n):
                    act.wait_ge(zn_turned, nth(b, n))
                    for k in range(KD):
                        i = act.activation(o_t[:, b, k], turn[:, b, k * P:(k + 1) * P], ACT.Identity,
                                           bias=ln_b[:, k:k + 1], scale=ln_g[:, k:k + 1])
                    i.then_inc(o_done, 1)

                def hand_over(b, n):
                    act.wait_ge(rope_done, nth(b, n))
                    act.activation(v[:, b], proj[:, b, D:2 * D], ACT.Copy).then_inc(v_kept, 1)
                    act.wait_ge(k_turned, nth(b, n))
                    act.activation(k_diag[:, b].rearrange("p k (m s) -> p k m s", s=STEP)[:, :, :, 0:MB],
                                   turn[:, b, 0:D].rearrange("p (k m s) -> p k m s", k=KD, s=MB),
                                   ACT.Copy).then_inc(k_diag_done, 1)

                act.wait_ge(wo_in, 16 * 5)
                for b in range(B):
                    drain_norm(b, 1)
                act.wait_ge(zeroed, 1)
                act.wait_ge(blocks_made, 1)
                for b in range(B):
                    hand_over(b, 1)
                for j in range(2):
                    for b in range(B):
                        act.wait_ge(kr_done, nth(b, 1))
                        spread(0, b, j, waited=False)

                def step(c, prev, nxt):
                    for j in range(2, NMB):
                        for b in range(B):
                            spread(c, b, j, waited=prev)
                    if prev:
                        for b in range(B):
                            drain_out(b, c)
                    if nxt:
                        for b in range(B):
                            drain_norm(b, c + 2)
                        for j in range(2):
                            for b in range(B):
                                act.wait_ge(kr_done, nth(b, c + 2))
                                spread(c + 1, b, j)
                    for b in range(B):
                        act.wait_ge(u_done, nth(b, (c + 1) * NMB))
                        if prev:
                            act.wait_ge(zn_done, nth(b, c))
                        act.activation(zs[:, b], z_ps[:, b, 0:D], ACT.Copy).then_inc(z_kept, 1)
                        if nxt:
                            hand_over(b, c + 2)

                walk(act, step)
                for b in range(B):
                    drain_out(b, NC)

            @block.vector
            def _(dve):
                def x_norm(c, b):
                    dve.bn_stats(stats[:, 0, b, :], flat(x[:, tile(c, b), :])).then_inc(x_stat, 1)

                def x_aggregate(b):
                    dve.bn_aggr(mv[:, 0, b, :], stats[:, 0, b, :]).then_inc(x_aggr, 1)

                def x_centre(c, b, n):
                    dve.wait_ge(x_rstd, nth(b, n))
                    dve.tensor_scalar(xn[:, b], flat(x[:, tile(c, b), :]), mv[:, 0, b, 0:1], rstd[:, 0, b:b + 1],
                                      ALU.subtract, ALU.mult).then_inc(xn_done, 1)

                def z_norm(b, n):
                    dve.wait_ge(z_kept, nth(b, n))
                    dve.bn_stats(stats[:, 1, b, :], zs[:, b]).then_inc(z_stat, 1)

                def z_aggregate(b):
                    dve.bn_aggr(mv[:, 1, b, :], stats[:, 1, b, :]).then_inc(z_aggr, 1)

                def z_centre(b, n):
                    dve.wait_ge(z_rstd, nth(b, n))
                    dve.tensor_scalar(zn[:, b], zs[:, b], mv[:, 1, b, 0:1], rstd[:, 1, b:b + 1],
                                      ALU.subtract, ALU.mult).then_inc(zn_done, 1)

                def out_rows(b, n):
                    dve.wait_ge(rows_full, nth(b, n))
                    dve.tensor_tensor(dx[:, b], proj[:, b, 0:D], gate_b[:, 1, 0, b, :], ALU.mult).then_inc(dx_done, 1)

                def split(b, n):
                    dve.wait_ge(h_done, nth(b, n))
                    dve.tensor_copy(h_hi[:, b], h[:, b]).then_inc(hi_done, 1)
                    dve.wait_ge(hi_done, nth(b, n))
                    dve.tensor_tensor(h_lo[:, b], h[:, b], h_hi[:, b].bitcast(F32), ALU.subtract).then_inc(hl_done, 1)

                def rope(c, b, n, waited=True):
                    dve.wait_ge(proj_full, nth(b, n))
                    if waited:
                        dve.wait_ge(kr_done, nth(b, n - 1))
                    hd = TD // 2
                    k = proj[:, b, 0:D]
                    cc = flat(cos[:, bass.ds(c, 1), :]).unsqueeze(1).broadcast_to([P, 2 * TH, hd])
                    ss = sin[:, bass.ds(c, 1), :].rearrange("p o (u d) -> p (o u) d", u=2).unsqueeze(1)
                    dve.tensor_tensor(t1[:, b].rearrange("p (g d) -> p g d", d=hd),
                                      k.rearrange("p (g d) -> p g d", d=hd), cc, ALU.mult)
                    dve.tensor_tensor(t2[:, b].rearrange("p (g u d) -> p g u d", u=2, d=hd),
                                      k.rearrange("p (g u d) -> p g u d", u=2, d=hd)[:, :, ::-1, :],
                                      ss.broadcast_to([P, TH, 2, hd]), ALU.mult).then_inc(rope_done, 1)

                def new_w(b, n):
                    dve.wait_ge(g_full, nth(b, n))
                    dve.tensor_tensor(w[:, b], g_ps[:, b, 0:D].rearrange("p (k e) -> p k e", k=KD),
                                      blocks[:].unsqueeze(1).broadcast_to([P, KD, P]), ALU.mult).then_inc(w_done, 1)

                for b in range(B):
                    x_norm(0, b)
                dve.wait_ge(x_stat, nth(1, 1))
                for b in range(B):
                    x_aggregate(b)
                dve.memset(k_diag[:], 0.0).then_inc(zeroed, 1)
                dve.tensor_scalar(ident_n[:], ident[:], 1.0 / INV_N, None, ALU.mult).then_inc(zeroed, 1)
                for b in range(B):
                    x_centre(0, b, 1)
                dve.wait_ge(w_in, 16)
                dve.tensor_copy(w_hi[:], stage[:]).then_inc(w_split, 1)
                dve.wait_ge(w_split, 1)
                dve.tensor_tensor(w_lo[:], stage[:], w_hi[:].bitcast(F32), ALU.subtract).then_inc(w_split, 1)
                dve.wait_ge(wo_in, 16 * 5)
                for b in range(B):
                    split(b, 1)
                for b in range(B):
                    rope(0, b, 1, waited=False)
                dve.wait_ge(blocks_made, 1)
                for b in range(B):
                    new_w(b, 1)

                def step(c, prev, nxt):
                    for n in range(NMB):
                        for b in range(B):
                            dve.wait_ge(z_full, nth(b, c * NMB + (n + 1)))
                            if n == 0:
                                dve.wait_ge(v_kept, nth(b, c + 1))
                            if n == 1 and b == 0 and prev:
                                dve.wait_ge(z_stat, nth(1, c))
                            if n == 1 and b == 0 and nxt:
                                dve.wait_ge(x_stat, nth(1, c + 2))
                            dve.tensor_tensor(u[:, b], v[:, b], z_ps[:, b, 0:D], ALU.subtract).then_inc(u_done, 1)
                        if n == 1 and prev:
                            for b in range(B):
                                z_aggregate(b)
                        if n == 1 and nxt:
                            for b in range(B):
                                x_aggregate(b)
                        for b in range(B):
                            new_w(b, c * NMB + (n + 2))
                        for b in range(B):
                            if n == 0 and prev:
                                z_norm(b, c)
                        for b in range(B):
                            if n == 0 and nxt:
                                x_norm(c + 1, b)
                        for b in range(B):
                            if n == 2 and prev:
                                z_centre(b, c)
                        for b in range(B):
                            if n == 2 and nxt:
                                x_centre(c + 1, b, c + 2)
                        for b in range(B):
                            if n == 4 and prev:
                                out_rows(b, c)
                        for b in range(B):
                            if n == 4 and nxt:
                                split(b, c + 2)
                        for b in range(B):
                            if n == 5 and nxt:
                                rope(c + 1, b, c + 2)

                walk(dve, step)
                for b in range(B):
                    z_norm(b, NC)
                dve.wait_ge(z_stat, nth(1, NC))
                for b in range(B):
                    z_aggregate(b)
                for b in range(B):
                    z_centre(b, NC)
                for b in range(B):
                    out_rows(b, NC)

            @block.tensor
            def _(pe):
                def norm_turn(b, n):
                    pe.wait_ge(xn_done, nth(b, n))
                    for k in range(KD):
                        t = pe.transpose(turn[:, b, k * P:(k + 1) * P], xn[:, b, k * P:(k + 1) * P], ident[:])
                    t.then_inc(xn_turned, 1)

                def out_turn(b, n):
                    pe.wait_ge(zn_done, nth(b, n))
                    for k in range(KD):
                        t = pe.transpose(turn[:, b, k * P:(k + 1) * P], zn[:, b, k * P:(k + 1) * P], ident[:])
                    t.then_inc(zn_turned, 1)

                def k_turn(b, n):
                    pe.wait_ge(kr_done, nth(b, n))
                    for k in range(KD):
                        t = pe.transpose(turn[:, b, k * P:(k + 1) * P], kr[:, b, k * P:(k + 1) * P], ident[:])
                    t.then_inc(k_turned, 1)

                def project(b, n):
                    pe.wait_ge(hl_done, nth(b, n))
                    for i, (hh, ww) in enumerate([(h_hi, w_hi), (h_hi, w_lo), (h_lo, w_hi)]):
                        for k in range(KD):
                            mm = pe.matmul(proj[:, b, :], hh[:, b, k], ww[:, k, :],
                                           start=(i == 0 and k == 0), stop=(i == 2 and k == KD - 1))
                    mm.then_inc(proj_full, 1)

                def out_rows(b, n):
                    pe.wait_ge(o_done, nth(b, n))
                    for k in range(KD):
                        mm = pe.matmul(proj[:, b, 0:D], o_t[:, b, k], wo[:, k, :], start=(k == 0), stop=(k == KD - 1))
                    mm.then_inc(rows_full, 1)

                pe.wait_ge(zeroed, 2)
                for b in range(B):
                    for k in range(KD):
                        mm = pe.matmul(g_ps[:, b, k * P:(k + 1) * P], ident[:], ident_n[:], start=(k == 0), stop=False,
                                       skip_group_check=True)
                    mm.then_inc(g_full, 1)
                for b in range(B):
                    norm_turn(b, 1)
                pe.wait_ge(w_split, 2)
                pe.wait_ge(wo_in, 16 * 5)
                for b in range(B):
                    project(b, 1)
                for b in range(B):
                    k_turn(b, 1)

                def step(c, prev, nxt):
                    for n in range(NMB):
                        for b in range(B):
                            pe.wait_ge(w_done, nth(b, c * NMB + (n + 1)))
                            if n == 0:
                                pe.wait_ge(k_diag_done, nth(b, c + 1))
                                if prev:
                                    pe.wait_ge(z_kept, nth(b, c))
                            for k in range(KD):
                                mm = pe.matmul(z_ps[:, b, k * P:(k + 1) * P], k_diag[:, b, k, n * P:(n + 1) * P],
                                               w[:, b, k], start=(n == 0 and k == 0), stop=(n == NMB - 1),
                                               skip_group_check=True)
                            mm.then_inc(z_full, 1)
                        if n == 3 and prev:
                            for b in range(B):
                                out_turn(b, c)
                        if n == 4 and prev:
                            for b in range(B):
                                out_rows(b, c)
                        if n == 4 and nxt:
                            for b in range(B):
                                norm_turn(b, c + 2)
                        if n == 5 and nxt:
                            for b in range(B):
                                if prev:
                                    pe.wait_ge(dx_done, nth(b, c))
                                else:
                                    pe.wait_ge(v_kept, nth(b, 1))
                                project(b, c + 2)
                        for b in range(B):
                            pe.wait_ge(u_done, nth(b, c * NMB + (n + 1)))
                            pe.wait_ge(k_rows_done, nth(b, c * NMB + (n + 1)))
                            for k in range(KD):
                                mm = pe.matmul(g_ps[:, b, k * P:(k + 1) * P], k_rows[:, b, n, k * P:(k + 1) * P],
                                               u[:, b, k * P:(k + 1) * P], start=False, stop=False, skip_group_check=True)
                            mm.then_inc(g_full, 1)
                        if n == 6 and nxt:
                            for b in range(B):
                                k_turn(b, c + 2)

                walk(pe, step)
                for b in range(B):
                    out_turn(b, NC)
                for b in range(B):
                    out_rows(b, NC)

    def moe_phase(self):
        nc, a = self.nc, self.a
        x, ident, mod_t, gate_b, half, eps = self.x, self.ident, self.mod_t, self.gate_b, self.half, self.eps
        TOK = GT * P
        NH = E + 2
        out = self.out.rearrange("b (c p) d -> p (b c) d", p=P)
        with ExitStack() as ctx:
            def sb(name, shape, dt=F32):
                return ctx.enter_context(nc.sbuf_tensor(name, shape, dt))

            def ps(name, shape, dt=F32):
                return ctx.enter_context(nc.psum_tensor(name, shape, dt))

            w1_hi, w1_lo = sb("w1_hi", [P, KD, NH * P], F32R), sb("w1_lo", [P, KD, NH * P], F32R)
            w1 = sb("w1_sb", [P, KD, NH * P])
            w2 = sb("w2_sb", [P, NH, D])
            b1, b2 = sb("b1_sb", [P, NH]), sb("b2_sb", [E + 1, D])
            gw = sb("gate_w_sb", [P, KD, E])
            stats, mv = sb("m_stats", [P, GT, 6]), sb("m_mv", [P, GT, 2])
            veps, rstd = sb("m_veps", [P, GT]), sb("m_rstd", [P, GT])
            xn = sb("m_xn", [P, GT, D])
            h = sb("m_h", [P, KD, TOK])
            h_hi, h_lo = sb("m_h_hi", [P, 2, KD, TOK], F32R), sb("m_h_lo", [P, 2, KD, TOK], F32R)
            act_t = sb("m_act", [P, 2, NH, TOK])
            lg, top = sb("logits_sb", [P, GT, E]), sb("top", [P, GT, E])
            at_u, at_f = sb("top_at", [P, GT, E], U32), sb("top_at_f", [P, GT, 2])
            lane = sb("lane", [P, E])
            euler = sb("euler", [P, 1])
            diff, ratio = sb("logit_diff", [P, GT]), sb("gate_ratio", [P, GT])
            total, pair = sb("gate_total", [P, GT]), sb("gate_pair", [P, 2, GT])
            pick = sb("picked", [P, 2, GT, E])
            gates = sb("gates", [P, 2, GT, E + 1])
            gates_t = sb("gates_t", [E + 1, 2, GT, P])
            acc = sb("m_acc", [P, 2, D])
            dx = sb("m_dx", [P, 2, D])

            turn = ps("m_turn", [P, 2, 512])
            hid = ps("m_hid", [P, 2, 512])
            small = ps("m_small", [P, 512])
            shared = ps("m_shared", [P, 512])
            expert = ps("m_expert", [P, 2, 512])

            names = ("w1_in w_in w_split const_made stat_done aggr_done veps_done rstd_done xn_done turn_full h_done hi_done "
                     "hl_done logit_full logit_kept top_step gate_step ratio_done gates_done gturn_full gturn_done "
                     "hid_full act_done shared_full shared_kept expert_full expert_done acc_step dx_done x_done out_done")
            s = {n: self.sem("m_" + n) for n in names.split()}
            block = ctx.enter_context(nc.Block())

            @block.sync
            def _(sp):
                sp.dma_start(w1[:], a["w1"].rearrange("(k p) n -> p k n", p=P)).then_inc(s["w1_in"], 16)
                sp.dma_start(gw[:], a["gw"].rearrange("(k p) n -> p k n", p=P)).then_inc(s["w_in"], 16)
                sp.dma_start(b1[:], a["b1"]).then_inc(s["w_in"], 16)
                sp.dma_start(b2[:], a["b2"]).then_inc(s["w_in"], 16)
                sp.dma_start(w2[:], a["w2"].rearrange("(m p) n -> p m n", p=P)).then_inc(s["w_in"], 16)
                for n in range(NT):
                    sp.wait_ge(s["x_done"], n + 1)
                    sp.dma_start(out[:, n, :], x[:, n, :]).then_inc(s["out_done"], 16)
                sp.wait_ge(s["out_done"], 16 * NT)

            @block.gpsimd
            def _(pool):
                pool.iota(lane[:], pattern=[[1, E]], base=0, channel_multiplier=0, allow_small_or_imprecise_dtypes=True)
                pool.memset(euler[:], float(np.e)).then_inc(s["const_made"], 1)

                def rstd_of(g):
                    pool.wait_ge(s["aggr_done"], GT * (g + 1))
                    pool.tensor_tensor(veps[:], mv[:, :, 1], eps[:].broadcast_to([P, GT]), ALU.add).then_inc(s["veps_done"], 1)
                    pool.wait_ge(s["veps_done"], g + 1)
                    pool.tensor_tensor(rstd[:], veps[:], half[:].broadcast_to([P, GT]), ALU.pow).then_inc(s["rstd_done"], 1)

                def ratio_of(g):
                    pool.wait_ge(s["top_step"], 3 * g + 3)
                    pool.tensor_tensor(ratio[:], euler[:].broadcast_to([P, GT]), diff[:], ALU.pow).then_inc(s["ratio_done"], 1)

                def add_rows(g):
                    for i in range(GT):
                        n = g * GT + i
                        pool.wait_ge(s["dx_done"], n + 1)
                        pool.tensor_tensor(x[:, n, :], x[:, n, :], dx[:, n % 2], ALU.add).then_inc(s["x_done"], 1)

                pool.wait_ge(s["const_made"], 1)
                rstd_of(0)
                ratio_of(0)
                for g in range(NG):
                    if g + 1 < NG:
                        rstd_of(g + 1)
                        ratio_of(g + 1)
                    add_rows(g)

            @block.scalar
            def _(act):
                act.wait_ge(s["w_in"], 16 * 4)

                def drain_norm(g):
                    b = g * GT // NC
                    for k in range(KD):
                        act.wait_ge(s["turn_full"], KD * g + k + 1)
                        if g:
                            act.wait_ge(s["hl_done"], g)
                            act.wait_ge(s["logit_full"], g)
                        act.activation(h[:, k, :], turn[:, k, :], ACT.Identity,
                                       bias=mod_t[:, 1, SB_ * KD + k, b:b + 1],
                                       scale=mod_t[:, 1, CB * KD + k, b:b + 1]).then_inc(s["h_done"], 1)

                def gates_turned(g):
                    act.wait_ge(s["gturn_full"], g + 1)
                    act.activation(gates_t[:, g % 2], small[0:E + 1, :].rearrange("p (i t) -> p i t", i=GT), ACT.Copy
                                   ).then_inc(s["gturn_done"], 1)

                def hidden(g, m):
                    n = g * NH + m
                    act.wait_ge(s["hid_full"], n + 1)
                    act.activation(act_t[:, g % 2, m], hid[:, n % 2, :], ACT.Gelu, bias=b1[:, m:m + 1]
                                   ).then_inc(s["act_done"], 1)

                def keep_shared(n):
                    act.wait_ge(s["shared_full"], n + 1)
                    if n >= 2:
                        act.wait_ge(s["dx_done"], n - 1)
                    act.activation(acc[:, n % 2], shared[:, 0:D], ACT.Copy).then_inc(s["shared_kept"], 1)

                drain_norm(0)
                gates_turned(0)
                for m in range(NH):
                    hidden(0, m)
                for g in range(NG):
                    if g + 1 < NG:
                        drain_norm(g + 1)
                        gates_turned(g + 1)
                    for m in range(NH if g + 1 < NG else 0):
                        hidden(g + 1, m)
                        if m % 2 == 0 and m // 2 < GT:
                            keep_shared(g * GT + m // 2)
                    if g + 1 == NG:
                        for i in range(GT):
                            keep_shared(g * GT + i)

            @block.vector
            def _(dve):
                def norms(g):
                    for i in range(GT):
                        dve.bn_stats(stats[:, i, :], x[:, g * GT + i, :]).then_inc(s["stat_done"], 1)
                    for i in range(GT):
                        dve.wait_ge(s["stat_done"], g * GT + i + 1)
                        dve.bn_aggr(mv[:, i, :], stats[:, i, :]).then_inc(s["aggr_done"], 1)

                def centre(g):
                    dve.wait_ge(s["rstd_done"], g + 1)
                    if g:
                        dve.wait_ge(s["turn_full"], KD * g)
                    for i in range(GT):
                        dve.tensor_scalar(xn[:, i, :], x[:, g * GT + i, :], mv[:, i, 0:1], rstd[:, i:i + 1],
                                          ALU.subtract, ALU.mult).then_inc(s["xn_done"], 1)

                def split(g):
                    dve.wait_ge(s["h_done"], KD * (g + 1))
                    dve.tensor_copy(h_hi[:, g % 2], h[:]).then_inc(s["hi_done"], 1)
                    dve.wait_ge(s["hi_done"], g + 1)
                    dve.tensor_tensor(h_lo[:, g % 2], h[:], h_hi[:, g % 2].bitcast(F32), ALU.subtract
                                      ).then_inc(s["hl_done"], 1)

                def gating(g):
                    q = g % 2
                    dve.wait_ge(s["logit_full"], g + 1)
                    dve.tensor_copy(lg[:], small[:, 0:GT * E].rearrange("p (i e) -> p i e", e=E)).then_inc(s["logit_kept"], 1)
                    dve.wait_ge(s["logit_kept"], g + 1)
                    for i in range(GT):
                        t = dve.max(top[:, i], lg[:, i])
                    t.then_inc(s["top_step"], 1)
                    dve.wait_ge(s["top_step"], 3 * g + 1)
                    for i in range(GT):
                        t = dve.max_index(at_u[:, i], top[:, i], lg[:, i])
                    t.then_inc(s["top_step"], 1)
                    dve.tensor_tensor(diff[:], top[:, :, 1], top[:, :, 0], ALU.subtract).then_inc(s["top_step"], 1)
                    dve.wait_ge(s["top_step"], 3 * g + 3)
                    base = 6 * g
                    dve.tensor_copy(at_f[:], at_u[:, :, 0:2]).then_inc(s["gate_step"], 1)
                    dve.wait_ge(s["ratio_done"], g + 1)
                    dve.tensor_scalar(total[:], ratio[:], 1.0, None, ALU.add).then_inc(s["gate_step"], 1)
                    dve.wait_ge(s["gate_step"], base + 2)
                    dve.reciprocal(pair[:, 0], total[:]).then_inc(s["gate_step"], 1)
                    dve.wait_ge(s["gate_step"], base + 3)
                    dve.tensor_tensor(pair[:, 1], ratio[:], pair[:, 0], ALU.mult)
                    for k in range(2):
                        t = dve.tensor_tensor(pick[:, k], lane[:].unsqueeze(1).broadcast_to([P, GT, E]),
                                              at_f[:, :, k:k + 1].broadcast_to([P, GT, E]), ALU.is_equal)
                    t.then_inc(s["gate_step"], 1)
                    dve.wait_ge(s["gate_step"], base + 4)
                    for k in range(2):
                        t = dve.tensor_tensor(pick[:, k], pick[:, k], pair[:, k].unsqueeze(2).broadcast_to([P, GT, E]),
                                              ALU.mult)
                    t.then_inc(s["gate_step"], 1)
                    dve.wait_ge(s["gate_step"], base + 5)
                    dve.tensor_tensor(gates[:, q, :, 0:E], pick[:, 0], pick[:, 1], ALU.add).then_inc(s["gates_done"], 1)
                    dve.memset(total[:], 0.0).then_inc(s["gate_step"], 1)

                def weigh(g, i, k):
                    n = g * GT + i
                    dve.wait_ge(s["expert_full"], 4 * n + k + 1)
                    if k == 0:
                        dve.wait_ge(s["shared_kept"], n + 1)
                    for j in range(2):
                        e = 2 * k + j
                        if e:
                            dve.wait_ge(s["acc_step"], E * n + e)
                        ins = dve.scalar_tensor_tensor(acc[:, n % 2], expert[:, k % 2, j * D:(j + 1) * D],
                                                       gates[:, g % 2, i, e:e + 1], acc[:, n % 2], ALU.mult, ALU.add)
                        ins.then_inc(s["acc_step"], 1)

                def gate_rows(g, i):
                    n = g * GT + i
                    b = g * GT // NC
                    dve.wait_ge(s["acc_step"], E * (n + 1))
                    if n >= 2:
                        dve.wait_ge(s["x_done"], n - 1)
                    dve.tensor_tensor(dx[:, n % 2], acc[:, n % 2], gate_b[:, 1, 1, b, :], ALU.mult).then_inc(s["dx_done"], 1)

                dve.memset(gates[:], 1.0)
                norms(0)
                centre(0)
                dve.wait_ge(s["w1_in"], 16)
                dve.tensor_copy(w1_hi[:], w1[:]).then_inc(s["w_split"], 1)
                dve.wait_ge(s["w_split"], 1)
                dve.tensor_tensor(w1_lo[:], w1[:], w1_hi[:].bitcast(F32), ALU.subtract).then_inc(s["w_split"], 1)
                split(0)
                dve.wait_ge(s["const_made"], 1)
                gating(0)
                for g in range(NG):
                    if g + 1 < NG:
                        norms(g + 1)
                        centre(g + 1)
                        split(g + 1)
                        gating(g + 1)
                    for i in range(GT):
                        for k in range(E // 2):
                            weigh(g, i, k)
                        gate_rows(g, i)

            @block.tensor
            def _(pe):
                def norm_turn(g):
                    pe.wait_ge(s["xn_done"], GT * (g + 1))
                    for k in range(KD):
                        if g:
                            pe.wait_ge(s["h_done"], KD * (g - 1) + k + 1)
                        for i in range(GT):
                            t = pe.transpose(turn[:, k, i * P:(i + 1) * P], xn[:, i, k * P:(k + 1) * P], ident[:])
                        t.then_inc(s["turn_full"], 1)

                def logits(g):
                    pe.wait_ge(s["h_done"], KD * (g + 1))
                    if g:
                        pe.wait_ge(s["gturn_done"], g)
                    for i in range(GT):
                        for k in range(KD):
                            mm = pe.matmul(small[:, i * E:(i + 1) * E], h[:, k, i * P:(i + 1) * P], gw[:, k, :],
                                           start=(k == 0), stop=(k == KD - 1))
                    mm.then_inc(s["logit_full"], 1)

                def gates_turn(g):
                    pe.wait_ge(s["gates_done"], g + 1)
                    for i in range(GT):
                        t = pe.transpose(small[0:E + 1, i * P:(i + 1) * P], gates[:, g % 2, i, :], ident[:])
                    t.then_inc(s["gturn_full"], 1)

                def hidden(g, m):
                    n = g * NH + m
                    if n >= 2:
                        pe.wait_ge(s["act_done"], n - 1)
                    cols = slice(m * P, (m + 1) * P)
                    for i, (ww, hh) in enumerate([(w1_hi, h_hi), (w1_lo, h_hi), (w1_hi, h_lo)]):
                        for k in range(KD):
                            mm = pe.matmul(hid[:, n % 2, :], ww[:, k, cols], hh[:, g % 2, k, :],
                                           start=(i == 0 and k == 0), stop=(i == 2 and k == KD - 1))
                    mm.then_inc(s["hid_full"], 1)

                def tile_rows(g, i):
                    n = g * GT + i
                    toks = slice(i * P, (i + 1) * P)
                    if n:
                        pe.wait_ge(s["shared_kept"], n)
                    pe.wait_ge(s["gturn_done"], g + 1)
                    pe.wait_ge(s["act_done"], (g + 1) * NH)
                    pe.matmul(shared[:, 0:D], gates_t[:, g % 2, i, :], b2[:], start=True, stop=False)
                    for m in range(E, NH):
                        mm = pe.matmul(shared[:, 0:D], act_t[:, g % 2, m, toks], w2[:, m, :], start=False, stop=(m == NH - 1))
                    mm.then_inc(s["shared_full"], 1)
                    for k in range(E // 2):
                        if 4 * n + k >= 2:
                            pe.wait_ge(s["acc_step"], 2 * (4 * n + k - 1))
                        for j in range(2):
                            e = 2 * k + j
                            mm = pe.matmul(expert[:, k % 2, j * D:(j + 1) * D], act_t[:, g % 2, e, toks], w2[:, e, :],
                                           start=True, stop=True)
                        mm.then_inc(s["expert_full"], 1)

                norm_turn(0)
                pe.wait_ge(s["w_in"], 16 * 4)
                logits(0)
                pe.wait_ge(s["w_split"], 2)
                pe.wait_ge(s["hl_done"], 1)
                gates_turn(0)
                for m in range(NH):
                    hidden(0, m)
                for g in range(NG):
                    if g + 1 < NG:
                        norm_turn(g + 1)
                        logits(g + 1)
                        pe.wait_ge(s["hl_done"], g + 2)
                        gates_turn(g + 1)
                    for m in range(NH):
                        if g + 1 < NG:
                            hidden(g + 1, m)
                        if m % 2 == 0 and m // 2 < GT:
                            tile_rows(g, m // 2)


def rope_tables(length, dim):
    power = np.arange(0, dim, 2, dtype=np.float32) / np.float32(dim)
    inv_freq = np.float32(1.0) / np.power(10000.0, power.astype(np.float64)).astype(np.float32)
    angle = np.outer(np.arange(length, dtype=np.float32), inv_freq).astype(np.float32).astype(np.float64)
    sin = np.sin(angle)
    return np.cos(angle).astype(np.float32), np.concatenate([-sin, sin], axis=1).astype(np.float32)


def kernel(**inputs):
    import concourse.bacc as bacc
    from concourse.bass_utils import run_bass_kernel_spmd

    i = {k: np.asarray(v) for k, v in inputs.items()}
    cos, sin = rope_tables(S, HD)
    cos1, sin1 = rope_tables(S, TD)
    quads = np.arange(FI).reshape(FI // 512, P, 4).transpose(0, 2, 1).reshape(-1)
    arrays = {
        "x": i["L0_attn_x"],
        "cond": np.stack([i[f"L{n}_c"].T.reshape(KD, P, B).transpose(1, 0, 2) for n in range(2)], axis=1),
        "wmod": np.stack([i["L0_wmod"], i["L1_wmod"]]),
        "wqkv": np.concatenate([i["L0_attn_Wk"].T, i["L0_attn_Wv"].T, i["L0_attn_Wq"].T], axis=1),
        "wo": i["L0_attn_Wo"].T,
        "cos": cos, "sin": sin, "cos1": cos1, "sin1": sin1,
        "wgu": np.concatenate([i["L0_ffn_w_gate"][:, quads], i["L0_ffn_w_up"][:, quads]], axis=1),
        "wd": i["L0_ffn_w_down"][quads, :],
        "wkv1": np.concatenate([i["L1_attn_Wk"].T, i["L1_attn_Wv"].T], axis=1),
        "wo1": i["L1_attn_Wo"].T,
        "ln_g": i["L1_attn_ln_gamma"], "ln_b": i["L1_attn_ln_beta"],
        "gw": i["L1_ffn_gate_w"],
        "w1": np.concatenate([i["L1_ffn_w1"].transpose(1, 0, 2).reshape(D, E * EH), i["L1_ffn_shared_w1"]], axis=1),
        "b1": np.concatenate([i["L1_ffn_b1"], i["L1_ffn_shared_b1"].reshape(2, EH)], axis=0).T,
        "w2": np.concatenate([i["L1_ffn_w2"].reshape(E * EH, D), i["L1_ffn_shared_w2"]], axis=0),
        "b2": np.concatenate([i["L1_ffn_b2"], i["L1_ffn_shared_b2"][None]], axis=0),
    }
    arrays = {k: np.ascontiguousarray(v) for k, v in arrays.items()}
    nc = bacc.Bacc("TRN2", target_bir_lowering=False, num_devices=1)
    aps = {k: nc.dram_tensor(f"in_{k}", v.shape, mybir.dt.from_np(v.dtype), kind="ExternalInput").ap()
           for k, v in arrays.items()}
    out = nc.dram_tensor("out", (B, S, D), F32, kind="ExternalOutput").ap()
    build(nc, aps, out)
    r = run_bass_kernel_spmd(nc, [{f"in_{k}": v for k, v in arrays.items()}], core_ids=[0])
    return r.results[0]["out"]
```

```python
from contextlib import ExitStack

import numpy as np

import concourse.bass as bass
from concourse import mybir

F32 = mybir.dt.float32
F32R = mybir.dt.float32r
BF16 = mybir.dt.bfloat16
U32 = mybir.dt.uint32
ALU = mybir.AluOpType
ACT = mybir.ActivationFunctionType
AX = mybir.AxisListType

P = 128
B, S, D = 2, 1024, 256
KD = D // P
NC = S // P
NT = B * NC
LN_EPS = 1e-5

H, KVH, HD = 16, 4, 128
REP = H // KVH
GW = REP * HD
QKV = (H + 2 * KVH) * HD
DEN_EPS = 1e-6
VW = HD + 1

FI = 1024
NM = FI // P
TH = 16
TD = D // TH
MB = 16
NMB = P // MB
INV_N = 2.0 / (MB * TD)
E, EH = 8, 128
GT = 4
NG = NT // GT

WCH = 512

SA, CA, GA, SB_, CB, GB = range(6)


def at(c, b, per, k):
    return c * (2 * per) + (per * b + k)


def build(nc, a, out):
    with ExitStack() as keep:
        Program(nc, a, out, keep).run()


class Program:
    def __init__(self, nc, a, out, keep):
        self.nc, self.a, self.out, self.keep = nc, a, out, keep

    def sem(self, name):
        return self.keep.enter_context(self.nc.semaphore(name))

    def run(self):
        nc = self.nc

        def sb(name, shape, dt=F32):
            return self.keep.enter_context(nc.sbuf_tensor(name, shape, dt))

        self.x = sb("x_sb", [P, NT, D])
        self.ident = sb("ident", [P, P])
        self.mod_t = sb("mod_t", [P, 2, 6 * KD, B])
        self.gate_b = sb("gate_b", [P, 2, 2, B, D])
        self.half = sb("minus_half", [P, 1])
        self.eps = sb("eps", [P, 1])
        self.w_hi, self.w_lo = sb("w_hi", [P, KD, QKV], F32R), sb("w_lo", [P, KD, QKV], F32R)
        self.stage = sb("w_stage", [P, 2, KD, WCH])
        self.scond = sb("silu_cond", [P, 2, KD, B])
        self.wide = sb("silu_cond_wide", [P, 2 * KD * B, P])
        self.w_in = [self.sem(f"w_in{i}") for i in range(2)]
        self.w_half = self.sem("w_half")
        self.w_ready = self.sem("w_ready")
        self.attention_phase()
        self.ffn_phase()
        self.scan_phase()
        self.moe_phase()

    def load_chunk(self, sp, n, src, width=WCH):
        if n >= 2:
            sp.wait_ge(self.w_ready, n - 1)
        sp.dma_start(self.stage[:, n % 2, :, 0:width], src.rearrange("(k p) n -> p k n", p=P)
                     ).then_inc(self.w_in[n % 2], 16)

    def split_chunk(self, dve, n, col, width=WCH):
        cols = slice(col, col + width)
        dve.wait_ge(self.w_in[n % 2], 16 * (n // 2 + 1))
        dve.tensor_copy(self.w_hi[:, :, cols], self.stage[:, n % 2, :, 0:width]).then_inc(self.w_half, 1)
        dve.wait_ge(self.w_half, n + 1)
        dve.tensor_tensor(self.w_lo[:, :, cols], self.stage[:, n % 2, :, 0:width],
                          self.w_hi[:, :, cols].bitcast(F32), ALU.subtract).then_inc(self.w_ready, 1)

    def modulation(self, l, wmod, scond, wide, sems, mod_ps, gate_ps, gmag, gneg):
        nc, mod_t, gate_b = self.nc, self.mod_t, self.gate_b
        s = sems

        def pe_vectors(pe, lo, hi, first):
            for m in range(lo * KD, hi * KD):
                for k in range(KD):
                    mm = pe.matmul(mod_ps[:, m * B:(m + 1) * B], wmod[:, k, m * P:(m + 1) * P], scond[:, l, k, :],
                                   start=(first and m == lo * KD and k == 0), stop=(k == KD - 1), skip_group_check=True)
            mm.then_inc(s["mod_full"], 1)

        def pe_gates(pe):
            for i, kind in enumerate((GA, GB)):
                for b in range(B):
                    for k in range(KD):
                        mm = pe.matmul(gate_ps[i * B + b], wide[:, (l * KD + k) * B + b, :],
                                       wmod[:, k, kind * D:(kind + 1) * D], start=(k == 0), stop=(k == KD - 1))
            mm.then_inc(s["gates_full"], 1)

        def dve_vectors(dve, lo, hi, n):
            dve.wait_ge(s["mod_full"], n)
            v = mod_t[:, l, lo * KD:hi * KD]
            dve.tensor_copy(v, mod_ps[:, lo * KD * B:hi * KD * B].rearrange("p (m b) -> p m b", b=B)
                            ).then_inc(s["mod_kept"], 1)
            dve.wait_ge(s["mod_kept"], n)
            for kind in (CA, CB):
                if lo <= kind < hi:
                    v = mod_t[:, l, kind * KD:(kind + 1) * KD]
                    dve.tensor_scalar(v, v, 1.0, None, ALU.add).then_inc(s["mod_done"], 1)

        def dve_gates(dve):
            dve.wait_ge(s["gates_full"], 1)
            for i in range(2 * B):
                dve.tensor_scalar(gneg[:, i], gate_ps[i], 0.0, 2.0, ALU.is_ge, ALU.mult)
                t = dve.tensor_scalar(gmag[:, i], gate_ps[i], -1.0, None, ALU.mult)
            t.then_inc(s["gate_step"], 1)
            dve.wait_ge(s["gate_step"], 1)
            for i in range(2 * B):
                t = dve.tensor_tensor(gmag[:, i], gate_ps[i], gmag[:, i], ALU.max)
            t.then_inc(s["gate_step"], 1)
            dve.wait_ge(s["gate_step"], 2)
            dve.tensor_scalar(gmag, gmag, 0.25, None, ALU.max).then_inc(s["gate_step"], 1)
            dve.wait_ge(s["gate_step"], 3)
            dve.scalar_tensor_tensor(gate_b[:, l].rearrange("p g b d -> p (g b) d"), gneg, -1.0, gmag,
                                     ALU.add, ALU.mult).then_inc(s["gate_done"], 1)
            dve.wait_ge(s["gate_done"], 1)

        return pe_vectors, pe_gates, dve_vectors, dve_gates

    def modulation_sems(self, l):
        return {n: self.sem(f"{n}{l}") for n in "mod_full mod_kept mod_done gates_full gate_step gate_done".split()}

    def attention_phase(self):
        nc, a = self.nc, self.a
        x, ident, mod_t, gate_b, half, eps = self.x, self.ident, self.mod_t, self.gate_b, self.half, self.eps
        NW = QKV // WCH
        RI = 1 + KVH
        with ExitStack() as ctx:
            def sb(name, shape, dt=F32):
                return ctx.enter_context(nc.sbuf_tensor(name, shape, dt))

            def ps(name, shape, dt=F32):
                return ctx.enter_context(nc.psum_tensor(name, shape, dt))

            w_hi, w_lo = self.w_hi, self.w_lo
            wmod = sb("a_wmod", [P, KD, 6 * D])
            cond, scond = sb("cond", [P, 2, KD, B]), self.scond
            wide = self.wide
            wo = sb("wo_sb", [P, H, D])
            cos, sin = sb("cos_sb", [P, NC, HD // 2]), sb("sin_sb", [P, NC, HD])
            causal = sb("causal", [P, P])
            stats, mv = sb("a_stats", [P, 2, 6]), sb("a_mv", [P, 2, 2])
            rstd, veps = sb("a_rstd", [P, 2]), sb("a_veps", [P, 2])
            xn = sb("a_xn", [P, 2, D])
            h = sb("a_h", [P, 2, KD, P])
            h_hi, h_lo = sb("a_h_hi", [P, 2, KD, P], F32R), sb("a_h_lo", [P, 2, KD, P], F32R)
            t1, t2 = sb("rope_cos", [P, 2, GW]), sb("rope_sin", [P, 2, GW])
            y, ex = sb("rope_sum", [P, 2, GW]), sb("rope_exp", [P, 2, GW])
            feat = sb("feat", [P, 2, RI, GW])
            k_t, q_t = sb("k_t", [P, KVH, P]), sb("q_t", [P, KVH, REP * P])
            v = sb("v_ones", [P, 2, KVH, VW])
            am = sb("score_masked", [P, 2, REP * P])
            on = sb("attn_out", [P, 2, GW])
            o_t = sb("attn_out_t", [P, H, P])
            state = sb("state", [P, 2, KVH, VW])
            den, rden = sb("den", [P, REP]), sb("rden", [P, REP])
            dx = sb("a_dx", [P, D])

            proj = ps("proj", [P, 2, 512])
            turn = ps("turn", [P, 2, 512])
            score = ps("score", [P, 2, 512])
            num = ps("num", [P, 2, 512])

            names = ("cond_in wmod_in x_in wo_in tab_in ident_zero const_made silu_done wide_done causal_made stat_done aggr_done veps_done rstd_done xn_done "
                     "hi_done hl_done proj_full proj_free turn_full turn_free score_full score_free num_full num_free "
                     "y_done relu_done exp_done feat_done den_done rden_done dx_done x_done cos_done mask_one")
            s = {n: self.sem("a_" + n) for n in names.split()}
            self.const_made = s["const_made"]
            msem = self.modulation_sems(0)
            pe_vectors, pe_gates, dve_vectors, dve_gates = self.modulation(
                0, wmod, scond, wide, msem, score[:, 0, :], [num[:, i // 2, i % 2 * D:(i % 2 + 1) * D] for i in range(2 * B)],
                t1[:].rearrange("p i (u d) -> p (i u) d", d=D), y[:].rearrange("p i (u d) -> p (i u) d", d=D))
            block = ctx.enter_context(nc.Block())

            def proj_item(c, b, j):
                return at(c, b, 7, 6 + j)

            def turn_item(c, b, j):
                return at(c, b, 10, 2 + j - (1 if last(c, b) else 0))

            def last(c, b):
                return isinstance(c, int) and c == NC - 1 and b == 1

            def walk(engine, step):
                with nc.Fori(0, NC - 1, engines=(engine.engine,), hint_back_edge=True) as c:
                    step(c, 0, True, True)
                    step(c, 1, True, True)
                step(NC - 1, 0, True, False)
                step(NC - 1, 1, False, False)

            @block.sync
            def _(sp):
                xr = a["x"].rearrange("b (c p) d -> p b c d", p=P)
                xs = x[:].rearrange("p (b c) d -> p b c d", b=B)

                def chunk(i):
                    self.load_chunk(sp, i, a["wqkv"][:, i * WCH:(i + 1) * WCH])

                sp.dma_start(cond[:], a["cond"]).then_inc(s["cond_in"], 16)
                wm = a["wmod"][0].rearrange("(k p) n -> p k n", p=P)
                sp.dma_start(wmod[:, :, 0:GA * D], wm[:, :, 0:GA * D]).then_inc(s["wmod_in"], 16)
                sp.dma_start(xs[:, :, 0, :], xr[:, :, 0, :]).then_inc(s["x_in"], 16)
                chunk(0)
                chunk(1)
                sp.dma_start(cos[:], a["cos"].rearrange("(c p) d -> p c d", p=P)).then_inc(s["tab_in"], 16)
                sp.dma_start(sin[:], a["sin"].rearrange("(c p) d -> p c d", p=P)).then_inc(s["tab_in"], 16)
                chunk(2)
                chunk(3)
                for b in range(B):
                    sp.dma_start(xs[:, b, 1:NC], xr[:, b, 1:NC]).then_inc(s["x_in"], 16)
                chunk(4)
                chunk(5)
                sp.dma_start(wmod[:, :, GA * D:6 * D], wm[:, :, GA * D:6 * D]).then_inc(s["wmod_in"], 16)
                sp.dma_start(wo[:], a["wo"].rearrange("(h p) n -> p h n", p=P)).then_inc(s["wo_in"], 16)
                for i in range(2 * FI // WCH):
                    self.load_chunk(sp, NW + i, a["wgu"][:, i * WCH:(i + 1) * WCH])

            @block.gpsimd
            def _(pool):
                pool.memset(ident[:], 0.0).then_inc(s["ident_zero"], 1)
                pool.memset(half[:], -0.5)
                pool.memset(eps[:], LN_EPS)
                pool.wait_ge(s["ident_zero"], 1)
                pool.affine_select(out=ident[:], in_=ident[:], compare_op=ALU.not_equal, fill=1.0, base=0,
                                   pattern=[[-1, P]], channel_multiplier=1).then_inc(s["const_made"], 1)
                pool.wait_ge(s["const_made"], 1)
                pool.memset(causal[:], 1.0).then_inc(s["mask_one"], 1)
                pool.wait_ge(s["mask_one"], 1)
                pool.affine_select(out=causal[:], in_=causal[:], compare_op=ALU.is_ge, fill=0.0, base=0,
                                   pattern=[[1, P]], channel_multiplier=-1).then_inc(s["causal_made"], 1)

                def rstd_of(n, b):
                    pool.wait_ge(s["aggr_done"], n)
                    pool.tensor_tensor(veps[:, b:b + 1], mv[:, b, 1:2], eps[:], ALU.add).then_inc(s["veps_done"], 1)
                    pool.wait_ge(s["veps_done"], n)
                    pool.tensor_tensor(rstd[:, b:b + 1], veps[:, b:b + 1], half[:], ALU.pow).then_inc(s["rstd_done"], 1)

                def add_rope(item, parity, drained, first=False):
                    pool.wait_ge(s["proj_free"], drained)
                    if not first:
                        pool.wait_ge(s["feat_done"], item - 1)
                    pool.tensor_tensor(y[:, parity], t1[:, parity], t2[:, parity], ALU.add).then_inc(s["y_done"], 1)

                rstd_of(1, 0)
                rstd_of(2, 1)
                for r in range(RI):
                    add_rope(r, r % 2, 2 + (r + 1 if r else 0) + 1, first=r < 2)

                def step(c, b, nxt, norm):
                    if norm:
                        rstd_of(at(c, b, 1, 3), b)
                    if nxt:
                        for r in range(RI):
                            j = r + 1 if r else 0
                            add_rope(at(c, b, RI, RI + r), (b + 1 + r) % 2, 2 + 1 + proj_item(c, b, j))

                walk(pool, step)

            @block.scalar
            def _(act):
                def drain_turn(c, b, j, dst, src):
                    n = turn_item(c, b, j)
                    act.wait_ge(s["turn_full"], n + 1)
                    act.activation(dst, src, ACT.Copy).then_inc(s["turn_free"], 1)

                def drain_norm(n, parity, bank, b):
                    act.wait_ge(s["turn_full"], n + 1)
                    for k in range(KD):
                        i = act.activation(h[:, parity, k, :], turn[:, bank, k * P:(k + 1) * P], ACT.Identity,
                                           bias=mod_t[:, 0, SA * KD + k, b:b + 1], scale=mod_t[:, 0, CA * KD + k, b:b + 1])
                    i.then_inc(s["turn_free"], 1)

                def exp_of(item, parity):
                    act.wait_ge(s["y_done"], item + 1)
                    act.activation(ex[:, parity], y[:, parity], ACT.Relu, scale=-1.0).then_inc(s["relu_done"], 1)
                    act.wait_ge(s["relu_done"], item + 1)
                    act.activation(ex[:, parity], ex[:, parity], ACT.Exp, scale=-1.0).then_inc(s["exp_done"], 1)

                act.wait_ge(s["cond_in"], 16)
                act.activation(scond[:], cond[:], ACT.Silu).then_inc(s["silu_done"], 1)
                act.wait_ge(msem["mod_done"], 1)
                drain_norm(0, 0, 0, 0)
                drain_norm(1, 1, 1, 1)
                for r in range(RI):
                    exp_of(r, r % 2)

                def step(c, b, nxt, norm):
                    tp = 1 if last(c, b) else 0

                    def bank(j):
                        return (j + tp) % 2

                    def e(r):
                        if nxt:
                            exp_of(at(c, b, RI, RI + r), (b + 1 + r) % 2)

                    drain_turn(c, b, 0, k_t[:], turn[:, bank(0), :].rearrange("p (g t) -> p g t", g=KVH))
                    for g in range(KVH):
                        drain_turn(c, b, 1 + g, q_t[:, g], turn[:, bank(1 + g), :])
                        if g == 2:
                            e(0)
                    for g in range(KVH):
                        drain_turn(c, b, 5 + g, o_t[:, g * REP:(g + 1) * REP, :],
                                   turn[:, bank(5 + g), :].rearrange("p (r t) -> p r t", r=REP))
                        e(1 + g)
                    if norm:
                        drain_norm(turn_item(c, b, 9), b, bank(9), b)

                walk(act, step)

            @block.vector
            def _(dve):
                dve.memset(state[:], 0.0)
                dve.memset(v[:, :, :, HD:VW], 1.0)
                dve.memset(dx[:], 0.0).then_inc(s["proj_free"], 2)
                dve.memset(h[:], 0.0).then_inc(s["turn_free"], 2)

                def norm(t, b):
                    dve.bn_stats(stats[:, b, :], x[:, t, :]).then_inc(s["stat_done"], 1)

                def aggregate(b):
                    dve.bn_aggr(mv[:, b, :], stats[:, b, :]).then_inc(s["aggr_done"], 1)

                def centre(t, n, b):
                    dve.wait_ge(s["rstd_done"], n)
                    dve.tensor_scalar(xn[:, b, :], x[:, t, :], mv[:, b, 0:1], rstd[:, b:b + 1],
                                      ALU.subtract, ALU.mult).then_inc(s["xn_done"], 1)

                def split(n, parity, drained):
                    dve.wait_ge(s["turn_free"], drained)
                    dve.tensor_copy(h_hi[:, parity], h[:, parity]).then_inc(s["hi_done"], 1)
                    dve.wait_ge(s["hi_done"], n)
                    dve.tensor_tensor(h_lo[:, parity], h[:, parity], h_hi[:, parity].bitcast(F32),
                                      ALU.subtract).then_inc(s["hl_done"], 1)

                def rope(item, parity, bank, c, n, first=False):
                    heads = proj[:, bank, :].rearrange("p (g d) -> p g d", d=HD)
                    halves = heads.rearrange("p g (u d) -> p g u d", u=2)
                    cc = cos[:, bass.ds(c, 1), :].rearrange("p o d -> p (o d)").unsqueeze(1)
                    ss = sin[:, bass.ds(c, 1), :].rearrange("p o (u d) -> p (o u) d", u=2).unsqueeze(1)
                    dve.wait_ge(s["proj_full"], n + 1)
                    if not first:
                        dve.wait_ge(s["y_done"], item - 1)
                    dve.tensor_tensor(t1[:, parity].rearrange("p (g d) -> p g d", d=HD // 2),
                                      proj[:, bank, :].rearrange("p (g d) -> p g d", d=HD // 2),
                                      cc.broadcast_to([P, 2 * REP, HD // 2]), ALU.mult)
                    dve.tensor_tensor(t2[:, parity].rearrange("p (g u d) -> p g u d", u=2, d=HD // 2),
                                      halves[:, :, ::-1, :], ss.broadcast_to([P, REP, 2, HD // 2]),
                                      ALU.mult).then_inc(s["proj_free"], 1)

                def keep_v(parity, bank, n):
                    dve.wait_ge(s["proj_full"], n + 1)
                    dve.tensor_copy(v[:, parity, :, 0:HD], proj[:, bank, :].rearrange("p (g d) -> p g d", d=HD)
                                    ).then_inc(s["proj_free"], 1)

                def feature(item, parity, dst):
                    dve.wait_ge(s["exp_done"], item + 1)
                    dve.scalar_tensor_tensor(dst, y[:, parity], 0.0, ex[:, parity], ALU.max, ALU.add
                                             ).then_inc(s["feat_done"], 1)

                dve.wait_ge(s["silu_done"], 1)
                dve.tensor_copy(wide[:], scond[:].rearrange("p l k b -> p (l k b)").unsqueeze(2)
                                .broadcast_to([P, 2 * KD * B, P])).then_inc(s["wide_done"], 1)
                dve.wait_ge(s["x_in"], 16)
                for b in range(B):
                    norm(b * NC, b)
                dve.wait_ge(s["stat_done"], B)
                for b in range(B):
                    aggregate(b)
                dve_vectors(dve, SA, GA, 1)
                centre(0, 1, 0)
                centre(NC, 2, 1)
                self.split_chunk(dve, 0, 0)
                split(1, 0, 2 + 1)
                self.split_chunk(dve, 1, WCH)
                dve.wait_ge(s["tab_in"], 32)
                rope(0, 0, 0, 0, 0, first=True)
                self.split_chunk(dve, 2, 2 * WCH)
                keep_v(0, 1, 1)
                for r in range(1, RI):
                    if r + 2 < NW:
                        self.split_chunk(dve, r + 2, (r + 2) * WCH)
                    rope(r, r % 2, (r + 1) % 2, 0, r + 1, first=r < 2)
                    feature(r - 1, (r - 1) % 2, feat[:, 0, r - 1, :])
                feature(RI - 1, (RI - 1) % 2, feat[:, 0, RI - 1, :])
                dve_vectors(dve, GA, 6, 2)
                dve.memset(den[:], 0.0).then_inc(s["score_free"], 2)
                dve.wait_ge(s["y_done"], RI)
                dve_gates(dve)
                dve.memset(rden[:], 0.0).then_inc(s["num_free"], 1)
                dve.wait_ge(s["causal_made"], 1)
                dve.wait_ge(s["x_in"], 16 * (1 + B))

                def step(c, b, nxt, norm_on):
                    nb = 1 - b
                    nc_ = c + b

                    def masked(g):
                        dve.wait_ge(s["score_full"], at(c, b, KVH, g + 1))
                        dve.tensor_tensor(am[:, g % 2].rearrange("p (r t) -> p r t", r=REP),
                                          score[:, g % 2, :].rearrange("p (r t) -> p r t", r=REP),
                                          causal[:].unsqueeze(1).broadcast_to([P, REP, P]),
                                          ALU.mult).then_inc(s["score_free"], 1)

                    def normalise(g):
                        dve.wait_ge(s["num_full"], at(c, b, KVH + 1, g + 1))
                        pairs = num[:, :, 0:2 * VW].rearrange("p k (h w) -> p k h w", w=VW)
                        dve.tensor_scalar(den[:].rearrange("p (k h) -> p k h", k=2), pairs[:, :, :, HD], DEN_EPS, None,
                                          ALU.add).then_inc(s["den_done"], 1)
                        dve.wait_ge(s["den_done"], at(c, b, KVH, g + 1))
                        dve.reciprocal(rden[:], den[:]).then_inc(s["rden_done"], 1)
                        dve.wait_ge(s["rden_done"], at(c, b, KVH, g + 1))
                        dve.tensor_tensor(on[:, g % 2].rearrange("p (k h d) -> p k h d", k=2, h=2),
                                          pairs[:, :, :, 0:HD],
                                          rden[:].rearrange("p (k h) -> p k h", k=2).unsqueeze(3)
                                          .broadcast_to([P, 2, 2, HD]), ALU.mult).then_inc(s["num_free"], 1)

                    def q_rope(r):
                        if nxt:
                            rope(at(c, b, RI, RI + r), (b + 1 + r) % 2, (b + (r + 1 if r else 0)) % 2, nc_,
                                 proj_item(c, b, r + 1 if r else 0))

                    def f(r):
                        if nxt:
                            feature(at(c, b, RI, RI + r), (b + 1 + r) % 2, feat[:, nb, r, :])

                    if nxt:
                        split(at(c, b, 1, 2), nb, 2 + 1 + at(c, b, 10, 1))
                    if norm_on:
                        norm(bass.ds(c + (b * NC + 1), 1), b)
                        dve.wait_ge(s["stat_done"], at(c, b, 1, 3))
                    masked(0)
                    if norm_on:
                        aggregate(b)
                    q_rope(0)
                    normalise(0)
                    if last(c, b):
                        for i in range(2 * FI // WCH):
                            self.split_chunk(dve, NW + i, i * WCH)
                            if i == 0:
                                masked(1)
                            if i == 1:
                                normalise(1)
                            if i == 2:
                                masked(2)
                            if i == 3:
                                normalise(2)
                    else:
                        masked(1)
                    if nxt:
                        keep_v(nb, (b + 1) % 2, proj_item(c, b, 1))
                    f(0)
                    if not last(c, b):
                        normalise(1)
                    if norm_on:
                        centre(bass.ds(c + (b * NC + 1), 1), at(c, b, 1, 3), b)
                    if not last(c, b):
                        masked(2)
                        q_rope(1)
                        normalise(2)
                    masked(3)
                    q_rope(2)
                    f(1)
                    normalise(3)
                    q_rope(3)
                    f(2)
                    dve.wait_ge(s["num_full"], at(c, b, KVH + 1, KVH + 1))
                    dve.tensor_tensor(state[:, b].rearrange("p (k h) w -> p k (h w)", k=2),
                                      num[:, :, 0:2 * VW], state[:, b].rearrange("p (k h) w -> p k (h w)", k=2),
                                      ALU.add).then_inc(s["num_free"], 1)
                    q_rope(4)
                    f(3)
                    n = at(c, b, 7, 6) if last(c, b) else proj_item(c, b, 6)
                    dve.wait_ge(s["proj_full"], n + 1)
                    dve.tensor_tensor(dx[:], proj[:, b, 0:D],
                                      gate_b[:, 0, 0, b, :], ALU.mult).then_inc(s["proj_free"], 1)
                    dve.wait_ge(s["proj_free"], 2 + n + 1)
                    xt = x[:, bass.ds(c + b * NC, 1), :].rearrange("p o d -> p (o d)")
                    dve.tensor_tensor(xt, xt, dx[:], ALU.add).then_inc(s["x_done"], 1)
                    f(4)

                walk(dve, step)

            @block.tensor
            def _(pe):
                pe.wait_ge(s["silu_done"], 1)
                pe.wait_ge(s["wmod_in"], 16)
                pe_vectors(pe, SA, GA, True)
                pe.wait_ge(s["const_made"], 1)

                def norm_turn(n, parity, bank, norms):
                    pe.wait_ge(s["xn_done"], norms)
                    pe.wait_ge(s["turn_free"], n + 1)
                    for k in range(KD):
                        t = pe.transpose(turn[:, bank, k * P:(k + 1) * P], xn[:, parity, k * P:(k + 1) * P], ident[:])
                    t.then_inc(s["turn_full"], 1)

                def project(parity, j, bank, n):
                    pe.wait_ge(s["proj_free"], n + 1)
                    cols = slice(j * 512, (j + 1) * 512)
                    passes = [(h_hi, w_hi), (h_hi, w_lo), (h_lo, w_hi)]
                    for i, (hh, ww) in enumerate(passes):
                        for k in range(KD):
                            mm = pe.matmul(proj[:, bank, :], hh[:, parity, k, :], ww[:, k, cols],
                                           start=(i == 0 and k == 0), stop=(i == 2 and k == KD - 1))
                    mm.then_inc(s["proj_full"], 1)

                norm_turn(0, 0, 0, 1)
                norm_turn(1, 1, 1, 2)
                pe.wait_ge(s["hl_done"], 1)
                for j in range(RI + 1):
                    pe.wait_ge(self.w_ready, j + 1)
                    project(0, j, j % 2, j)
                pe.wait_ge(s["wmod_in"], 32)
                pe.wait_ge(s["wide_done"], 1)
                pe.wait_ge(msem["mod_kept"], 1)
                pe_vectors(pe, GA, 6, True)
                pe_gates(pe)
                pe.wait_ge(s["wo_in"], 16)

                def step(c, b, nxt, norm_on):
                    tp = 1 if last(c, b) else 0

                    def bank(j):
                        return (j + tp) % 2

                    def turn4(j, src):
                        n = turn_item(c, b, j)
                        pe.wait_ge(s["turn_free"], n + 1)
                        for r in range(4):
                            t = pe.transpose(turn[:, bank(j), r * P:(r + 1) * P], src[:, r * P:(r + 1) * P], ident[:])
                        t.then_inc(s["turn_full"], 1)

                    def q_turn(g):
                        pe.wait_ge(s["feat_done"], at(c, b, RI, 2 + g))
                        turn4(1 + g, feat[:, b, 1 + g, :])

                    def scores(g):
                        pe.wait_ge(s["turn_free"], 2 + 1 + turn_item(c, b, 1 + g))
                        pe.wait_ge(s["score_free"], at(c, b, KVH, g + 1))
                        pe.matmul(score[:, g % 2, :], k_t[:, g, :], q_t[:, g, :], start=True, stop=True
                                  ).then_inc(s["score_full"], 1)

                    def numerators(g):
                        pe.wait_ge(s["score_free"], 2 + at(c, b, KVH, g + 1))
                        pe.wait_ge(s["num_free"], at(c, b, KVH + 1, g + 1))
                        for r in range(REP):
                            dst = num[:, r // 2, (r % 2) * VW:(r % 2 + 1) * VW]
                            pe.matmul(dst, am[:, g % 2, r * P:(r + 1) * P], v[:, b, g, :], start=True, stop=False)
                            mm = pe.matmul(dst, q_t[:, g, r * P:(r + 1) * P], state[:, b, g, :], start=False, stop=True)
                        mm.then_inc(s["num_full"], 1)

                    def out_turn(g):
                        pe.wait_ge(s["num_free"], 1 + at(c, b, KVH + 1, g + 1))
                        turn4(5 + g, on[:, g % 2, :])

                    def p(j):
                        if nxt:
                            project(1 - b, j, (b + j) % 2, proj_item(c, b, j))

                    pe.wait_ge(s["feat_done"], at(c, b, RI, 1))
                    turn4(0, feat[:, b, 0, :])
                    q_turn(0)
                    q_turn(1)
                    scores(0)
                    q_turn(2)
                    if nxt:
                        pe.wait_ge(s["hl_done"], at(c, b, 1, 2))
                    p(0)
                    numerators(0)
                    scores(1)
                    q_turn(3)
                    p(1)
                    numerators(1)
                    out_turn(0)
                    scores(2)
                    p(2)
                    numerators(2)
                    out_turn(1)
                    scores(3)
                    p(3)
                    numerators(3)
                    out_turn(2)
                    p(4)
                    pe.wait_ge(s["num_free"], at(c, b, KVH + 1, KVH + 1))
                    for g in range(KVH):
                        mm = pe.matmul(num[:, g // 2, (g % 2) * VW:(g % 2 + 1) * VW], feat[:, b, 0, g * P:(g + 1) * P],
                                       v[:, b, g, :], start=True, stop=True)
                    mm.then_inc(s["num_full"], 1)
                    out_turn(3)
                    p(5)
                    if norm_on:
                        norm_turn(turn_item(c, b, 9), b, bank(9), at(c, b, 1, 3))
                    n = at(c, b, 7, 6) if last(c, b) else proj_item(c, b, 6)
                    pe.wait_ge(s["proj_free"], n + 1)
                    pe.wait_ge(s["turn_free"], 2 + 1 + turn_item(c, b, 8))
                    for i in range(H):
                        mm = pe.matmul(proj[:, b, 0:D], o_t[:, i, :], wo[:, i, :],
                                       start=(i == 0), stop=(i == H - 1))
                    mm.then_inc(s["proj_full"], 1)

                walk(pe, step)

    def ffn_phase(self):
        nc, a = self.nc, self.a
        x, ident, mod_t, gate_b, half, eps = self.x, self.ident, self.mod_t, self.gate_b, self.half, self.eps
        TOK = GT * P
        NQ = NM // 4
        self.small_in = self.sem("scan_small_in")
        self.scan_small = [self.keep.enter_context(nc.sbuf_tensor(n, shape, F32)) for n, shape in (
            ("t_cos", [P, NC, TD // 2]), ("t_sin", [P, NC, TD]), ("t_wo", [P, KD, D]), ("ln_gamma", [P, KD]),
            ("ln_beta", [P, KD]))]
        with ExitStack() as ctx:
            def sb(name, shape, dt=F32):
                return ctx.enter_context(nc.sbuf_tensor(name, shape, dt))

            def ps(name, shape, dt=F32):
                return ctx.enter_context(nc.psum_tensor(name, shape, dt))

            w_hi, w_lo = self.w_hi, self.w_lo
            wmod = sb("f_wmod", [P, KD, 6 * D])
            wd = sb("wd_sb", [P, NM, D])
            stats, mv = sb("f_stats", [P, GT, 6]), sb("f_mv", [P, GT, 2])
            veps, rstd = sb("f_veps", [P, GT]), sb("f_rstd", [P, GT])
            xn = sb("f_xn", [P, GT, D])
            h = sb("f_h", [P, KD, TOK])
            h_hi, h_lo = sb("f_h_hi", [P, 2, KD, TOK], F32R), sb("f_h_lo", [P, 2, KD, TOK], F32R)
            sg = sb("silu_gate", [P, 2, TOK])
            hid = sb("hidden", [P, 2, NM, TOK])
            mag = sb("magnitude", [P, NM, TOK])
            beats = sb("beats", [P, 6, TOK], BF16)
            wins = sb("wins", [P, 4, TOK], BF16)
            part = sb("wins_part", [P, 4, TOK], BF16)
            dx = sb("f_dx", [P, 2, D])
            turn = ps("f_turn", [P, 2, 512])
            gate, up = ps("gate_ps2", [P, 2, 512]), ps("up_ps", [P, 2, 512])
            rows = ps("f_rows", [P, 2, 512])

            names = ("wd_in wmod_in stat_done aggr_done veps_done rstd_done xn_done h_done hi_done hl_done "
                     "turn_full gate_full up_full silu_done hid_done mag_done pick_step pick_done rows_full dx_done x_done")
            s = {n: self.sem("f_" + n) for n in names.split()}
            msem = self.modulation_sems(1)
            scratch = hid[:].rearrange("p i m t -> p (i m t)")
            pe_vectors, pe_gates, dve_vectors, dve_gates = self.modulation(
                1, wmod, self.scond, self.wide, msem, turn[:, 0, :],
                [up[:, i // 2, i % 2 * D:(i % 2 + 1) * D] for i in range(2 * B)],
                scratch[:, 0:2 * B * D].rearrange("p (i d) -> p i d", d=D),
                scratch[:, 2 * B * D:4 * B * D].rearrange("p (i d) -> p i d", d=D))
            WKV = self.wkv_col = 2 * FI
            NCH = QKV // WCH + 2 * FI // WCH
            self.chunks = NCH + 1
            block = ctx.enter_context(nc.Block())

            @block.sync
            def _(sp):
                sp.dma_start(wd[:], a["wd"].rearrange("(m p) n -> p m n", p=P)).then_inc(s["wd_in"], 16)
                sp.dma_start(wmod[:], a["wmod"][1].rearrange("(k p) n -> p k n", p=P)).then_inc(s["wmod_in"], 16)
                self.load_chunk(sp, NCH, a["wkv1"])
                for i in range(2):
                    self.load_chunk(sp, NCH + 1 + i, a["w1"][:, i * WCH:(i + 1) * WCH])
                cos, sin, wo, ln_g, ln_b = self.scan_small
                sp.dma_start(cos[:], a["cos1"].rearrange("(c p) d -> p c d", p=P)).then_inc(self.small_in, 16)
                sp.dma_start(sin[:], a["sin1"].rearrange("(c p) d -> p c d", p=P)).then_inc(self.small_in, 16)
                sp.dma_start(wo[:], a["wo1"].rearrange("(k p) n -> p k n", p=P)).then_inc(self.small_in, 16)
                with nc.allow_non_contiguous_dma(reason="two vectors of 256"):
                    sp.dma_start(ln_g[:], a["ln_g"].rearrange("(k p) -> p k", p=P)).then_inc(self.small_in, 16)
                    sp.dma_start(ln_b[:], a["ln_b"].rearrange("(k p) -> p k", p=P)).then_inc(self.small_in, 16)

            @block.gpsimd
            def _(pool):
                def rstd_of(g):
                    pool.wait_ge(s["aggr_done"], GT * (g + 1))
                    pool.tensor_tensor(veps[:], mv[:, :, 1], eps[:].broadcast_to([P, GT]), ALU.add).then_inc(s["veps_done"], 1)
                    pool.wait_ge(s["veps_done"], g + 1)
                    pool.tensor_tensor(rstd[:], veps[:], half[:].broadcast_to([P, GT]), ALU.pow).then_inc(s["rstd_done"], 1)

                def add_rows(g):
                    for i in range(GT):
                        n = g * GT + i
                        pool.wait_ge(s["dx_done"], n + 1)
                        pool.tensor_tensor(x[:, n, :], x[:, n, :], dx[:, n % 2], ALU.add).then_inc(s["x_done"], 1)

                rstd_of(0)
                for g in range(NG):
                    if g + 1 < NG:
                        rstd_of(g + 1)
                    if g:
                        add_rows(g - 1)
                add_rows(NG - 1)

            @block.scalar
            def _(act):
                def drain_norm(g):
                    b = g * GT // NC
                    for k in range(KD):
                        act.wait_ge(s["turn_full"], KD * g + k + 1)
                        if g:
                            act.wait_ge(s["hl_done"], g)
                        act.activation(h[:, k, :], turn[:, k, :], ACT.Identity,
                                       bias=mod_t[:, 0, SB_ * KD + k, b:b + 1],
                                       scale=mod_t[:, 0, CB * KD + k, b:b + 1]).then_inc(s["h_done"], 1)

                def magnitude(g, m):
                    n = g * NM + m
                    act.wait_ge(s["hid_done"], n + 1)
                    if g:
                        act.wait_ge(s["pick_done"], NQ * (g - 1) + m // 4 + 1)
                    act.activation(mag[:, m], hid[:, g % 2, m], ACT.Abs).then_inc(s["mag_done"], 1)

                drain_norm(0)
                for g in range(NG):
                    for m in range(NM):
                        n = g * NM + m
                        act.wait_ge(s["gate_full"], n + 1)
                        if n >= 2:
                            act.wait_ge(s["hid_done"], n - 1)
                        act.activation(sg[:, n % 2], gate[:, n % 2, :], ACT.Silu).then_inc(s["silu_done"], 1)
                        if n:
                            magnitude((n - 1) // NM, (n - 1) % NM)
                        if m == 5 and g + 1 < NG:
                            drain_norm(g + 1)
                magnitude(NG - 1, NM - 1)

            @block.vector
            def _(dve):
                def norms(g):
                    for i in range(GT):
                        dve.bn_stats(stats[:, i, :], x[:, g * GT + i, :]).then_inc(s["stat_done"], 1)
                    for i in range(GT):
                        dve.wait_ge(s["stat_done"], g * GT + i + 1)
                        dve.bn_aggr(mv[:, i, :], stats[:, i, :]).then_inc(s["aggr_done"], 1)

                def centre(g):
                    dve.wait_ge(s["rstd_done"], g + 1)
                    if g:
                        dve.wait_ge(s["turn_full"], KD * g)
                    for i in range(GT):
                        dve.tensor_scalar(xn[:, i, :], x[:, g * GT + i, :], mv[:, i, 0:1], rstd[:, i:i + 1],
                                          ALU.subtract, ALU.mult).then_inc(s["xn_done"], 1)

                def split(g):
                    dve.wait_ge(s["h_done"], KD * (g + 1))
                    dve.tensor_copy(h_hi[:, g % 2], h[:]).then_inc(s["hi_done"], 1)
                    dve.wait_ge(s["hi_done"], g + 1)
                    dve.tensor_tensor(h_lo[:, g % 2], h[:], h_hi[:, g % 2].bitcast(F32), ALU.subtract
                                      ).then_inc(s["hl_done"], 1)

                steps = [0]

                def pick(g, q):
                    m0 = 4 * q
                    pairs = [(0, 1), (0, 2), (0, 3), (1, 2), (1, 3), (2, 3)]
                    c = {pr: beats[:, i] for i, pr in enumerate(pairs)}

                    def op(f, need=0):
                        def go():
                            if need:
                                dve.wait_ge(s["pick_step"], base + need)
                            f().then_inc(s["pick_step"], 1)
                        return go

                    base = (g * NQ + q) * 14
                    ops = []
                    for i, (u, w) in enumerate(pairs):
                        def duel(i=i, u=u, w=w):
                            dve.wait_ge(s["mag_done"], g * NM + m0 + 4)
                            return dve.tensor_tensor(beats[:, i], mag[:, m0 + u], mag[:, m0 + w], ALU.is_ge)
                        ops.append(op(duel))
                    sums = [(0, c[0, 1], c[0, 2], ALU.add), (1, c[1, 2], c[0, 1], ALU.subtract),
                            (2, c[2, 3], c[0, 2], ALU.subtract), (3, c[0, 3], c[1, 3], ALU.add)]
                    for i, u, w, o in sums:
                        ops.append(op(lambda i=i, u=u, w=w, o=o: dve.tensor_tensor(part[:, i], u, w, o), 6))
                    ends = [(0, c[0, 3], ALU.add), (1, c[1, 3], ALU.add), (2, c[1, 2], ALU.subtract), (3, c[2, 3], ALU.add)]
                    for i, w, o in ends:
                        ops.append(op(lambda i=i, w=w, o=o: dve.tensor_tensor(wins[:, i], part[:, i], w, o), 7 + i))
                    tests = [(0, 2.0, ALU.is_ge), (1, 1.0, ALU.is_ge), (2, 0.0, ALU.is_ge), (3, 1.0, ALU.is_le)]
                    for i, bound, o in tests:
                        def keep(i=i, bound=bound, o=o):
                            dve.wait_ge(s["pick_step"], base + 11 + i)
                            t = hid[:, g % 2, m0 + i]
                            ins = dve.scalar_tensor_tensor(t, wins[:, i], bound, t, o, ALU.mult)
                            if i == 3:
                                ins.then_inc(s["pick_done"], 1)
                        ops.append(keep)
                    return ops

                def out_rows(g, i):
                    b = g * GT // NC
                    n = g * GT + i
                    dve.wait_ge(s["rows_full"], n + 1)
                    if n >= 2:
                        dve.wait_ge(s["x_done"], n - 1)
                    dve.tensor_tensor(dx[:, n % 2], rows[:, n % 2, 0:D], gate_b[:, 0, 1, b, :], ALU.mult
                                      ).then_inc(s["dx_done"], 1)

                norms(0)
                centre(0)
                split(0)
                self.split_chunk(dve, NCH, WKV)
                ops = []
                for g in range(NG):
                    for m in range(NM):
                        n = g * NM + m
                        dve.wait_ge(s["up_full"], n + 1)
                        dve.wait_ge(s["silu_done"], n + 1)
                        if g >= 2 and m == 0:
                            dve.wait_ge(s["rows_full"], GT * (g - 1))
                        dve.tensor_tensor(hid[:, g % 2, m], up[:, n % 2, :], sg[:, n % 2], ALU.mult
                                          ).then_inc(s["hid_done"], 1)
                        if m % 4 == 0 and n:
                            ops = pick((n - 4) // NM, (n - 4) % NM // 4)
                        for o in ops[:5]:
                            o()
                        ops = ops[5:]
                        if g + 1 < NG:
                            if m == 1:
                                norms(g + 1)
                            if m == 3:
                                centre(g + 1)
                            if m == 6:
                                split(g + 1)
                        if m >= NM - GT and g:
                            out_rows(g - 1, m - (NM - GT))
                dve_vectors(dve, 0, 6, 1)
                for o in pick(NG - 1, NQ - 1):
                    o()
                for i in range(GT):
                    out_rows(NG - 1, i)
                dve_gates(dve)

            @block.tensor
            def _(pe):
                def norm_turn(g):
                    pe.wait_ge(s["xn_done"], GT * (g + 1))
                    for k in range(KD):
                        if g:
                            pe.wait_ge(s["h_done"], KD * (g - 1) + k + 1)
                        for i in range(GT):
                            t = pe.transpose(turn[:, k, i * P:(i + 1) * P], xn[:, i, k * P:(k + 1) * P], ident[:])
                        t.then_inc(s["turn_full"], 1)

                def hidden(g, m):
                    n = g * NM + m
                    for dst, off, full, used in ((gate, 0, "gate_full", "silu_done"), (up, FI, "up_full", "hid_done")):
                        if n >= 2:
                            pe.wait_ge(s[used], n - 1)
                        cols = slice(off + m * P, off + (m + 1) * P)
                        for i, (ww, hh) in enumerate([(w_hi, h_hi), (w_lo, h_hi), (w_hi, h_lo)]):
                            for k in range(KD):
                                mm = pe.matmul(dst[:, n % 2, :], ww[:, k, cols], hh[:, g % 2, k, :],
                                               start=(i == 0 and k == 0), stop=(i == 2 and k == KD - 1))
                        mm.then_inc(s[full], 1)

                def down(g, i):
                    pe.wait_ge(s["pick_done"], NQ * (g + 1))
                    n = g * GT + i
                    if n >= 2:
                        pe.wait_ge(s["dx_done"], n - 1)
                    for m in range(NM):
                        mm = pe.matmul(rows[:, n % 2, 0:D], hid[:, g % 2, m, i * P:(i + 1) * P], wd[:, m, :],
                                       start=(m == 0), stop=(m == NM - 1))
                    mm.then_inc(s["rows_full"], 1)

                norm_turn(0)
                for g in range(NG):
                    pe.wait_ge(s["hl_done"], g + 1)
                    for m in range(NM):
                        hidden(g, m)
                        if m == 4 and g + 1 < NG:
                            norm_turn(g + 1)
                        if m >= NM - GT and g:
                            pe.wait_ge(s["wd_in"], 16)
                            down(g - 1, m - (NM - GT))
                pe.wait_ge(s["wmod_in"], 16)
                pe.wait_ge(s["h_done"], KD * NG)
                pe_vectors(pe, 0, 6, True)
                pe.wait_ge(s["hid_done"], NG * NM)
                pe_gates(pe)
                for i in range(GT):
                    down(NG - 1, i)

    def scan_phase(self):
        nc, a = self.nc, self.a
        x, ident, mod_t, gate_b, half, eps = self.x, self.ident, self.mod_t, self.gate_b, self.half, self.eps
        NH = E + 2
        self.moe_in = self.sem("moe_in")
        self.moe_small = [self.keep.enter_context(nc.sbuf_tensor(n, shape, F32)) for n, shape in (
            ("w2_sb", [P, NH, D]), ("b1_sb", [P, NH]), ("b2_sb", [E + 1, D]), ("gate_w_sb", [P, KD, E]))]
        with ExitStack() as ctx:
            def sb(name, shape, dt=F32):
                return ctx.enter_context(nc.sbuf_tensor(name, shape, dt))

            def ps(name, shape, dt=F32):
                return ctx.enter_context(nc.psum_tensor(name, shape, dt))

            w_cols = slice(self.wkv_col, self.wkv_col + 2 * D)
            w_hi, w_lo = self.w_hi[:, :, w_cols], self.w_lo[:, :, w_cols]
            cos, sin, wo, ln_g, ln_b = self.scan_small
            NCH = self.chunks
            blocks, ident_n = sb("head_blocks", [P, P]), sb("ident_n", [P, P])
            rows_of = sb("rows_of", [P, NMB])
            stats, mv = sb("t_stats", [P, 2, 2, 6]), sb("t_mv", [P, 2, 2, 2])
            veps, rstd = sb("t_veps", [P, 2, 2]), sb("t_rstd", [P, 2, 2])
            xn, zn = sb("t_xn", [P, B, D]), sb("t_zn", [P, B, D])
            h = sb("t_h", [P, B, KD, P])
            h_hi, h_lo = sb("t_h_hi", [P, B, KD, P], F32R), sb("t_h_lo", [P, B, KD, P], F32R)
            t1, t2 = sb("t_rope_cos", [P, B, D]), sb("t_rope_sin", [P, B, D])
            kr, v = sb("t_k", [P, B, D]), sb("t_v", [P, B, D])
            STEP = P + MB
            k_diag = sb("k_diag", [P, B, KD, NMB * STEP])
            k_rows = sb("k_rows", [P, B, NMB, D])
            u = sb("t_u", [P, B, D])
            w = sb("t_w", [P, B, KD, P])
            zs = sb("t_z", [P, B, D])
            o_t = sb("t_o", [P, B, KD, P])
            dx = sb("t_dx", [P, B, D])
            z_ps, g_ps = ps("z_ps", [P, B, 512]), ps("g_ps", [P, B, 512])
            proj, turn = ps("t_proj", [P, B, 512]), ps("t_turn", [P, B, 512])

            def sems(name):
                return self.sem("t_" + name)

            def nth(b, n):
                return n * B + (b + 1 - B)

            const_step = self.sem("t_const_step")
            zeroed, blocks_made = self.sem("t_zeroed"), self.sem("t_blocks_made")
            z_full, u_done, g_full, w_done = sems("z_full"), sems("u_done"), sems("g_full"), sems("w_done")
            z_kept, v_kept, k_diag_done, k_rows_done = sems("z_kept"), sems("v_kept"), sems("kdiag"), sems("krows")
            x_stat, x_aggr, x_rstd, xn_done = sems("x_stat"), sems("x_aggr"), sems("x_rstd"), sems("xn_done")
            z_stat, z_aggr, z_rstd, zn_done = sems("z_stat"), sems("z_aggr"), sems("z_rstd"), sems("zn_done")
            xv_done, zv_done = sems("x_veps"), sems("z_veps")
            xn_turned, zn_turned, k_turned = sems("xn_turned"), sems("zn_turned"), sems("k_turned")
            h_done, hi_done, hl_done, o_done = sems("h_done"), sems("hi_done"), sems("hl_done"), sems("o_done")
            proj_full, rope_done, kr_done = sems("proj_full"), sems("rope_done"), sems("kr_done")
            rows_full, dx_done, x_done = sems("rows_full"), sems("dx_done"), sems("x_done")
            block = ctx.enter_context(nc.Block())

            def tile(c, b):
                return bass.ds(c + b * NC, 1)

            def flat(ap):
                return ap.rearrange("p o d -> p (o d)")

            def walk(engine, step):
                step(0, False, True, True)
                with nc.Fori(1, NC - 2, engines=(engine.engine,), hint_back_edge=True) as c:
                    step(c, True, True, True)
                step(NC - 2, True, True, False)
                step(NC - 1, True, False, False)

            @block.sync
            def _(sp):
                w2, b1, b2, gw = self.moe_small
                sp.dma_start(gw[:], a["gw"].rearrange("(k p) n -> p k n", p=P)).then_inc(self.moe_in, 16)
                sp.dma_start(b1[:], a["b1"]).then_inc(self.moe_in, 16)
                sp.dma_start(b2[:], a["b2"]).then_inc(self.moe_in, 16)
                sp.dma_start(w2[:], a["w2"].rearrange("(m p) n -> p m n", p=P)).then_inc(self.moe_in, 16)
                self.load_chunk(sp, NCH + 2, a["w1"][:, 2 * WCH:NH * P], NH * P - 2 * WCH)

            @block.gpsimd
            def _(pool):
                pool.memset(blocks[:], INV_N).then_inc(const_step, 1)
                pool.memset(rows_of[:], 1.0).then_inc(const_step, 1)
                pool.wait_ge(const_step, 2)
                n = 2
                for base, sign in ((0, 1), (MB - 1, -1)):
                    for dst, pattern in ((blocks[:].rearrange("p (h e) -> p h e", e=TD), [[-sign * TD, P // TD], [0, TD]]),
                                         (rows_of[:], [[-sign * MB, NMB]])):
                        pool.affine_select(out=dst, in_=dst, compare_op=ALU.is_ge, fill=0.0, base=base,
                                           pattern=pattern, channel_multiplier=sign).then_inc(const_step, 1)
                    n += 2
                    pool.wait_ge(const_step, n)
                pool.memset(veps[:], 0.0).then_inc(blocks_made, 1)

                def rstd_of(i, b, n, aggr, stepped, done):
                    pool.wait_ge(aggr, nth(b, n))
                    pool.tensor_tensor(veps[:, i, b:b + 1], mv[:, i, b, 1:2], eps[:], ALU.add).then_inc(stepped, 1)
                    pool.wait_ge(stepped, nth(b, n))
                    pool.tensor_tensor(rstd[:, i, b:b + 1], veps[:, i, b:b + 1], half[:], ALU.pow).then_inc(done, 1)

                def add_rope(b, n):
                    pool.wait_ge(rope_done, nth(b, n))
                    pool.tensor_tensor(kr[:, b], t1[:, b], t2[:, b], ALU.add).then_inc(kr_done, 1)

                def add_rows(c, b, n):
                    pool.wait_ge(dx_done, nth(b, n))
                    xt = flat(x[:, tile(c, b), :])
                    pool.tensor_tensor(xt, xt, dx[:, b], ALU.add).then_inc(x_done, 1)

                pool.wait_ge(blocks_made, 1)
                for n in (1, 2):
                    for b in range(B):
                        rstd_of(0, b, n, x_aggr, xv_done, x_rstd)
                for b in range(B):
                    add_rope(b, 1)

                def step(c, prev, nxt, ahead):
                    if prev:
                        for b in range(B):
                            rstd_of(1, b, c, z_aggr, zv_done, z_rstd)
                    if nxt:
                        pool.wait_ge(k_rows_done, nth(0, (c + 1) * NMB))
                        add_rope(0, c + 2)
                    if ahead:
                        for b in range(B):
                            rstd_of(0, b, c + 3, x_aggr, xv_done, x_rstd)
                    if nxt:
                        pool.wait_ge(k_rows_done, nth(1, (c + 1) * NMB))
                        add_rope(1, c + 2)
                    if prev:
                        for b in range(B):
                            add_rows(c - 1, b, c)

                walk(pool, step)
                for b in range(B):
                    rstd_of(1, b, NC, z_aggr, zv_done, z_rstd)
                for b in range(B):
                    add_rows(NC - 1, b, NC)

            @block.scalar
            def _(act):
                def spread(c, b, j, waited=True):
                    if waited:
                        act.wait_ge(g_full, nth(b, c * NMB + (j - NMB + 2)))
                    act.activation(k_rows[:, b, j], kr[:, b], ACT.Copy, scale=rows_of[:, j:j + 1]
                                   ).then_inc(k_rows_done, 1)

                def drain_norm(b, n):
                    act.wait_ge(xn_turned, nth(b, n))
                    for k in range(KD):
                        i = act.activation(h[:, b, k], turn[:, b, k * P:(k + 1) * P], ACT.Identity,
                                           bias=mod_t[:, 1, SA * KD + k, b:b + 1], scale=mod_t[:, 1, CA * KD + k, b:b + 1])
                    i.then_inc(h_done, 1)

                def drain_out(b, n):
                    act.wait_ge(zn_turned, nth(b, n))
                    for k in range(KD):
                        i = act.activation(o_t[:, b, k], turn[:, b, k * P:(k + 1) * P], ACT.Identity,
                                           bias=ln_b[:, k:k + 1], scale=ln_g[:, k:k + 1])
                    i.then_inc(o_done, 1)

                def keep_v(b, n):
                    act.wait_ge(rope_done, nth(b, n))
                    act.activation(v[:, b], proj[:, b, D:2 * D], ACT.Copy).then_inc(v_kept, 1)

                def spread_blocks(b, n, waited=True):
                    act.wait_ge(k_turned, nth(b, n))
                    if waited:
                        act.wait_ge(z_full, nth(b, (n - 1) * NMB))
                    act.activation(k_diag[:, b].rearrange("p k (m s) -> p k m s", s=STEP)[:, :, :, 0:MB],
                                   turn[:, b, 0:D].rearrange("p (k m s) -> p k m s", k=KD, s=MB),
                                   ACT.Copy).then_inc(k_diag_done, 1)

                act.wait_ge(self.small_in, 16 * 5)
                for b in range(B):
                    drain_norm(b, 1)
                act.wait_ge(zeroed, 1)
                act.wait_ge(blocks_made, 1)
                for b in range(B):
                    keep_v(b, 1)
                    spread_blocks(b, 1, waited=False)
                for j in range(2):
                    for b in range(B):
                        act.wait_ge(kr_done, nth(b, 1))
                        spread(0, b, j, waited=False)

                def step(c, prev, nxt, ahead):
                    for j in (2, 3):
                        for b in range(B):
                            spread(c, b, j, waited=prev)
                    if nxt:
                        for b in range(B):
                            drain_norm(b, c + 2)
                    for j in range(4, NMB):
                        for b in range(B):
                            spread(c, b, j, waited=prev)
                    if prev:
                        for b in range(B):
                            drain_out(b, c)
                    if nxt:
                        for j in range(2):
                            for b in range(B):
                                act.wait_ge(kr_done, nth(b, c + 2))
                                spread(c + 1, b, j)
                        for b in range(B):
                            spread_blocks(b, c + 2)
                    for b in range(B):
                        act.wait_ge(u_done, nth(b, (c + 1) * NMB))
                        if prev:
                            act.wait_ge(zn_done, nth(b, c))
                        act.activation(zs[:, b], z_ps[:, b, 0:D], ACT.Copy).then_inc(z_kept, 1)
                        if nxt:
                            keep_v(b, c + 2)

                walk(act, step)
                for b in range(B):
                    drain_out(b, NC)

            @block.vector
            def _(dve):
                def x_norm(c, b):
                    dve.bn_stats(stats[:, 0, b, :], flat(x[:, tile(c, b), :])).then_inc(x_stat, 1)

                def x_aggregate(b):
                    dve.bn_aggr(mv[:, 0, b, :], stats[:, 0, b, :]).then_inc(x_aggr, 1)

                def x_centre(c, b, n):
                    dve.wait_ge(x_rstd, nth(b, n))
                    dve.tensor_scalar(xn[:, b], flat(x[:, tile(c, b), :]), mv[:, 0, b, 0:1], rstd[:, 0, b:b + 1],
                                      ALU.subtract, ALU.mult).then_inc(xn_done, 1)

                def z_norm(b, n):
                    dve.wait_ge(z_kept, nth(b, n))
                    dve.bn_stats(stats[:, 1, b, :], zs[:, b]).then_inc(z_stat, 1)

                def z_aggregate(b):
                    dve.bn_aggr(mv[:, 1, b, :], stats[:, 1, b, :]).then_inc(z_aggr, 1)

                def z_centre(b, n):
                    dve.wait_ge(z_rstd, nth(b, n))
                    dve.tensor_scalar(zn[:, b], zs[:, b], mv[:, 1, b, 0:1], rstd[:, 1, b:b + 1],
                                      ALU.subtract, ALU.mult).then_inc(zn_done, 1)

                def out_rows(b, n):
                    dve.wait_ge(rows_full, nth(b, n))
                    dve.tensor_tensor(dx[:, b], turn[:, b, D:2 * D], gate_b[:, 1, 0, b, :], ALU.mult).then_inc(dx_done, 1)

                def split(b, n):
                    dve.wait_ge(h_done, nth(b, n))
                    dve.tensor_copy(h_hi[:, b], h[:, b]).then_inc(hi_done, 1)
                    dve.wait_ge(hi_done, nth(b, n))
                    dve.tensor_tensor(h_lo[:, b], h[:, b], h_hi[:, b].bitcast(F32), ALU.subtract).then_inc(hl_done, 1)

                def rope(c, b, n, waited=True):
                    dve.wait_ge(proj_full, nth(b, n))
                    if waited:
                        dve.wait_ge(kr_done, nth(b, n - 1))
                    hd = TD // 2
                    k = proj[:, b, 0:D]
                    cc = flat(cos[:, bass.ds(c, 1), :]).unsqueeze(1).broadcast_to([P, 2 * TH, hd])
                    ss = sin[:, bass.ds(c, 1), :].rearrange("p o (u d) -> p (o u) d", u=2).unsqueeze(1)
                    dve.tensor_tensor(t1[:, b].rearrange("p (g d) -> p g d", d=hd),
                                      k.rearrange("p (g d) -> p g d", d=hd), cc, ALU.mult)
                    dve.tensor_tensor(t2[:, b].rearrange("p (g u d) -> p g u d", u=2, d=hd),
                                      k.rearrange("p (g u d) -> p g u d", u=2, d=hd)[:, :, ::-1, :],
                                      ss.broadcast_to([P, TH, 2, hd]), ALU.mult).then_inc(rope_done, 1)

                def new_w(b, n):
                    dve.wait_ge(g_full, nth(b, n))
                    dve.tensor_tensor(w[:, b], g_ps[:, b, 0:D].rearrange("p (k e) -> p k e", k=KD),
                                      blocks[:].unsqueeze(1).broadcast_to([P, KD, P]), ALU.mult).then_inc(w_done, 1)

                for b in range(B):
                    x_norm(0, b)
                dve.wait_ge(x_stat, nth(1, 1))
                for b in range(B):
                    x_aggregate(b)
                dve.memset(k_diag[:], 0.0).then_inc(zeroed, 1)
                dve.tensor_scalar(ident_n[:], ident[:], 1.0 / INV_N, None, ALU.mult).then_inc(zeroed, 1)
                for b in range(B):
                    x_centre(0, b, 1)
                for b in range(B):
                    x_norm(1, b)
                dve.wait_ge(x_stat, nth(1, 2))
                for b in range(B):
                    x_aggregate(b)
                for b in range(B):
                    split(b, 1)
                for b in range(B):
                    x_centre(1, b, 2)
                dve.wait_ge(self.small_in, 16 * 5)
                for b in range(B):
                    rope(0, b, 1, waited=False)
                dve.wait_ge(blocks_made, 1)
                for b in range(B):
                    new_w(b, 1)

                def step(c, prev, nxt, ahead):
                    for n in range(NMB):
                        for b in range(B):
                            dve.wait_ge(z_full, nth(b, c * NMB + (n + 1)))
                            if n == 0:
                                dve.wait_ge(v_kept, nth(b, c + 1))
                            if n == 1 and b == 0 and prev:
                                dve.wait_ge(z_stat, nth(1, c))
                            if n == 4 and b == 0 and ahead:
                                dve.wait_ge(x_stat, nth(1, c + 3))
                            dve.tensor_tensor(u[:, b], v[:, b], z_ps[:, b, 0:D], ALU.subtract).then_inc(u_done, 1)
                        if n == 1 and prev:
                            for b in range(B):
                                z_aggregate(b)
                        if n == 4 and ahead:
                            for b in range(B):
                                x_aggregate(b)
                        for b in range(B):
                            new_w(b, c * NMB + (n + 2))
                        if n == 0 and prev:
                            for b in range(B):
                                z_norm(b, c)
                        if n == 1 and nxt:
                            for b in range(B):
                                split(b, c + 2)
                        if n == 2 and prev:
                            for b in range(B):
                                z_centre(b, c)
                        if n == 3 and nxt:
                            rope(c + 1, 0, c + 2)
                        if n == 3 and ahead:
                            for b in range(B):
                                x_norm(c + 2, b)
                        if n == 5 and nxt:
                            rope(c + 1, 1, c + 2)
                        if n == 5 and prev:
                            out_rows(0, c)
                        if n == 5 and ahead:
                            for b in range(B):
                                x_centre(c + 2, b, c + 3)
                        if n == 6 and prev:
                            out_rows(1, c)
                        if not nxt and 3 <= n <= 5:
                            i = n - 3
                            self.split_chunk(dve, NCH + i, i * WCH, min(WCH, NH * P - i * WCH))

                walk(dve, step)
                for b in range(B):
                    z_norm(b, NC)
                dve.wait_ge(z_stat, nth(1, NC))
                for b in range(B):
                    z_aggregate(b)
                for b in range(B):
                    z_centre(b, NC)
                for b in range(B):
                    out_rows(b, NC)

            @block.tensor
            def _(pe):
                def norm_turn(b, n):
                    pe.wait_ge(xn_done, nth(b, n))
                    for k in range(KD):
                        t = pe.transpose(turn[:, b, k * P:(k + 1) * P], xn[:, b, k * P:(k + 1) * P], ident[:])
                    t.then_inc(xn_turned, 1)

                def out_turn(b, n):
                    pe.wait_ge(zn_done, nth(b, n))
                    for k in range(KD):
                        t = pe.transpose(turn[:, b, k * P:(k + 1) * P], zn[:, b, k * P:(k + 1) * P], ident[:])
                    t.then_inc(zn_turned, 1)

                def k_turn(b, n):
                    pe.wait_ge(kr_done, nth(b, n))
                    for k in range(KD):
                        t = pe.transpose(turn[:, b, k * P:(k + 1) * P], kr[:, b, k * P:(k + 1) * P], ident[:])
                    t.then_inc(k_turned, 1)

                def project(b, n, i):
                    hh, ww = [(h_hi, w_hi), (h_hi, w_lo), (h_lo, w_hi)][i]
                    if i == 0:
                        pe.wait_ge(hl_done, nth(b, n))
                    for k in range(KD):
                        mm = pe.matmul(proj[:, b, :], hh[:, b, k], ww[:, k, :],
                                       start=(i == 0 and k == 0), stop=(i == 2 and k == KD - 1))
                    if i == 2:
                        mm.then_inc(proj_full, 1)

                def out_rows(b, n):
                    pe.wait_ge(o_done, nth(b, n))
                    for k in range(KD):
                        mm = pe.matmul(turn[:, b, D:2 * D], o_t[:, b, k], wo[:, k, :], start=(k == 0), stop=(k == KD - 1))
                    mm.then_inc(rows_full, 1)

                pe.wait_ge(zeroed, 2)
                for b in range(B):
                    for k in range(KD):
                        mm = pe.matmul(g_ps[:, b, k * P:(k + 1) * P], ident[:], ident_n[:], start=(k == 0), stop=False,
                                       skip_group_check=True)
                    mm.then_inc(g_full, 1)
                for b in range(B):
                    norm_turn(b, 1)
                for b in range(B):
                    for i in range(3):
                        project(b, 1, i)
                for b in range(B):
                    k_turn(b, 1)
                pe.wait_ge(self.small_in, 16 * 5)

                def step(c, prev, nxt, ahead):
                    def filler(n, end):
                        slot = 2 * n + end
                        if nxt:
                            if slot < 2:
                                norm_turn(slot, c + 2)
                            for b in range(B):
                                first = (2 * 2, 2 * 4)[b]
                                if first <= slot < first + 3:
                                    if slot == first:
                                        pe.wait_ge(v_kept, nth(b, c + 1))
                                    project(b, c + 2, slot - first)
                        if prev:
                            if slot == 7:
                                for b in range(B):
                                    if nxt:
                                        pe.wait_ge(h_done, nth(b, c + 2))
                                    out_turn(b, c)
                            if 11 <= slot < 13:
                                out_rows(slot - 11, c)
                        if nxt and 13 <= slot < 15:
                            if prev:
                                pe.wait_ge(dx_done, nth(slot - 13, c))
                            k_turn(slot - 13, c + 2)

                    for n in range(NMB):
                        for b in range(B):
                            pe.wait_ge(w_done, nth(b, c * NMB + (n + 1)))
                            if n == 0:
                                pe.wait_ge(k_diag_done, nth(b, c + 1))
                                if prev:
                                    pe.wait_ge(z_kept, nth(b, c))
                            for k in range(KD):
                                mm = pe.matmul(z_ps[:, b, k * P:(k + 1) * P], k_diag[:, b, k, n * P:(n + 1) * P],
                                               w[:, b, k], start=(n == 0 and k == 0), stop=(n == NMB - 1),
                                               skip_group_check=True)
                            mm.then_inc(z_full, 1)
                        filler(n, 0)
                        for b in range(B):
                            pe.wait_ge(u_done, nth(b, c * NMB + (n + 1)))
                            pe.wait_ge(k_rows_done, nth(b, c * NMB + (n + 1)))
                            for k in range(KD):
                                mm = pe.matmul(g_ps[:, b, k * P:(k + 1) * P], k_rows[:, b, n, k * P:(k + 1) * P],
                                               u[:, b, k * P:(k + 1) * P], start=False, stop=False, skip_group_check=True)
                            mm.then_inc(g_full, 1)
                        filler(n, 1)

                walk(pe, step)
                for b in range(B):
                    out_turn(b, NC)
                for b in range(B):
                    out_rows(b, NC)

    def moe_phase(self):
        nc, a = self.nc, self.a
        x, ident, mod_t, gate_b, half, eps = self.x, self.ident, self.mod_t, self.gate_b, self.half, self.eps
        TOK = GT * P
        NH = E + 2
        out = self.out.rearrange("b (c p) d -> p (b c) d", p=P)
        with ExitStack() as ctx:
            def sb(name, shape, dt=F32):
                return ctx.enter_context(nc.sbuf_tensor(name, shape, dt))

            def ps(name, shape, dt=F32):
                return ctx.enter_context(nc.psum_tensor(name, shape, dt))

            w_hi, w_lo = self.w_hi, self.w_lo
            w2, b1, b2, gw = self.moe_small
            stats, mv = sb("m_stats", [P, GT, 6]), sb("m_mv", [P, GT, 2])
            veps, rstd = sb("m_veps", [P, GT]), sb("m_rstd", [P, GT])
            xn = sb("m_xn", [P, GT, D])
            h = sb("m_h", [P, KD, TOK])
            h_hi, h_lo = sb("m_h_hi", [P, 2, KD, TOK], F32R), sb("m_h_lo", [P, 2, KD, TOK], F32R)
            act_t = sb("m_act", [P, 2, NH, TOK])
            lg, top = sb("logits_sb", [P, GT, E]), sb("top", [P, GT, E])
            at_u, at_f = sb("top_at", [P, GT, E], U32), sb("top_at_f", [P, GT, 2])
            lane = sb("lane", [P, E])
            euler = sb("euler", [P, 1])
            diff, ratio = sb("logit_diff", [P, GT]), sb("gate_ratio", [P, GT])
            total, pair = sb("gate_total", [P, GT]), sb("gate_pair", [P, 2, GT])
            pick = sb("picked", [P, 2, GT, E])
            gates = sb("gates", [P, 2, GT, E + 1])
            gates_t = sb("gates_t", [E + 1, 2, GT, P])
            acc = sb("m_acc", [P, 2, D])
            dx = sb("m_dx", [P, 2, D])

            turn = ps("m_turn", [P, 2, 512])
            hid = ps("m_hid", [P, 2, 512])
            small = ps("m_small", [P, 512])
            shared = ps("m_shared", [P, 512])
            expert = ps("m_expert", [P, 2, 512])

            names = ("const_made stat_done aggr_done veps_done rstd_done xn_done turn_full h_done hi_done "
                     "hl_done logit_full logit_kept top_step gate_step ratio_done gates_done gturn_full gturn_done "
                     "hid_full act_done shared_full shared_kept expert_full acc_step dx_done x_done out_done")
            s = {n: self.sem("m_" + n) for n in names.split()}
            block = ctx.enter_context(nc.Block())

            @block.sync
            def _(sp):
                for n in range(NT):
                    sp.wait_ge(s["x_done"], n + 1)
                    sp.dma_start(out[:, n, :], x[:, n, :]).then_inc(s["out_done"], 16)
                sp.wait_ge(s["out_done"], 16 * NT)

            @block.gpsimd
            def _(pool):
                pool.iota(lane[:], pattern=[[1, E]], base=0, channel_multiplier=0, allow_small_or_imprecise_dtypes=True)
                pool.memset(euler[:], float(np.e)).then_inc(s["const_made"], 1)

                def rstd_of(g):
                    pool.wait_ge(s["aggr_done"], GT * (g + 1))
                    pool.tensor_tensor(veps[:], mv[:, :, 1], eps[:].broadcast_to([P, GT]), ALU.add).then_inc(s["veps_done"], 1)
                    pool.wait_ge(s["veps_done"], g + 1)
                    pool.tensor_tensor(rstd[:], veps[:], half[:].broadcast_to([P, GT]), ALU.pow).then_inc(s["rstd_done"], 1)

                def ratio_of(g):
                    pool.wait_ge(s["top_step"], 3 * g + 3)
                    pool.tensor_tensor(ratio[:], euler[:].broadcast_to([P, GT]), diff[:], ALU.pow).then_inc(s["ratio_done"], 1)

                def add_row(g, i):
                    n = g * GT + i
                    pool.wait_ge(s["dx_done"], n + 1)
                    pool.tensor_tensor(x[:, n, :], x[:, n, :], dx[:, n % 2], ALU.add).then_inc(s["x_done"], 1)

                pool.wait_ge(s["const_made"], 1)
                rstd_of(0)
                for g in range(-1, NG):
                    if g + 2 < NG:
                        rstd_of(g + 2)
                    if g >= 0:
                        add_row(g, 0)
                    if g + 1 < NG:
                        ratio_of(g + 1)
                    for i in range(1, GT if g >= 0 else 0):
                        add_row(g, i)

            @block.scalar
            def _(act):
                def drain_norm(g):
                    b = g * GT // NC
                    for k in range(KD):
                        act.wait_ge(s["turn_full"], KD * g + k + 1)
                        if g:
                            act.wait_ge(s["hl_done"], g)
                            act.wait_ge(s["logit_full"], g)
                        act.activation(h[:, k, :], turn[:, k, :], ACT.Identity,
                                       bias=mod_t[:, 1, SB_ * KD + k, b:b + 1],
                                       scale=mod_t[:, 1, CB * KD + k, b:b + 1]).then_inc(s["h_done"], 1)

                def gates_turned(g):
                    act.wait_ge(s["gturn_full"], g + 1)
                    act.activation(gates_t[:, g % 2], small[0:E + 1, :].rearrange("p (i t) -> p i t", i=GT), ACT.Copy
                                   ).then_inc(s["gturn_done"], 1)

                def hidden(g, m):
                    n = g * NH + m
                    act.wait_ge(s["hid_full"], n + 1)
                    act.activation(act_t[:, g % 2, m], hid[:, n % 2, :], ACT.Gelu, bias=b1[:, m:m + 1]
                                   ).then_inc(s["act_done"], 1)

                def keep_shared(n):
                    act.wait_ge(s["shared_full"], n + 1)
                    if n >= 2:
                        act.wait_ge(s["dx_done"], n - 1)
                    act.activation(acc[:, n % 2], shared[:, 0:D], ACT.Copy).then_inc(s["shared_kept"], 1)

                drain_norm(0)
                act.wait_ge(self.moe_in, 16 * 4)
                for g in range(-1, NG):
                    for m in range(NH):
                        if g + 1 < NG:
                            hidden(g + 1, m)
                        if g >= 0 and m % 2 == 0 and m // 2 < GT:
                            keep_shared(g * GT + m // 2)
                        if m == 5 and g + 2 < NG:
                            drain_norm(g + 2)
                    if g + 1 < NG:
                        gates_turned(g + 1)

            @block.vector
            def _(dve):
                def norms(g):
                    for i in range(GT):
                        dve.bn_stats(stats[:, i, :], x[:, g * GT + i, :]).then_inc(s["stat_done"], 1)
                    for i in range(GT):
                        dve.wait_ge(s["stat_done"], g * GT + i + 1)
                        dve.bn_aggr(mv[:, i, :], stats[:, i, :]).then_inc(s["aggr_done"], 1)

                def centre(g):
                    dve.wait_ge(s["rstd_done"], g + 1)
                    if g:
                        dve.wait_ge(s["turn_full"], KD * g)
                    for i in range(GT):
                        dve.tensor_scalar(xn[:, i, :], x[:, g * GT + i, :], mv[:, i, 0:1], rstd[:, i:i + 1],
                                          ALU.subtract, ALU.mult).then_inc(s["xn_done"], 1)

                def split(g):
                    dve.wait_ge(s["h_done"], KD * (g + 1))
                    dve.tensor_copy(h_hi[:, g % 2], h[:]).then_inc(s["hi_done"], 1)
                    dve.wait_ge(s["hi_done"], g + 1)
                    dve.tensor_tensor(h_lo[:, g % 2], h[:], h_hi[:, g % 2].bitcast(F32), ALU.subtract
                                      ).then_inc(s["hl_done"], 1)

                def gating(g):
                    q = g % 2
                    dve.wait_ge(s["logit_full"], g + 1)
                    dve.tensor_copy(lg[:], small[:, 0:GT * E].rearrange("p (i e) -> p i e", e=E)).then_inc(s["logit_kept"], 1)
                    dve.wait_ge(s["logit_kept"], g + 1)
                    for i in range(GT):
                        t = dve.max(top[:, i], lg[:, i])
                    t.then_inc(s["top_step"], 1)
                    dve.wait_ge(s["top_step"], 3 * g + 1)
                    for i in range(GT):
                        t = dve.max_index(at_u[:, i], top[:, i], lg[:, i])
                    t.then_inc(s["top_step"], 1)
                    dve.tensor_tensor(diff[:], top[:, :, 1], top[:, :, 0], ALU.subtract).then_inc(s["top_step"], 1)
                    dve.wait_ge(s["top_step"], 3 * g + 3)
                    base = 6 * g
                    dve.tensor_copy(at_f[:], at_u[:, :, 0:2]).then_inc(s["gate_step"], 1)
                    dve.wait_ge(s["ratio_done"], g + 1)
                    dve.tensor_scalar(total[:], ratio[:], 1.0, None, ALU.add).then_inc(s["gate_step"], 1)
                    dve.wait_ge(s["gate_step"], base + 2)
                    dve.reciprocal(pair[:, 0], total[:]).then_inc(s["gate_step"], 1)
                    dve.wait_ge(s["gate_step"], base + 3)
                    dve.tensor_tensor(pair[:, 1], ratio[:], pair[:, 0], ALU.mult)
                    for k in range(2):
                        t = dve.tensor_tensor(pick[:, k], lane[:].unsqueeze(1).broadcast_to([P, GT, E]),
                                              at_f[:, :, k:k + 1].broadcast_to([P, GT, E]), ALU.is_equal)
                    t.then_inc(s["gate_step"], 1)
                    dve.wait_ge(s["gate_step"], base + 4)
                    for k in range(2):
                        t = dve.tensor_tensor(pick[:, k], pick[:, k], pair[:, k].unsqueeze(2).broadcast_to([P, GT, E]),
                                              ALU.mult)
                    t.then_inc(s["gate_step"], 1)
                    dve.wait_ge(s["gate_step"], base + 5)
                    dve.tensor_tensor(gates[:, q, :, 0:E], pick[:, 0], pick[:, 1], ALU.add).then_inc(s["gates_done"], 1)
                    dve.memset(total[:], 0.0).then_inc(s["gate_step"], 1)

                def weigh(g, i, k):
                    n = g * GT + i
                    dve.wait_ge(s["expert_full"], 4 * n + k + 1)
                    if k == 0:
                        dve.wait_ge(s["shared_kept"], n + 1)
                    for j in range(2):
                        e = 2 * k + j
                        if e:
                            dve.wait_ge(s["acc_step"], E * n + e)
                        ins = dve.scalar_tensor_tensor(acc[:, n % 2], expert[:, k % 2, j * D:(j + 1) * D],
                                                       gates[:, g % 2, i, e:e + 1], acc[:, n % 2], ALU.mult, ALU.add)
                        ins.then_inc(s["acc_step"], 1)

                def gate_rows(g, i):
                    n = g * GT + i
                    b = g * GT // NC
                    dve.wait_ge(s["acc_step"], E * (n + 1))
                    if n >= 2:
                        dve.wait_ge(s["x_done"], n - 1)
                    dve.tensor_tensor(dx[:, n % 2], acc[:, n % 2], gate_b[:, 1, 1, b, :], ALU.mult).then_inc(s["dx_done"], 1)

                dve.memset(gates[:], 1.0)
                norms(0)
                centre(0)
                split(0)
                dve.wait_ge(s["const_made"], 1)
                for g in range(-1, NG):
                    if g + 2 < NG:
                        norms(g + 2)
                    for i in range(GT):
                        if g >= 0:
                            for k in range(E // 2):
                                weigh(g, i, k)
                            gate_rows(g, i)
                        if i == 0 and g + 1 < NG:
                            gating(g + 1)
                        if i == 1 and g + 2 < NG:
                            centre(g + 2)
                    if g + 2 < NG:
                        split(g + 2)

            @block.tensor
            def _(pe):
                def norm_turn(g):
                    pe.wait_ge(s["xn_done"], GT * (g + 1))
                    for k in range(KD):
                        if g:
                            pe.wait_ge(s["h_done"], KD * (g - 1) + k + 1)
                        for i in range(GT):
                            t = pe.transpose(turn[:, k, i * P:(i + 1) * P], xn[:, i, k * P:(k + 1) * P], ident[:])
                        t.then_inc(s["turn_full"], 1)

                def logits(g):
                    pe.wait_ge(s["h_done"], KD * (g + 1))
                    if g:
                        pe.wait_ge(s["gturn_done"], g)
                    for i in range(GT):
                        for k in range(KD):
                            mm = pe.matmul(small[:, i * E:(i + 1) * E], h[:, k, i * P:(i + 1) * P], gw[:, k, :],
                                           start=(k == 0), stop=(k == KD - 1))
                    mm.then_inc(s["logit_full"], 1)

                def gates_turn(g):
                    pe.wait_ge(s["gates_done"], g + 1)
                    for i in range(GT):
                        t = pe.transpose(small[0:E + 1, i * P:(i + 1) * P], gates[:, g % 2, i, :], ident[:])
                    t.then_inc(s["gturn_full"], 1)

                def hidden(g, m):
                    n = g * NH + m
                    if n >= 2:
                        pe.wait_ge(s["act_done"], n - 1)
                    cols = slice(m * P, (m + 1) * P)
                    for i, (ww, hh) in enumerate([(w_hi, h_hi), (w_lo, h_hi), (w_hi, h_lo)]):
                        for k in range(KD):
                            mm = pe.matmul(hid[:, n % 2, :], ww[:, k, cols], hh[:, g % 2, k, :],
                                           start=(i == 0 and k == 0), stop=(i == 2 and k == KD - 1))
                    mm.then_inc(s["hid_full"], 1)

                def tile_rows(g, i):
                    n = g * GT + i
                    toks = slice(i * P, (i + 1) * P)
                    if n:
                        pe.wait_ge(s["shared_kept"], n)
                    pe.wait_ge(s["gturn_done"], g + 1)
                    pe.wait_ge(s["act_done"], (g + 1) * NH)
                    pe.matmul(shared[:, 0:D], gates_t[:, g % 2, i, :], b2[:], start=True, stop=False)
                    for m in range(E, NH):
                        mm = pe.matmul(shared[:, 0:D], act_t[:, g % 2, m, toks], w2[:, m, :], start=False, stop=(m == NH - 1))
                    mm.then_inc(s["shared_full"], 1)
                    for k in range(E // 2):
                        if 4 * n + k >= 2:
                            pe.wait_ge(s["acc_step"], 2 * (4 * n + k - 1))
                        for j in range(2):
                            e = 2 * k + j
                            mm = pe.matmul(expert[:, k % 2, j * D:(j + 1) * D], act_t[:, g % 2, e, toks], w2[:, e, :],
                                           start=True, stop=True)
                        mm.then_inc(s["expert_full"], 1)

                norm_turn(0)
                pe.wait_ge(self.moe_in, 16 * 4)
                pe.wait_ge(self.w_ready, self.chunks + 3)
                for g in range(-1, NG):
                    if g + 1 < NG:
                        pe.wait_ge(s["hl_done"], g + 2)
                    for m in range(NH):
                        if g + 1 < NG:
                            hidden(g + 1, m)
                            if m == 0:
                                logits(g + 1)
                        if g >= 0 and m % 2 == 0 and m // 2 < GT:
                            tile_rows(g, m // 2)
                        if m == 5 and g + 2 < NG:
                            norm_turn(g + 2)
                    if g + 1 < NG:
                        gates_turn(g + 1)


def rope_tables(length, dim):
    power = np.arange(0, dim, 2, dtype=np.float32) / np.float32(dim)
    inv_freq = np.float32(1.0) / np.power(10000.0, power.astype(np.float64)).astype(np.float32)
    angle = np.outer(np.arange(length, dtype=np.float32), inv_freq).astype(np.float32).astype(np.float64)
    sin = np.sin(angle)
    return np.cos(angle).astype(np.float32), np.concatenate([-sin, sin], axis=1).astype(np.float32)


def kernel(**inputs):
    import concourse.bacc as bacc
    from concourse.bass_utils import run_bass_kernel_spmd

    i = {k: np.asarray(v) for k, v in inputs.items()}
    cos, sin = rope_tables(S, HD)
    cos1, sin1 = rope_tables(S, TD)
    quads = np.arange(FI).reshape(FI // 512, P, 4).transpose(0, 2, 1).reshape(-1)
    arrays = {
        "x": i["L0_attn_x"],
        "cond": np.stack([i[f"L{n}_c"].T.reshape(KD, P, B).transpose(1, 0, 2) for n in range(2)], axis=1),
        "wmod": np.stack([i["L0_wmod"], i["L1_wmod"]]),
        "wqkv": np.concatenate([i["L0_attn_Wk"].T, i["L0_attn_Wv"].T, i["L0_attn_Wq"].T], axis=1),
        "wo": i["L0_attn_Wo"].T,
        "cos": cos, "sin": sin, "cos1": cos1, "sin1": sin1,
        "wgu": np.concatenate([i["L0_ffn_w_gate"][:, quads], i["L0_ffn_w_up"][:, quads]], axis=1),
        "wd": i["L0_ffn_w_down"][quads, :],
        "wkv1": np.concatenate([i["L1_attn_Wk"].T, i["L1_attn_Wv"].T], axis=1),
        "wo1": i["L1_attn_Wo"].T,
        "ln_g": i["L1_attn_ln_gamma"], "ln_b": i["L1_attn_ln_beta"],
        "gw": i["L1_ffn_gate_w"],
        "w1": np.concatenate([i["L1_ffn_w1"].transpose(1, 0, 2).reshape(D, E * EH), i["L1_ffn_shared_w1"]], axis=1),
        "b1": np.concatenate([i["L1_ffn_b1"], i["L1_ffn_shared_b1"].reshape(2, EH)], axis=0).T,
        "w2": np.concatenate([i["L1_ffn_w2"].reshape(E * EH, D), i["L1_ffn_shared_w2"]], axis=0),
        "b2": np.concatenate([i["L1_ffn_b2"], i["L1_ffn_shared_b2"][None]], axis=0),
    }
    arrays = {k: np.ascontiguousarray(v) for k, v in arrays.items()}
    nc = bacc.Bacc("TRN2", target_bir_lowering=False, num_devices=1)
    aps = {k: nc.dram_tensor(f"in_{k}", v.shape, mybir.dt.from_np(v.dtype), kind="ExternalInput").ap()
           for k, v in arrays.items()}
    out = nc.dram_tensor("out", (B, S, D), F32, kind="ExternalOutput").ap()
    build(nc, aps, out)
    r = run_bass_kernel_spmd(nc, [{f"in_{k}": v for k, v in arrays.items()}], core_ids=[0])
    return r.results[0]["out"]
```

```python
from contextlib import ExitStack

import numpy as np

import concourse.bass as bass
from concourse import mybir

F32 = mybir.dt.float32
F32R = mybir.dt.float32r
BF16 = mybir.dt.bfloat16
U32 = mybir.dt.uint32
ALU = mybir.AluOpType
ACT = mybir.ActivationFunctionType
AX = mybir.AxisListType

P = 128
B, S, D = 2, 1024, 256
KD = D // P
NC = S // P
NT = B * NC
LN_EPS = 1e-5

H, KVH, HD = 16, 4, 128
REP = H // KVH
GW = REP * HD
QKV = (H + 2 * KVH) * HD
DEN_EPS = 1e-6
VW = HD + 1

FI = 1024
NM = FI // P
TH = 16
TD = D // TH
MB = 16
NMB = P // MB
INV_N = 2.0 / (MB * TD)
E, EH = 8, 128
GT = 4
NG = NT // GT

WCH = 512

SA, CA, GA, SB_, CB, GB = range(6)


def at(c, b, per, k):
    return c * (2 * per) + (per * b + k)


def nth(b, n):
    return n * B + (b + 1 - B)


def build(nc, a, out):
    with ExitStack() as keep:
        Program(nc, a, out, keep).run()


class Program:
    def __init__(self, nc, a, out, keep):
        self.nc, self.a, self.out, self.keep = nc, a, out, keep

    def sem(self, name):
        return self.keep.enter_context(self.nc.semaphore(name))

    def run(self):
        nc = self.nc

        def sb(name, shape, dt=F32):
            return self.keep.enter_context(nc.sbuf_tensor(name, shape, dt))

        self.x = sb("x_sb", [P, NT, D])
        self.ident = sb("ident", [P, P])
        self.mod_t = sb("mod_t", [P, 2, 6 * KD, B])
        self.gate_b = sb("gate_b", [P, 2, 2, B, D])
        self.half = sb("minus_half", [P, 1])
        self.eps = sb("eps", [P, 1])
        self.w_hi, self.w_lo = sb("w_hi", [P, KD, QKV], F32R), sb("w_lo", [P, KD, QKV], F32R)
        self.scond = sb("silu_cond", [P, 2, KD, B])
        self.wide = sb("silu_cond_wide", [P, 2 * KD * B, P])
        self.g_stats, self.g_mv = sb("g_stats", [P, GT, 6]), sb("g_mv", [P, GT, 2])
        self.g_veps, self.g_rstd = sb("g_veps", [P, GT]), sb("g_rstd", [P, GT])
        self.g_xn = sb("g_xn", [P, GT, D])
        self.w_in = [self.sem(f"w_in{i}") for i in range(QKV // WCH)]
        self.w_half = self.sem("w_half")
        self.w_ready = self.sem("w_ready")
        self.attention_phase()
        self.ffn_phase()
        self.scan_phase()
        self.moe_phase()

    def stage_for(self, ctx, name, first, slots):
        self.stage = ctx.enter_context(self.nc.sbuf_tensor(name, [P, slots, KD, WCH], F32))
        self.first, self.slots = first, slots

    def raw(self, n, width):
        return self.stage[:, (n - self.first) % self.slots, :, 0:width]

    def load_chunk(self, sp, n, src, width=WCH):
        if n - self.first >= self.slots:
            sp.wait_ge(self.w_ready, n - self.slots + 1)
        sp.dma_start(self.raw(n, width), src.rearrange("(k p) n -> p k n", p=P)).then_inc(self.w_in[n % len(self.w_in)], 16)

    def chunk_high(self, engine, n, col, width=WCH):
        engine.wait_ge(self.w_in[n % len(self.w_in)], 16 * (n // len(self.w_in) + 1))
        if n:
            engine.wait_ge(self.w_half, n)
        dst = self.w_hi[:, :, col:col + width]
        if engine.engine == self.nc.scalar.engine:
            i = engine.activation(dst, self.raw(n, width), ACT.Copy)
        else:
            i = engine.tensor_copy(dst, self.raw(n, width))
        i.then_inc(self.w_half, 1)

    def chunk_low(self, dve, n, col, width=WCH):
        cols = slice(col, col + width)
        dve.wait_ge(self.w_half, n + 1)
        dve.tensor_tensor(self.w_lo[:, :, cols], self.raw(n, width), self.w_hi[:, :, cols].bitcast(F32), ALU.subtract
                          ).then_inc(self.w_ready, 1)

    def split_chunk(self, dve, n, col, width=WCH):
        self.chunk_high(dve, n, col, width)
        self.chunk_low(dve, n, col, width)

    def modulation(self, l, wmod, scond, wide, sems, mod_ps, gate_ps, gmag, gneg):
        mod_t, gate_b, s = self.mod_t, self.gate_b, sems

        def pe_vectors(pe, lo, hi, first):
            for m in range(lo * KD, hi * KD):
                for k in range(KD):
                    mm = pe.matmul(mod_ps[:, m * B:(m + 1) * B], wmod[:, k, m * P:(m + 1) * P], scond[:, l, k, :],
                                   start=(first and m == lo * KD and k == 0), stop=(k == KD - 1), skip_group_check=True)
            mm.then_inc(s["mod_full"], 1)

        def pe_gates(pe):
            for i, kind in enumerate((GA, GB)):
                for b in range(B):
                    for k in range(KD):
                        mm = pe.matmul(gate_ps[:, i, b * D:(b + 1) * D], wide[:, (l * KD + k) * B + b, :],
                                       wmod[:, k, kind * D:(kind + 1) * D], start=(k == 0), stop=(k == KD - 1))
            mm.then_inc(s["gates_full"], 1)

        def dve_vectors(dve, lo, hi, n):
            dve.wait_ge(s["mod_full"], n)
            v = mod_t[:, l, lo * KD:hi * KD]
            dve.tensor_copy(v, mod_ps[:, lo * KD * B:hi * KD * B].rearrange("p (m b) -> p m b", b=B)
                            ).then_inc(s["mod_kept"], 1)
            dve.wait_ge(s["mod_kept"], n)
            for kind in (CA, CB):
                if lo <= kind < hi:
                    v = mod_t[:, l, kind * KD:(kind + 1) * KD]
                    dve.tensor_scalar(v, v, 1.0, None, ALU.add).then_inc(s["mod_done"], 1)

        def dve_gates(dve):
            dve.wait_ge(s["gate_abs"], 1)
            dve.tensor_scalar(gneg, gate_ps, 0.0, 2.0, ALU.is_ge, ALU.mult)
            dve.tensor_scalar(gmag, gmag, 0.25, None, ALU.max).then_inc(s["gate_step"], 1)
            dve.wait_ge(s["gate_step"], 1)
            dve.scalar_tensor_tensor(gate_b[:, l].rearrange("p g b d -> p g (b d)"), gneg, -1.0, gmag,
                                     ALU.add, ALU.mult).then_inc(s["gate_done"], 1)
            dve.wait_ge(s["gate_done"], 1)

        def act_gates(act):
            act.wait_ge(s["gates_full"], 1)
            act.activation(gmag, gate_ps, ACT.Abs).then_inc(s["gate_abs"], 1)

        return pe_vectors, pe_gates, dve_vectors, dve_gates, act_gates

    def group_sems(self, prefix, names):
        names = "stat_done aggr_done veps_done rstd_done xn_done turn_full h_done hi_done hl_done " + names
        return {n: self.sem(prefix + n) for n in names.split()}

    def group_norm(self, s):
        x, stats, mv, veps, rstd, xn = self.x, self.g_stats, self.g_mv, self.g_veps, self.g_rstd, self.g_xn

        def norms(dve, g):
            for i in range(GT):
                dve.bn_stats(stats[:, i, :], x[:, g * GT + i, :]).then_inc(s["stat_done"], 1)
            for i in range(GT):
                dve.wait_ge(s["stat_done"], g * GT + i + 1)
                dve.bn_aggr(mv[:, i, :], stats[:, i, :]).then_inc(s["aggr_done"], 1)

        def rstd_of(pool, g):
            pool.wait_ge(s["aggr_done"], GT * (g + 1))
            pool.tensor_tensor(veps[:], mv[:, :, 1], self.eps[:].broadcast_to([P, GT]), ALU.add).then_inc(s["veps_done"], 1)
            pool.wait_ge(s["veps_done"], g + 1)
            pool.tensor_tensor(rstd[:], veps[:], self.half[:].broadcast_to([P, GT]), ALU.pow).then_inc(s["rstd_done"], 1)

        def centre(dve, g):
            dve.wait_ge(s["rstd_done"], g + 1)
            if g:
                dve.wait_ge(s["turn_full"], KD * g)
            for i in range(GT):
                dve.tensor_scalar(xn[:, i, :], x[:, g * GT + i, :], mv[:, i, 0:1], rstd[:, i:i + 1],
                                  ALU.subtract, ALU.mult).then_inc(s["xn_done"], 1)

        return norms, rstd_of, centre

    def scan_norm_ops(self):
        x, stats, mv, veps, rstd, xn = self.x, self.t_stats, self.t_mv, self.t_veps, self.t_rstd, self.t_xn
        s = self.scan_s

        def x_norm(dve, c, b):
            dve.bn_stats(stats[:, 0, b, :], x[:, bass.ds(c + b * NC, 1), :].rearrange("p o d -> p (o d)")
                         ).then_inc(s["x_stat"], 1)

        def x_aggregate(dve, b):
            dve.bn_aggr(mv[:, 0, b, :], stats[:, 0, b, :]).then_inc(s["x_aggr"], 1)

        def x_rstd(pool, b, n):
            pool.wait_ge(s["x_aggr"], nth(b, n))
            pool.tensor_tensor(veps[:, 0, b:b + 1], mv[:, 0, b, 1:2], self.eps[:], ALU.add).then_inc(s["x_veps"], 1)
            pool.wait_ge(s["x_veps"], nth(b, n))
            pool.tensor_tensor(rstd[:, 0, b:b + 1], veps[:, 0, b:b + 1], self.half[:], ALU.pow).then_inc(s["x_rstd"], 1)

        def x_centre(dve, c, b, n):
            dve.wait_ge(s["x_rstd"], nth(b, n))
            dve.tensor_scalar(xn[:, b], x[:, bass.ds(c + b * NC, 1), :].rearrange("p o d -> p (o d)"),
                              mv[:, 0, b, 0:1], rstd[:, 0, b:b + 1], ALU.subtract, ALU.mult).then_inc(s["xn_done"], 1)

        return x_norm, x_aggregate, x_rstd, x_centre

    def modulation_sems(self, l):
        return {n: self.sem(f"{n}{l}") for n in "mod_full mod_kept mod_done gates_full gate_abs gate_step gate_done".split()}

    def attention_phase(self):
        nc, a = self.nc, self.a
        x, ident, mod_t, gate_b, half, eps = self.x, self.ident, self.mod_t, self.gate_b, self.half, self.eps
        NW = QKV // WCH
        RI = 1 + KVH
        with ExitStack() as ctx:
            def sb(name, shape, dt=F32):
                return ctx.enter_context(nc.sbuf_tensor(name, shape, dt))

            def ps(name, shape, dt=F32):
                return ctx.enter_context(nc.psum_tensor(name, shape, dt))

            w_hi, w_lo = self.w_hi, self.w_lo
            self.stage_for(ctx, "a_stage", 0, 3)
            wmod = sb("a_wmod", [P, KD, 6 * D])
            cond, scond = sb("cond", [P, 2, KD, B]), self.scond
            wide = self.wide
            wo = sb("wo_sb", [P, H, D])
            cos, sin = sb("cos_sb", [P, NC, HD // 2]), sb("sin_sb", [P, NC, HD])
            causal = sb("causal", [P, P])
            stats, mv = sb("a_stats", [P, 2, 6]), sb("a_mv", [P, 2, 2])
            rstd, veps = sb("a_rstd", [P, 2]), sb("a_veps", [P, 2])
            xn = sb("a_xn", [P, 2, D])
            h = sb("a_h", [P, 2, KD, P])
            h_hi, h_lo = sb("a_h_hi", [P, 2, KD, P], F32R), sb("a_h_lo", [P, 2, KD, P], F32R)
            t1, t2 = sb("rope_cos", [P, 2, GW]), sb("rope_sin", [P, 2, GW])
            y, ex = sb("rope_sum", [P, 2, GW]), sb("rope_exp", [P, 2, GW])
            feat = sb("feat", [P, 2, RI, GW])
            k_t, q_t = sb("k_t", [P, KVH, P]), sb("q_t", [P, KVH, REP * P])
            v = sb("v_ones", [P, 2, KVH, VW])
            am = sb("score_masked", [P, 2, REP * P])
            on = sb("attn_out", [P, 2, GW])
            o_t = sb("attn_out_t", [P, H, P])
            state = sb("state", [P, 2, KVH, VW])
            den, rden = sb("den", [P, REP]), sb("rden", [P, REP])
            dx = sb("a_dx", [P, D])

            proj = ps("proj", [P, 2, 512])
            turn = ps("turn", [P, 2, 512])
            score = ps("score", [P, 2, 512])
            num = ps("num", [P, 2, 512])

            names = ("cond_in wmod_in wmod_ffn_in x0_in x1_in x_in wo_in tab_in ident_zero const_made silu_done wide_done causal_made stat_done aggr_done veps_done rstd_done xn_done "
                     "hi_done hl_done proj_full proj_free turn_full turn_free score_full score_free num_full num_free "
                     "y_done relu_done exp_done feat_done den_done rden_done dx_done x_done mask_one")
            s = {n: self.sem("a_" + n) for n in names.split()}
            self.ffn_s = self.group_sems("f_", "wd_in wmod_in gate_full up_full silu_done hid_done mag_done pick_step "
                                         "pick_done rows_full dx_done x_done")
            ffn_norms, ffn_rstd, ffn_centre = self.group_norm(self.ffn_s)
            msem = self.modulation_sems(0)
            pe_vectors, pe_gates, dve_vectors, dve_gates, act_gates = self.modulation(
                0, wmod, scond, wide, msem, score[:, 0, :], num[:], am[:], on[:])
            block = ctx.enter_context(nc.Block())

            def proj_item(c, b, j):
                return at(c, b, 7, 6 + j)

            def turn_item(c, b, j):
                return at(c, b, 10, 2 + j - (1 if last(c, b) else 0))

            def last(c, b):
                return isinstance(c, int) and c == NC - 1 and b == 1

            def walk(engine, step):
                with nc.Fori(0, NC - 1, engines=(engine.engine,), hint_back_edge=True) as c:
                    step(c, 0, True, True)
                    step(c, 1, True, True)
                step(NC - 1, 0, True, False)
                step(NC - 1, 1, False, False)

            @block.sync
            def _(sp):
                xr = a["x"].rearrange("b (c p) d -> p b c d", p=P)
                xs = x[:].rearrange("p (b c) d -> p b c d", b=B)

                def chunk(i):
                    self.load_chunk(sp, i, a["wqkv"][:, i * WCH:(i + 1) * WCH])

                sp.dma_start(cond[:], a["cond"]).then_inc(s["cond_in"], 16)
                wm = a["wmod"][0].rearrange("(k p) n -> p k n", p=P)
                sp.dma_start(wmod[:, :, 0:GA * D], wm[:, :, 0:GA * D]).then_inc(s["wmod_in"], 16)
                sp.dma_start(xs[:, :, 0, :], xr[:, :, 0, :]).then_inc(s["x0_in"], 16)
                chunk(0)
                chunk(1)
                sp.dma_start(cos[:], a["cos"].rearrange("(c p) d -> p c d", p=P)).then_inc(s["tab_in"], 16)
                sp.dma_start(sin[:], a["sin"].rearrange("(c p) d -> p c d", p=P)).then_inc(s["tab_in"], 16)
                chunk(2)
                sp.dma_start(xs[:, :, 1, :], xr[:, :, 1, :]).then_inc(s["x1_in"], 16)
                chunk(3)
                sp.dma_start(wmod[:, :, GA * D:6 * D], wm[:, :, GA * D:6 * D]).then_inc(s["wmod_ffn_in"], 16)
                chunk(4)
                chunk(5)
                sp.dma_start(wo[:], a["wo"].rearrange("(h p) n -> p h n", p=P)).then_inc(s["wo_in"], 16)
                for b in range(B):
                    sp.dma_start(xs[:, b, 2:NC], xr[:, b, 2:NC]).then_inc(s["x_in"], 16)
                for i in range(2 * FI // WCH):
                    self.load_chunk(sp, NW + i, a["wgu"][:, i * WCH:(i + 1) * WCH])

            @block.gpsimd
            def _(pool):
                pool.memset(ident[:], 0.0).then_inc(s["ident_zero"], 1)
                pool.memset(half[:], -0.5)
                pool.memset(eps[:], LN_EPS)
                pool.wait_ge(s["ident_zero"], 1)
                pool.affine_select(out=ident[:], in_=ident[:], compare_op=ALU.not_equal, fill=1.0, base=0,
                                   pattern=[[-1, P]], channel_multiplier=1).then_inc(s["const_made"], 1)
                pool.wait_ge(s["const_made"], 1)
                pool.memset(causal[:], 1.0).then_inc(s["mask_one"], 1)
                pool.wait_ge(s["mask_one"], 1)
                pool.affine_select(out=causal[:], in_=causal[:], compare_op=ALU.is_ge, fill=0.0, base=0,
                                   pattern=[[1, P]], channel_multiplier=-1).then_inc(s["causal_made"], 1)

                def rstd_of(n, b):
                    pool.wait_ge(s["aggr_done"], n)
                    pool.tensor_tensor(veps[:, b:b + 1], mv[:, b, 1:2], eps[:], ALU.add).then_inc(s["veps_done"], 1)
                    pool.wait_ge(s["veps_done"], n)
                    pool.tensor_tensor(rstd[:, b:b + 1], veps[:, b:b + 1], half[:], ALU.pow).then_inc(s["rstd_done"], 1)

                def add_rope(item, parity, drained, first=False):
                    pool.wait_ge(s["proj_free"], drained)
                    if not first:
                        pool.wait_ge(s["feat_done"], item - 1)
                    pool.tensor_tensor(y[:, parity], t1[:, parity], t2[:, parity], ALU.add).then_inc(s["y_done"], 1)

                rstd_of(1, 0)
                rstd_of(2, 1)
                for r in range(RI):
                    add_rope(r, r % 2, 2 + (r + 1 if r else 0) + 1, first=r < 2)

                def step(c, b, nxt, norm):
                    if norm:
                        rstd_of(at(c, b, 1, 3), b)
                    if nxt:
                        for r in range(RI):
                            j = r + 1 if r else 0
                            add_rope(at(c, b, RI, RI + r), (b + 1 + r) % 2, 2 + 1 + proj_item(c, b, j))

                walk(pool, step)
                ffn_rstd(pool, 0)

            @block.scalar
            def _(act):
                def drain_turn(c, b, j, dst, src):
                    n = turn_item(c, b, j)
                    act.wait_ge(s["turn_full"], n + 1)
                    act.activation(dst, src, ACT.Copy).then_inc(s["turn_free"], 1)

                def drain_norm(n, parity, bank, b):
                    act.wait_ge(s["turn_full"], n + 1)
                    for k in range(KD):
                        i = act.activation(h[:, parity, k, :], turn[:, bank, k * P:(k + 1) * P], ACT.Identity,
                                           bias=mod_t[:, 0, SA * KD + k, b:b + 1], scale=mod_t[:, 0, CA * KD + k, b:b + 1])
                    i.then_inc(s["turn_free"], 1)

                def exp_of(item, parity):
                    act.wait_ge(s["y_done"], item + 1)
                    act.activation(ex[:, parity], y[:, parity], ACT.Relu, scale=-1.0).then_inc(s["relu_done"], 1)
                    act.wait_ge(s["relu_done"], item + 1)
                    act.activation(ex[:, parity], ex[:, parity], ACT.Exp, scale=-1.0).then_inc(s["exp_done"], 1)

                act.wait_ge(s["cond_in"], 16)
                act.activation(scond[:], cond[:], ACT.Silu).then_inc(s["silu_done"], 1)
                act.wait_ge(msem["mod_done"], 1)
                drain_norm(0, 0, 0, 0)
                drain_norm(1, 1, 1, 1)

                for n in range(1, 3):
                    self.chunk_high(act, n, n * WCH)
                for r in range(RI):
                    if r + 3 < NW:
                        self.chunk_high(act, r + 3, (r + 3) * WCH)
                    exp_of(r, r % 2)
                act_gates(act)

                def step(c, b, nxt, norm):
                    tp = 1 if last(c, b) else 0

                    def bank(j):
                        return (j + tp) % 2

                    def e(r):
                        if nxt:
                            exp_of(at(c, b, RI, RI + r), (b + 1 + r) % 2)

                    drain_turn(c, b, 0, k_t[:], turn[:, bank(0), :].rearrange("p (g t) -> p g t", g=KVH))
                    for g in range(KVH):
                        drain_turn(c, b, 1 + g, q_t[:, g], turn[:, bank(1 + g), :])
                        if g == 2:
                            e(0)
                    for g in range(KVH):
                        drain_turn(c, b, 5 + g, o_t[:, g * REP:(g + 1) * REP, :],
                                   turn[:, bank(5 + g), :].rearrange("p (r t) -> p r t", r=REP))
                        e(1 + g)
                    if norm:
                        drain_norm(turn_item(c, b, 9), b, bank(9), b)

                walk(act, step)

            @block.vector
            def _(dve):
                dve.memset(state[:], 0.0)
                dve.memset(v[:, :, :, HD:VW], 1.0)
                dve.memset(dx[:], 0.0).then_inc(s["proj_free"], 2)
                dve.memset(h[:], 0.0).then_inc(s["turn_free"], 2)

                def norm(t, b):
                    dve.bn_stats(stats[:, b, :], x[:, t, :]).then_inc(s["stat_done"], 1)

                def aggregate(b):
                    dve.bn_aggr(mv[:, b, :], stats[:, b, :]).then_inc(s["aggr_done"], 1)

                def centre(t, n, b):
                    dve.wait_ge(s["rstd_done"], n)
                    dve.tensor_scalar(xn[:, b, :], x[:, t, :], mv[:, b, 0:1], rstd[:, b:b + 1],
                                      ALU.subtract, ALU.mult).then_inc(s["xn_done"], 1)

                def split(n, parity, drained):
                    dve.wait_ge(s["turn_free"], drained)
                    dve.tensor_copy(h_hi[:, parity], h[:, parity]).then_inc(s["hi_done"], 1)
                    dve.wait_ge(s["hi_done"], n)
                    dve.tensor_tensor(h_lo[:, parity], h[:, parity], h_hi[:, parity].bitcast(F32),
                                      ALU.subtract).then_inc(s["hl_done"], 1)

                def rope(item, parity, bank, c, n, first=False):
                    heads = proj[:, bank, :].rearrange("p (g d) -> p g d", d=HD)
                    halves = heads.rearrange("p g (u d) -> p g u d", u=2)
                    cc = cos[:, bass.ds(c, 1), :].rearrange("p o d -> p (o d)").unsqueeze(1)
                    ss = sin[:, bass.ds(c, 1), :].rearrange("p o (u d) -> p (o u) d", u=2).unsqueeze(1)
                    dve.wait_ge(s["proj_full"], n + 1)
                    if not first:
                        dve.wait_ge(s["y_done"], item - 1)
                    dve.tensor_tensor(t1[:, parity].rearrange("p (g d) -> p g d", d=HD // 2),
                                      proj[:, bank, :].rearrange("p (g d) -> p g d", d=HD // 2),
                                      cc.broadcast_to([P, 2 * REP, HD // 2]), ALU.mult)
                    dve.tensor_tensor(t2[:, parity].rearrange("p (g u d) -> p g u d", u=2, d=HD // 2),
                                      halves[:, :, ::-1, :], ss.broadcast_to([P, REP, 2, HD // 2]),
                                      ALU.mult).then_inc(s["proj_free"], 1)

                def keep_v(parity, bank, n):
                    dve.wait_ge(s["proj_full"], n + 1)
                    dve.tensor_copy(v[:, parity, :, 0:HD], proj[:, bank, :].rearrange("p (g d) -> p g d", d=HD)
                                    ).then_inc(s["proj_free"], 1)

                def feature(item, parity, dst):
                    dve.wait_ge(s["exp_done"], item + 1)
                    dve.scalar_tensor_tensor(dst, y[:, parity], 0.0, ex[:, parity], ALU.max, ALU.add
                                             ).then_inc(s["feat_done"], 1)

                dve.wait_ge(s["silu_done"], 1)
                dve.tensor_copy(wide[:], scond[:].rearrange("p l k b -> p (l k b)").unsqueeze(2)
                                .broadcast_to([P, 2 * KD * B, P])).then_inc(s["wide_done"], 1)
                dve.wait_ge(s["x0_in"], 16)
                for b in range(B):
                    norm(b * NC, b)
                dve.wait_ge(s["stat_done"], B)
                for b in range(B):
                    aggregate(b)
                dve_vectors(dve, SA, GA, 1)
                centre(0, 1, 0)
                centre(NC, 2, 1)

                def project_rope(r):
                    rope(r, r % 2, (r + 1) % 2, 0, r + 1, first=r < 2)
                    feature(r - 1, (r - 1) % 2, feat[:, 0, r - 1, :])

                self.split_chunk(dve, 0, 0)
                split(1, 0, 2 + 1)
                self.chunk_low(dve, 1, WCH)
                dve.wait_ge(s["tab_in"], 32)
                rope(0, 0, 0, 0, 0, first=True)
                self.chunk_low(dve, 2, 2 * WCH)
                keep_v(0, 1, 1)
                for r in range(1, RI):
                    if r + 2 < NW:
                        self.chunk_low(dve, r + 2, (r + 2) * WCH)
                    project_rope(r)
                feature(RI - 1, (RI - 1) % 2, feat[:, 0, RI - 1, :])
                dve_vectors(dve, SB_, GB, 2)
                dve.memset(den[:], 0.0).then_inc(s["score_free"], 2)
                dve_gates(dve)
                dve.memset(rden[:], 0.0).then_inc(s["num_free"], 1)
                dve.wait_ge(s["causal_made"], 1)
                dve.wait_ge(s["x1_in"], 16)

                def step(c, b, nxt, norm_on):
                    nb = 1 - b
                    nc_ = c + b

                    def masked(g):
                        dve.wait_ge(s["score_full"], at(c, b, KVH, g + 1))
                        dve.tensor_tensor(am[:, g % 2].rearrange("p (r t) -> p r t", r=REP),
                                          score[:, g % 2, :].rearrange("p (r t) -> p r t", r=REP),
                                          causal[:].unsqueeze(1).broadcast_to([P, REP, P]),
                                          ALU.mult).then_inc(s["score_free"], 1)

                    def normalise(g):
                        dve.wait_ge(s["num_full"], at(c, b, KVH + 1, g + 1))
                        pairs = num[:, :, 0:2 * VW].rearrange("p k (h w) -> p k h w", w=VW)
                        dve.tensor_scalar(den[:].rearrange("p (k h) -> p k h", k=2), pairs[:, :, :, HD], DEN_EPS, None,
                                          ALU.add).then_inc(s["den_done"], 1)
                        dve.wait_ge(s["den_done"], at(c, b, KVH, g + 1))
                        dve.reciprocal(rden[:], den[:]).then_inc(s["rden_done"], 1)
                        dve.wait_ge(s["rden_done"], at(c, b, KVH, g + 1))
                        dve.tensor_tensor(on[:, g % 2].rearrange("p (k h d) -> p k h d", k=2, h=2),
                                          pairs[:, :, :, 0:HD],
                                          rden[:].rearrange("p (k h) -> p k h", k=2).unsqueeze(3)
                                          .broadcast_to([P, 2, 2, HD]), ALU.mult).then_inc(s["num_free"], 1)

                    def q_rope(r):
                        if nxt:
                            rope(at(c, b, RI, RI + r), (b + 1 + r) % 2, (b + (r + 1 if r else 0)) % 2, nc_,
                                 proj_item(c, b, r + 1 if r else 0))

                    def f(r):
                        if nxt:
                            feature(at(c, b, RI, RI + r), (b + 1 + r) % 2, feat[:, nb, r, :])

                    if nxt:
                        split(at(c, b, 1, 2), nb, 2 + 1 + at(c, b, 10, 1))
                    if norm_on:
                        norm(bass.ds(c + (b * NC + 1), 1), b)
                        dve.wait_ge(s["stat_done"], at(c, b, 1, 3))
                    masked(0)
                    if norm_on:
                        aggregate(b)
                    q_rope(0)
                    normalise(0)
                    if last(c, b):
                        for i in range(2 * FI // WCH):
                            self.split_chunk(dve, NW + i, i * WCH)
                            if i == 0:
                                masked(1)
                            if i == 1:
                                normalise(1)
                            if i == 2:
                                masked(2)
                            if i == 3:
                                normalise(2)
                    else:
                        masked(1)
                    if nxt:
                        keep_v(nb, (b + 1) % 2, proj_item(c, b, 1))
                    f(0)
                    if not last(c, b):
                        normalise(1)
                    if norm_on:
                        centre(bass.ds(c + (b * NC + 1), 1), at(c, b, 1, 3), b)
                    if not last(c, b):
                        masked(2)
                        q_rope(1)
                        normalise(2)
                    masked(3)
                    q_rope(2)
                    f(1)
                    normalise(3)
                    q_rope(3)
                    f(2)
                    dve.wait_ge(s["num_full"], at(c, b, KVH + 1, KVH + 1))
                    dve.tensor_tensor(state[:, b].rearrange("p (k h) w -> p k (h w)", k=2),
                                      num[:, :, 0:2 * VW], state[:, b].rearrange("p (k h) w -> p k (h w)", k=2),
                                      ALU.add).then_inc(s["num_free"], 1)
                    q_rope(4)
                    f(3)
                    if last(c, b):
                        dve.wait_ge(s["x_done"], NT - 1)
                        ffn_norms(dve, 0)
                        ffn_centre(dve, 0)
                    n = at(c, b, 7, 6) if last(c, b) else proj_item(c, b, 6)
                    dve.wait_ge(s["proj_full"], n + 1)
                    dve.tensor_tensor(dx[:], proj[:, b, 0:D],
                                      gate_b[:, 0, 0, b, :], ALU.mult).then_inc(s["proj_free"], 1)
                    dve.wait_ge(s["proj_free"], 2 + n + 1)
                    xt = x[:, bass.ds(c + b * NC, 1), :].rearrange("p o d -> p (o d)")
                    dve.tensor_tensor(xt, xt, dx[:], ALU.add).then_inc(s["x_done"], 1)
                    f(4)
                    dve.wait_ge(s["x_in"], 16 * B)

                walk(dve, step)

            @block.tensor
            def _(pe):
                pe.wait_ge(s["silu_done"], 1)
                pe.wait_ge(s["wmod_in"], 16)
                pe_vectors(pe, SA, GA, True)
                pe.wait_ge(s["const_made"], 1)

                def norm_turn(n, parity, bank, norms):
                    pe.wait_ge(s["xn_done"], norms)
                    pe.wait_ge(s["turn_free"], n + 1)
                    for k in range(KD):
                        t = pe.transpose(turn[:, bank, k * P:(k + 1) * P], xn[:, parity, k * P:(k + 1) * P], ident[:])
                    t.then_inc(s["turn_full"], 1)

                def project(parity, j, bank, n):
                    pe.wait_ge(s["proj_free"], n + 1)
                    cols = slice(j * 512, (j + 1) * 512)
                    passes = [(h_hi, w_hi), (h_hi, w_lo), (h_lo, w_hi)]
                    for i, (hh, ww) in enumerate(passes):
                        for k in range(KD):
                            mm = pe.matmul(proj[:, bank, :], hh[:, parity, k, :], ww[:, k, cols],
                                           start=(i == 0 and k == 0), stop=(i == 2 and k == KD - 1))
                    mm.then_inc(s["proj_full"], 1)

                norm_turn(0, 0, 0, 1)
                norm_turn(1, 1, 1, 2)
                pe.wait_ge(s["hl_done"], 1)
                for j in range(RI + 1):
                    pe.wait_ge(self.w_ready, j + 1)
                    project(0, j, j % 2, j)
                    if j == 3:
                        pe.wait_ge(s["wmod_ffn_in"], 16)
                        pe.wait_ge(msem["mod_kept"], 1)
                        pe_vectors(pe, SB_, GB, True)
                    if j == 4:
                        pe.wait_ge(s["wide_done"], 1)
                        pe_gates(pe)

                def step(c, b, nxt, norm_on):
                    tp = 1 if last(c, b) else 0

                    def bank(j):
                        return (j + tp) % 2

                    def turn4(j, src):
                        n = turn_item(c, b, j)
                        pe.wait_ge(s["turn_free"], n + 1)
                        for r in range(4):
                            t = pe.transpose(turn[:, bank(j), r * P:(r + 1) * P], src[:, r * P:(r + 1) * P], ident[:])
                        t.then_inc(s["turn_full"], 1)

                    def q_turn(g):
                        pe.wait_ge(s["feat_done"], at(c, b, RI, 2 + g))
                        turn4(1 + g, feat[:, b, 1 + g, :])

                    def scores(g):
                        pe.wait_ge(s["turn_free"], 2 + 1 + turn_item(c, b, 1 + g))
                        pe.wait_ge(s["score_free"], at(c, b, KVH, g + 1))
                        pe.matmul(score[:, g % 2, :], k_t[:, g, :], q_t[:, g, :], start=True, stop=True
                                  ).then_inc(s["score_full"], 1)

                    def numerators(g):
                        pe.wait_ge(s["score_free"], 2 + at(c, b, KVH, g + 1))
                        pe.wait_ge(s["num_free"], at(c, b, KVH + 1, g + 1))
                        for r in range(REP):
                            dst = num[:, r // 2, (r % 2) * VW:(r % 2 + 1) * VW]
                            pe.matmul(dst, am[:, g % 2, r * P:(r + 1) * P], v[:, b, g, :], start=True, stop=False)
                            mm = pe.matmul(dst, q_t[:, g, r * P:(r + 1) * P], state[:, b, g, :], start=False, stop=True)
                        mm.then_inc(s["num_full"], 1)

                    def out_turn(g):
                        pe.wait_ge(s["num_free"], 1 + at(c, b, KVH + 1, g + 1))
                        turn4(5 + g, on[:, g % 2, :])

                    def p(j):
                        if nxt:
                            project(1 - b, j, (b + j) % 2, proj_item(c, b, j))

                    pe.wait_ge(s["feat_done"], at(c, b, RI, 1))
                    turn4(0, feat[:, b, 0, :])
                    q_turn(0)
                    q_turn(1)
                    scores(0)
                    q_turn(2)
                    if nxt:
                        pe.wait_ge(s["hl_done"], at(c, b, 1, 2))
                    p(0)
                    numerators(0)
                    scores(1)
                    q_turn(3)
                    p(1)
                    numerators(1)
                    out_turn(0)
                    scores(2)
                    p(2)
                    numerators(2)
                    out_turn(1)
                    scores(3)
                    p(3)
                    numerators(3)
                    out_turn(2)
                    p(4)
                    pe.wait_ge(s["num_free"], at(c, b, KVH + 1, KVH + 1))
                    for g in range(KVH):
                        mm = pe.matmul(num[:, g // 2, (g % 2) * VW:(g % 2 + 1) * VW], feat[:, b, 0, g * P:(g + 1) * P],
                                       v[:, b, g, :], start=True, stop=True)
                    mm.then_inc(s["num_full"], 1)
                    out_turn(3)
                    p(5)
                    if norm_on:
                        norm_turn(turn_item(c, b, 9), b, bank(9), at(c, b, 1, 3))
                    n = at(c, b, 7, 6) if last(c, b) else proj_item(c, b, 6)
                    pe.wait_ge(s["proj_free"], n + 1)
                    pe.wait_ge(s["turn_free"], 2 + 1 + turn_item(c, b, 8))
                    pe.wait_ge(s["wo_in"], 16)
                    for i in range(H):
                        mm = pe.matmul(proj[:, b, 0:D], o_t[:, i, :], wo[:, i, :],
                                       start=(i == 0), stop=(i == H - 1))
                    mm.then_inc(s["proj_full"], 1)

                walk(pe, step)

    def ffn_phase(self):
        nc, a = self.nc, self.a
        x, ident, mod_t, gate_b = self.x, self.ident, self.mod_t, self.gate_b
        TOK = GT * P
        NQ = NM // 4
        self.small_in = self.sem("scan_small_in")
        self.scan_small = [self.keep.enter_context(nc.sbuf_tensor(n, shape, F32)) for n, shape in (
            ("t_cos", [P, NC, TD // 2]), ("t_sin", [P, NC, TD]), ("t_wo", [P, KD, D]), ("ln_gamma", [P, KD]),
            ("ln_beta", [P, KD]))]
        self.t_stats, self.t_mv, self.t_veps, self.t_rstd, self.t_xn, self.blocks, self.ident_n, self.rows_of = [
            self.keep.enter_context(nc.sbuf_tensor(n, shape, F32)) for n, shape in (
                ("t_stats", [P, 2, B, 6]), ("t_mv", [P, 2, B, 2]), ("t_veps", [P, 2, B]), ("t_rstd", [P, 2, B]),
                ("t_xn", [P, B, D]), ("head_blocks", [P, P]), ("ident_n", [P, P]), ("rows_of", [P, NMB]))]
        self.scan_s = {n: self.sem("t_" + n) for n in "x_stat x_aggr x_veps x_rstd xn_done const_step".split()}
        with ExitStack() as ctx:
            def sb(name, shape, dt=F32):
                return ctx.enter_context(nc.sbuf_tensor(name, shape, dt))

            def ps(name, shape, dt=F32):
                return ctx.enter_context(nc.psum_tensor(name, shape, dt))

            w_hi, w_lo = self.w_hi, self.w_lo
            wmod = sb("f_wmod", [P, KD, 6 * D])
            wd = sb("wd_sb", [P, NM, D])
            xn = self.g_xn
            h = sb("f_h", [P, KD, TOK])
            h_hi, h_lo = sb("f_h_hi", [P, 2, KD, TOK], F32R), sb("f_h_lo", [P, 2, KD, TOK], F32R)
            sg = sb("silu_gate", [P, 2, TOK])
            hid = sb("hidden", [P, 2, NM, TOK])
            mag = sb("magnitude", [P, NM, TOK])
            beats = sb("beats", [P, 6, TOK], BF16)
            wins = sb("wins", [P, 4, TOK], BF16)
            part = sb("wins_part", [P, 4, TOK], BF16)
            dx = sb("f_dx", [P, 2, D])
            turn = ps("f_turn", [P, 2, 512])
            gate, up = ps("gate_ps2", [P, 2, 512]), ps("up_ps", [P, 2, 512])
            rows = ps("f_rows", [P, 2, 512])

            s = self.ffn_s
            norms, rstd_of, centre = self.group_norm(s)
            scan_norm, scan_aggregate, scan_rstd, scan_centre = self.scan_norm_ops()
            msem = self.modulation_sems(1)
            scratch = hid[:].rearrange("p i m t -> p (i m t)")
            pe_vectors, pe_gates, dve_vectors, dve_gates, act_gates = self.modulation(
                1, wmod, self.scond, self.wide, msem, turn[:, 0, :], up[:],
                scratch[:, 0:2 * B * D].rearrange("p (i d) -> p i d", i=2),
                scratch[:, 2 * B * D:4 * B * D].rearrange("p (i d) -> p i d", i=2))
            WKV = self.wkv_col = 2 * FI
            NCH = QKV // WCH + 2 * FI // WCH
            self.chunks = NCH + 1
            self.stage_for(ctx, "f_stage", NCH, 1)
            block = ctx.enter_context(nc.Block())

            @block.sync
            def _(sp):
                sp.dma_start(wd[:], a["wd"].rearrange("(m p) n -> p m n", p=P)).then_inc(s["wd_in"], 16)
                sp.dma_start(wmod[:], a["wmod"][1].rearrange("(k p) n -> p k n", p=P)).then_inc(s["wmod_in"], 16)
                self.load_chunk(sp, NCH, a["wkv1"])
                cos, sin, wo, ln_g, ln_b = self.scan_small
                sp.dma_start(cos[:], a["cos1"].rearrange("(c p) d -> p c d", p=P)).then_inc(self.small_in, 16)
                sp.dma_start(sin[:], a["sin1"].rearrange("(c p) d -> p c d", p=P)).then_inc(self.small_in, 16)
                sp.dma_start(wo[:], a["wo1"].rearrange("(k p) n -> p k n", p=P)).then_inc(self.small_in, 16)
                with nc.allow_non_contiguous_dma(reason="two vectors of 256"):
                    sp.dma_start(ln_g[:], a["ln_g"].rearrange("(k p) -> p k", p=P)).then_inc(self.small_in, 16)
                    sp.dma_start(ln_b[:], a["ln_b"].rearrange("(k p) -> p k", p=P)).then_inc(self.small_in, 16)

            @block.gpsimd
            def _(pool):
                const_step = self.scan_s["const_step"]
                blocks, rows_of = self.blocks, self.rows_of
                rstd_of(pool, 1)
                pool.memset(blocks[:], INV_N).then_inc(const_step, 1)
                pool.memset(rows_of[:], 1.0).then_inc(const_step, 1)
                pool.memset(self.ident_n[:], 0.0).then_inc(const_step, 1)
                pool.wait_ge(const_step, 3)
                n = 3
                for base, sign in ((0, 1), (MB - 1, -1)):
                    for dst, pattern in ((blocks[:].rearrange("p (h e) -> p h e", e=TD), [[-sign * TD, P // TD], [0, TD]]),
                                         (rows_of[:], [[-sign * MB, NMB]])):
                        pool.affine_select(out=dst, in_=dst, compare_op=ALU.is_ge, fill=0.0, base=base,
                                           pattern=pattern, channel_multiplier=sign).then_inc(const_step, 1)
                    n += 2
                    pool.wait_ge(const_step, n)
                pool.affine_select(out=self.ident_n[:], in_=self.ident_n[:], compare_op=ALU.not_equal, fill=1.0 / INV_N,
                                   base=0, pattern=[[-1, P]], channel_multiplier=1).then_inc(const_step, 1)

                def add_rows(g):
                    for i in range(GT):
                        n = g * GT + i
                        pool.wait_ge(s["dx_done"], n + 1)
                        pool.tensor_tensor(x[:, n, :], x[:, n, :], dx[:, n % 2], ALU.add).then_inc(s["x_done"], 1)

                for g in range(NG):
                    if g + 2 < NG:
                        rstd_of(pool, g + 2)
                    if g:
                        add_rows(g - 1)
                for b in range(B):
                    scan_rstd(pool, b, 1)
                add_rows(NG - 1)

            @block.scalar
            def _(act):
                def drain_norm(g):
                    b = g * GT // NC
                    for k in range(KD):
                        act.wait_ge(s["turn_full"], KD * g + k + 1)
                        if g:
                            act.wait_ge(s["hl_done"], g)
                        act.activation(h[:, k, :], turn[:, k, :], ACT.Identity,
                                       bias=mod_t[:, 0, SB_ * KD + k, b:b + 1],
                                       scale=mod_t[:, 0, CB * KD + k, b:b + 1]).then_inc(s["h_done"], 1)

                def magnitude(g, m):
                    n = g * NM + m
                    act.wait_ge(s["hid_done"], n + 1)
                    if g:
                        act.wait_ge(s["pick_done"], NQ * (g - 1) + m // 4 + 1)
                    act.activation(mag[:, m], hid[:, g % 2, m], ACT.Abs).then_inc(s["mag_done"], 1)

                drain_norm(0)
                for g in range(NG):
                    for m in range(NM):
                        n = g * NM + m
                        act.wait_ge(s["gate_full"], n + 1)
                        if n >= 2:
                            act.wait_ge(s["hid_done"], n - 1)
                        act.activation(sg[:, n % 2], gate[:, n % 2, :], ACT.Silu).then_inc(s["silu_done"], 1)
                        if n:
                            magnitude((n - 1) // NM, (n - 1) % NM)
                        if m == 2 and g + 1 < NG:
                            drain_norm(g + 1)
                magnitude(NG - 1, NM - 1)
                act_gates(act)

            @block.vector
            def _(dve):
                def split(g):
                    dve.wait_ge(s["h_done"], KD * (g + 1))
                    dve.tensor_copy(h_hi[:, g % 2], h[:]).then_inc(s["hi_done"], 1)
                    dve.wait_ge(s["hi_done"], g + 1)
                    dve.tensor_tensor(h_lo[:, g % 2], h[:], h_hi[:, g % 2].bitcast(F32), ALU.subtract
                                      ).then_inc(s["hl_done"], 1)

                def pick(g, q):
                    m0 = 4 * q
                    pairs = [(0, 1), (0, 2), (0, 3), (1, 2), (1, 3), (2, 3)]
                    c = {pr: beats[:, i] for i, pr in enumerate(pairs)}

                    def op(f, need=0):
                        def go():
                            if need:
                                dve.wait_ge(s["pick_step"], base + need)
                            f().then_inc(s["pick_step"], 1)
                        return go

                    base = (g * NQ + q) * 14
                    ops = []
                    for i, (u, w) in enumerate(pairs):
                        def duel(i=i, u=u, w=w):
                            dve.wait_ge(s["mag_done"], g * NM + m0 + 4)
                            return dve.tensor_tensor(beats[:, i], mag[:, m0 + u], mag[:, m0 + w], ALU.is_ge)
                        ops.append(op(duel))
                    sums = [(0, c[0, 1], c[0, 2], ALU.add), (1, c[1, 2], c[0, 1], ALU.subtract),
                            (2, c[2, 3], c[0, 2], ALU.subtract), (3, c[0, 3], c[1, 3], ALU.add)]
                    for i, u, w, o in sums:
                        ops.append(op(lambda i=i, u=u, w=w, o=o: dve.tensor_tensor(part[:, i], u, w, o), 6))
                    ends = [(0, c[0, 3], ALU.add), (1, c[1, 3], ALU.add), (2, c[1, 2], ALU.subtract), (3, c[2, 3], ALU.add)]
                    for i, w, o in ends:
                        ops.append(op(lambda i=i, w=w, o=o: dve.tensor_tensor(wins[:, i], part[:, i], w, o), 7 + i))
                    tests = [(0, 2.0, ALU.is_ge), (1, 1.0, ALU.is_ge), (2, 0.0, ALU.is_ge), (3, 1.0, ALU.is_le)]
                    for i, bound, o in tests:
                        def keep(i=i, bound=bound, o=o):
                            dve.wait_ge(s["pick_step"], base + 11 + i)
                            t = hid[:, g % 2, m0 + i]
                            ins = dve.scalar_tensor_tensor(t, wins[:, i], bound, t, o, ALU.mult)
                            if i == 3:
                                ins.then_inc(s["pick_done"], 1)
                        ops.append(keep)
                    return ops

                def out_rows(g, i):
                    b = g * GT // NC
                    n = g * GT + i
                    dve.wait_ge(s["rows_full"], n + 1)
                    if n >= 2:
                        dve.wait_ge(s["x_done"], n - 1)
                    dve.tensor_tensor(dx[:, n % 2], rows[:, n % 2, 0:D], gate_b[:, 0, 1, b, :], ALU.mult
                                      ).then_inc(s["dx_done"], 1)

                norms(dve, 1)
                split(0)
                centre(dve, 1)
                ops = []
                for g in range(NG):
                    for m in range(NM):
                        n = g * NM + m
                        dve.wait_ge(s["up_full"], n + 1)
                        dve.wait_ge(s["silu_done"], n + 1)
                        if g >= 2 and m == 0:
                            dve.wait_ge(s["rows_full"], GT * (g - 1))
                        dve.tensor_tensor(hid[:, g % 2, m], up[:, n % 2, :], sg[:, n % 2], ALU.mult
                                          ).then_inc(s["hid_done"], 1)
                        if m % 4 == 0 and n:
                            ops = pick((n - 4) // NM, (n - 4) % NM // 4)
                        for o in ops[:5]:
                            o()
                        ops = ops[5:]
                        if g == 2 and m == 3:
                            self.split_chunk(dve, NCH, WKV)
                        norms_at, split_at, centre_at = (2, 3, 3) if g == 0 else (4, 5, 6)
                        if m == norms_at and g + 2 < NG:
                            norms(dve, g + 2)
                        if m == split_at and g + 1 < NG:
                            split(g + 1)
                        if m == centre_at and g + 2 < NG:
                            centre(dve, g + 2)
                        if m >= NM - GT and g:
                            out_rows(g - 1, m - (NM - GT))
                dve.wait_ge(msem["mod_full"], 2)
                dve_vectors(dve, SA, GA, 1)
                dve_vectors(dve, SB_, GB, 2)
                for o in pick(NG - 1, NQ - 1):
                    o()
                dve.wait_ge(s["x_done"], NC + 1)
                for b in range(B):
                    scan_norm(dve, 0, b)
                dve.wait_ge(self.scan_s["x_stat"], nth(1, 1))
                for b in range(B):
                    scan_aggregate(dve, b)
                for b in range(B):
                    scan_centre(dve, 0, b, 1)
                dve_gates(dve)
                for i in range(GT):
                    out_rows(NG - 1, i)

            @block.tensor
            def _(pe):
                def norm_turn(g):
                    pe.wait_ge(s["xn_done"], GT * (g + 1))
                    for k in range(KD):
                        if g:
                            pe.wait_ge(s["h_done"], KD * (g - 1) + k + 1)
                        for i in range(GT):
                            t = pe.transpose(turn[:, k, i * P:(i + 1) * P], xn[:, i, k * P:(k + 1) * P], ident[:])
                        t.then_inc(s["turn_full"], 1)

                def hidden(g, m):
                    n = g * NM + m
                    for dst, off, full, used in ((gate, 0, "gate_full", "silu_done"), (up, FI, "up_full", "hid_done")):
                        if n >= 2:
                            pe.wait_ge(s[used], n - 1)
                        cols = slice(off + m * P, off + (m + 1) * P)
                        for i, (ww, hh) in enumerate([(w_hi, h_hi), (w_lo, h_hi), (w_hi, h_lo)]):
                            for k in range(KD):
                                mm = pe.matmul(dst[:, n % 2, :], ww[:, k, cols], hh[:, g % 2, k, :],
                                               start=(i == 0 and k == 0), stop=(i == 2 and k == KD - 1))
                        mm.then_inc(s[full], 1)

                def down(g, i, ms=range(NM)):
                    pe.wait_ge(s["pick_done"], NQ * g + ms[-1] // 4 + 1)
                    n = g * GT + i
                    if n >= 2:
                        pe.wait_ge(s["dx_done"], n - 1)
                    for m in ms:
                        mm = pe.matmul(rows[:, n % 2, 0:D], hid[:, g % 2, m, i * P:(i + 1) * P], wd[:, m, :],
                                       start=(m == 0), stop=(m == NM - 1))
                    if ms[-1] == NM - 1:
                        mm.then_inc(s["rows_full"], 1)

                norm_turn(0)
                for g in range(NG):
                    pe.wait_ge(s["hl_done"], g + 1)
                    for m in range(NM):
                        hidden(g, m)
                        if m == 1 and g + 1 < NG:
                            norm_turn(g + 1)
                        if m >= NM - GT and g:
                            pe.wait_ge(s["wd_in"], 16)
                            down(g - 1, m - (NM - GT))
                pe.wait_ge(s["wmod_in"], 16)
                pe.wait_ge(s["h_done"], KD * NG)
                pe_vectors(pe, SA, GA, True)
                pe_vectors(pe, SB_, GB, False)
                pe.wait_ge(s["hid_done"], NG * NM)
                pe_gates(pe)
                for i in range(2):
                    down(NG - 1, i, range(NM // 2))
                for i in range(2):
                    down(NG - 1, i, range(NM // 2, NM))
                for i in range(2, GT):
                    down(NG - 1, i)

    def scan_phase(self):
        nc, a = self.nc, self.a
        x, ident, mod_t, gate_b, half, eps = self.x, self.ident, self.mod_t, self.gate_b, self.half, self.eps
        NH = E + 2
        self.moe_s = self.group_sems("m_", "const_made logit_full logit_kept top_step gate_step ratio_done gates_done "
                                     "gturn_full gturn_done hid_full act_done shared_full shared_kept expert_full "
                                     "acc_step dx_done x_done out_done")
        self.e_h, self.e_h_hi, self.e_h_lo = [
            self.keep.enter_context(nc.sbuf_tensor(n, shape, dt)) for n, shape, dt in (
                ("m_h", [P, KD, GT * P], F32), ("m_h_hi", [P, 2, KD, GT * P], F32R), ("m_h_lo", [P, 2, KD, GT * P], F32R))]
        self.moe_in = self.sem("moe_in")
        self.moe_small = [self.keep.enter_context(nc.sbuf_tensor(n, shape, F32)) for n, shape in (
            ("w2_sb", [P, NH, D]), ("b1_sb", [P, NH]), ("b2_sb", [E + 1, D]), ("gate_w_sb", [P, KD, E]))]
        with ExitStack() as ctx:
            def sb(name, shape, dt=F32):
                return ctx.enter_context(nc.sbuf_tensor(name, shape, dt))

            def ps(name, shape, dt=F32):
                return ctx.enter_context(nc.psum_tensor(name, shape, dt))

            w_cols = slice(self.wkv_col, self.wkv_col + 2 * D)
            w_hi, w_lo = self.w_hi[:, :, w_cols], self.w_lo[:, :, w_cols]
            cos, sin, wo, ln_g, ln_b = self.scan_small
            NCH = self.chunks
            blocks, ident_n, rows_of = self.blocks, self.ident_n, self.rows_of
            stats, mv, veps, rstd = self.t_stats, self.t_mv, self.t_veps, self.t_rstd
            xn, zn = self.t_xn, sb("t_zn", [P, B, D])
            h = sb("t_h", [P, B, KD, P])
            h_hi, h_lo = sb("t_h_hi", [P, B, KD, P], F32R), sb("t_h_lo", [P, B, KD, P], F32R)
            t1, t2 = sb("t_rope_cos", [P, B, D]), sb("t_rope_sin", [P, B, D])
            kr, v = sb("t_k", [P, B, D]), sb("t_v", [P, B, D])
            STEP = P + MB
            k_diag = sb("k_diag", [P, B, KD, NMB * STEP])
            k_rows = sb("k_rows", [P, B, NMB, D])
            u = sb("t_u", [P, B, D])
            w = sb("t_w", [P, B, KD, P])
            zs = sb("t_z", [P, B, D])
            o_t = sb("t_o", [P, B, KD, P])
            dx = sb("t_dx", [P, B, D])
            z_ps, g_ps = ps("z_ps", [P, B, 512]), ps("g_ps", [P, B, 512])
            proj, turn = ps("t_proj", [P, B, 512]), ps("t_turn", [P, B, 512])

            def sems(name):
                return self.sem("t_" + name)

            self.stage_for(ctx, "t_stage", NCH, 3)
            x_norm, x_aggregate, x_rstd_of, x_centre = self.scan_norm_ops()
            x_stat, xn_done = self.scan_s["x_stat"], self.scan_s["xn_done"]
            e_norms, e_rstd, e_centre = self.group_norm(self.moe_s)
            zeroed = self.sem("t_zeroed")
            z_full, u_done, g_full, w_done = sems("z_full"), sems("u_done"), sems("g_full"), sems("w_done")
            z_kept, v_kept, k_diag_done, k_rows_done = sems("z_kept"), sems("v_kept"), sems("kdiag"), sems("krows")
            z_stat, z_aggr, z_rstd, zn_done = sems("z_stat"), sems("z_aggr"), sems("z_rstd"), sems("zn_done")
            zv_done = sems("z_veps")
            xn_turned, zn_turned, k_turned = sems("xn_turned"), sems("zn_turned"), sems("k_turned")
            h_done, hi_done, hl_done, o_done = sems("h_done"), sems("hi_done"), sems("hl_done"), sems("o_done")
            proj_full, rope_done, kr_done = sems("proj_full"), sems("rope_done"), sems("kr_done")
            rows_full, dx_done, x_done = sems("rows_full"), sems("dx_done"), sems("x_done")
            block = ctx.enter_context(nc.Block())

            def tile(c, b):
                return bass.ds(c + b * NC, 1)

            def flat(ap):
                return ap.rearrange("p o d -> p (o d)")

            def walk(engine, step):
                step(0, False, True, True)
                with nc.Fori(1, NC - 2, engines=(engine.engine,), hint_back_edge=True) as c:
                    step(c, True, True, True)
                step(NC - 2, True, True, False)
                step(NC - 1, True, False, False)

            @block.sync
            def _(sp):
                w2, b1, b2, gw = self.moe_small
                sp.dma_start(gw[:], a["gw"].rearrange("(k p) n -> p k n", p=P)).then_inc(self.moe_in, 16)
                sp.dma_start(b1[:], a["b1"]).then_inc(self.moe_in, 16)
                sp.dma_start(b2[:], a["b2"]).then_inc(self.moe_in, 16)
                sp.dma_start(w2[:], a["w2"].rearrange("(m p) n -> p m n", p=P)).then_inc(self.moe_in, 16)
                for i in range(3):
                    w = min(WCH, NH * P - i * WCH)
                    self.load_chunk(sp, NCH + i, a["w1"][:, i * WCH:i * WCH + w], w)

            @block.gpsimd
            def _(pool):
                pool.memset(k_diag[:], 0.0).then_inc(zeroed, 1)

                def z_rstd_of(b, n):
                    pool.wait_ge(z_aggr, nth(b, n))
                    pool.tensor_tensor(veps[:, 1, b:b + 1], mv[:, 1, b, 1:2], eps[:], ALU.add).then_inc(zv_done, 1)
                    pool.wait_ge(zv_done, nth(b, n))
                    pool.tensor_tensor(rstd[:, 1, b:b + 1], veps[:, 1, b:b + 1], half[:], ALU.pow).then_inc(z_rstd, 1)

                def add_rope(b, n):
                    pool.wait_ge(rope_done, nth(b, n))
                    pool.tensor_tensor(kr[:, b], t1[:, b], t2[:, b], ALU.add).then_inc(kr_done, 1)

                def add_rows(c, b, n):
                    pool.wait_ge(dx_done, nth(b, n))
                    xt = flat(x[:, tile(c, b), :])
                    pool.tensor_tensor(xt, xt, dx[:, b], ALU.add).then_inc(x_done, 1)

                for b in range(B):
                    x_rstd_of(pool, b, 2)
                for b in range(B):
                    add_rope(b, 1)

                def step(c, prev, nxt, ahead):
                    if prev:
                        for b in range(B):
                            z_rstd_of(b, c)
                    if not nxt:
                        e_rstd(pool, 0)
                        for i in range(3):
                            self.chunk_low(pool, NCH + i, i * WCH, min(WCH, NH * P - i * WCH))
                    if nxt:
                        pool.wait_ge(k_rows_done, nth(0, (c + 1) * NMB))
                        add_rope(0, c + 2)
                    if ahead:
                        for b in range(B):
                            x_rstd_of(pool, b, c + 3)
                    if nxt:
                        pool.wait_ge(k_rows_done, nth(1, (c + 1) * NMB))
                        add_rope(1, c + 2)
                    if prev:
                        for b in range(B):
                            add_rows(c - 1, b, c)

                walk(pool, step)
                for b in range(B):
                    z_rstd_of(b, NC)
                for b in range(B):
                    add_rows(NC - 1, b, NC)

            @block.scalar
            def _(act):
                def spread(c, b, j, waited=True):
                    if waited:
                        act.wait_ge(g_full, nth(b, c * NMB + (j - NMB + 2)))
                    act.activation(k_rows[:, b, j], kr[:, b], ACT.Copy, scale=rows_of[:, j:j + 1]
                                   ).then_inc(k_rows_done, 1)

                def drain_norm(b, n):
                    act.wait_ge(xn_turned, nth(b, n))
                    for k in range(KD):
                        i = act.activation(h[:, b, k], turn[:, b, k * P:(k + 1) * P], ACT.Identity,
                                           bias=mod_t[:, 1, SA * KD + k, b:b + 1], scale=mod_t[:, 1, CA * KD + k, b:b + 1])
                    i.then_inc(h_done, 1)

                def drain_out(b, n):
                    act.wait_ge(zn_turned, nth(b, n))
                    for k in range(KD):
                        i = act.activation(o_t[:, b, k], turn[:, b, k * P:(k + 1) * P], ACT.Identity,
                                           bias=ln_b[:, k:k + 1], scale=ln_g[:, k:k + 1])
                    i.then_inc(o_done, 1)

                def keep_v(b, n):
                    act.wait_ge(rope_done, nth(b, n))
                    act.activation(v[:, b], proj[:, b, D:2 * D], ACT.Copy).then_inc(v_kept, 1)

                def spread_blocks(b, n, waited=True):
                    act.wait_ge(k_turned, nth(b, n))
                    if waited:
                        act.wait_ge(z_full, nth(b, (n - 1) * NMB))
                    act.activation(k_diag[:, b].rearrange("p k (m s) -> p k m s", s=STEP)[:, :, :, 0:MB],
                                   turn[:, b, 0:D].rearrange("p (k m s) -> p k m s", k=KD, s=MB),
                                   ACT.Copy).then_inc(k_diag_done, 1)

                act.wait_ge(self.small_in, 16 * 5)
                for b in range(B):
                    drain_norm(b, 1)
                act.wait_ge(zeroed, 1)
                for b in range(B):
                    keep_v(b, 1)
                    spread_blocks(b, 1, waited=False)
                for j in range(2):
                    for b in range(B):
                        act.wait_ge(kr_done, nth(b, 1))
                        spread(0, b, j, waited=False)

                def step(c, prev, nxt, ahead):
                    for j in (2, 3):
                        for b in range(B):
                            spread(c, b, j, waited=prev)
                    if nxt:
                        for b in range(B):
                            drain_norm(b, c + 2)
                    for j in range(4, NMB):
                        for b in range(B):
                            spread(c, b, j, waited=prev)
                    if prev:
                        for b in range(B):
                            drain_out(b, c)
                    if not nxt:
                        self.drain_group_norm(act, 0, proj)
                        for i in range(3):
                            self.chunk_high(act, NCH + i, i * WCH, min(WCH, NH * P - i * WCH))
                    if nxt:
                        for j in range(2):
                            for b in range(B):
                                act.wait_ge(kr_done, nth(b, c + 2))
                                spread(c + 1, b, j)
                        for b in range(B):
                            spread_blocks(b, c + 2)
                    for b in range(B):
                        act.wait_ge(u_done, nth(b, (c + 1) * NMB))
                        if prev:
                            act.wait_ge(zn_done, nth(b, c))
                        act.activation(zs[:, b], z_ps[:, b, 0:D], ACT.Copy).then_inc(z_kept, 1)
                        if nxt:
                            keep_v(b, c + 2)

                walk(act, step)
                for b in range(B):
                    drain_out(b, NC)

            @block.vector
            def _(dve):
                def z_norm(b, n):
                    dve.wait_ge(z_kept, nth(b, n))
                    dve.bn_stats(stats[:, 1, b, :], zs[:, b]).then_inc(z_stat, 1)

                def z_aggregate(b):
                    dve.bn_aggr(mv[:, 1, b, :], stats[:, 1, b, :]).then_inc(z_aggr, 1)

                def z_centre(b, n):
                    dve.wait_ge(z_rstd, nth(b, n))
                    dve.tensor_scalar(zn[:, b], zs[:, b], mv[:, 1, b, 0:1], rstd[:, 1, b:b + 1],
                                      ALU.subtract, ALU.mult).then_inc(zn_done, 1)

                def out_rows(b, n):
                    dve.wait_ge(rows_full, nth(b, n))
                    dve.tensor_tensor(dx[:, b], turn[:, b, D:2 * D], gate_b[:, 1, 0, b, :], ALU.mult).then_inc(dx_done, 1)

                def split(b, n):
                    dve.wait_ge(h_done, nth(b, n))
                    dve.tensor_copy(h_hi[:, b], h[:, b]).then_inc(hi_done, 1)
                    dve.wait_ge(hi_done, nth(b, n))
                    dve.tensor_tensor(h_lo[:, b], h[:, b], h_hi[:, b].bitcast(F32), ALU.subtract).then_inc(hl_done, 1)

                def rope(c, b, n, waited=True):
                    dve.wait_ge(proj_full, nth(b, n))
                    if waited:
                        dve.wait_ge(kr_done, nth(b, n - 1))
                    hd = TD // 2
                    k = proj[:, b, 0:D]
                    cc = flat(cos[:, bass.ds(c, 1), :]).unsqueeze(1).broadcast_to([P, 2 * TH, hd])
                    ss = sin[:, bass.ds(c, 1), :].rearrange("p o (u d) -> p (o u) d", u=2).unsqueeze(1)
                    dve.tensor_tensor(t1[:, b].rearrange("p (g d) -> p g d", d=hd),
                                      k.rearrange("p (g d) -> p g d", d=hd), cc, ALU.mult)
                    dve.tensor_tensor(t2[:, b].rearrange("p (g u d) -> p g u d", u=2, d=hd),
                                      k.rearrange("p (g u d) -> p g u d", u=2, d=hd)[:, :, ::-1, :],
                                      ss.broadcast_to([P, TH, 2, hd]), ALU.mult).then_inc(rope_done, 1)

                def new_w(b, n):
                    dve.wait_ge(g_full, nth(b, n))
                    dve.tensor_tensor(w[:, b], g_ps[:, b, 0:D].rearrange("p (k e) -> p k e", k=KD),
                                      blocks[:].unsqueeze(1).broadcast_to([P, KD, P]), ALU.mult).then_inc(w_done, 1)

                for b in range(B):
                    x_norm(dve, 1, b)
                dve.wait_ge(x_stat, nth(1, 2))
                for b in range(B):
                    x_aggregate(dve, b)
                for b in range(B):
                    split(b, 1)
                for b in range(B):
                    dve.wait_ge(xn_turned, nth(b, 1))
                    x_centre(dve, 1, b, 2)
                dve.wait_ge(self.small_in, 16 * 5)
                for b in range(B):
                    rope(0, b, 1, waited=False)
                for b in range(B):
                    new_w(b, 1)

                def step(c, prev, nxt, ahead):
                    for n in range(NMB):
                        for b in range(B):
                            dve.wait_ge(z_full, nth(b, c * NMB + (n + 1)))
                            if n == 0:
                                dve.wait_ge(v_kept, nth(b, c + 1))
                            if n == 1 and b == 0 and prev:
                                dve.wait_ge(z_stat, nth(1, c))
                            if n == 4 and b == 0 and ahead:
                                dve.wait_ge(x_stat, nth(1, c + 3))
                            dve.tensor_tensor(u[:, b], v[:, b], z_ps[:, b, 0:D], ALU.subtract).then_inc(u_done, 1)
                        if n == 1 and prev:
                            for b in range(B):
                                z_aggregate(b)
                        if n == 4 and ahead:
                            for b in range(B):
                                x_aggregate(dve, b)
                        for b in range(B):
                            new_w(b, c * NMB + (n + 2))
                        if n == 0 and prev:
                            for b in range(B):
                                z_norm(b, c)
                        if n == 1 and nxt:
                            for b in range(B):
                                split(b, c + 2)
                        if n == 2 and prev:
                            for b in range(B):
                                z_centre(b, c)
                        if n == 3 and nxt:
                            rope(c + 1, 0, c + 2)
                        if n == 3 and ahead:
                            for b in range(B):
                                x_norm(dve, c + 2, b)
                        if n == 5 and nxt:
                            rope(c + 1, 1, c + 2)
                        if n == 5 and prev:
                            out_rows(0, c)
                        if n == 5 and ahead:
                            for b in range(B):
                                x_centre(dve, c + 2, b, c + 3)
                        if n == 6 and prev:
                            out_rows(1, c)
                        if not nxt and n == 1:
                            dve.wait_ge(x_done, nth(1, GT))
                            e_norms(dve, 0)
                        if not nxt and n == 2:
                            e_centre(dve, 0)
                        if not nxt and n == 6:
                            self.split_group(dve, 0)

                walk(dve, step)
                for b in range(B):
                    z_norm(b, NC)
                dve.wait_ge(z_stat, nth(1, NC))
                for b in range(B):
                    z_aggregate(b)
                for b in range(B):
                    z_centre(b, NC)
                for b in range(B):
                    out_rows(b, NC)

            @block.tensor
            def _(pe):
                def norm_turn(b, n):
                    pe.wait_ge(xn_done, nth(b, n))
                    for k in range(KD):
                        t = pe.transpose(turn[:, b, k * P:(k + 1) * P], xn[:, b, k * P:(k + 1) * P], ident[:])
                    t.then_inc(xn_turned, 1)

                def out_turn(b, n):
                    pe.wait_ge(zn_done, nth(b, n))
                    for k in range(KD):
                        t = pe.transpose(turn[:, b, k * P:(k + 1) * P], zn[:, b, k * P:(k + 1) * P], ident[:])
                    t.then_inc(zn_turned, 1)

                def k_turn(b, n):
                    pe.wait_ge(kr_done, nth(b, n))
                    for k in range(KD):
                        t = pe.transpose(turn[:, b, k * P:(k + 1) * P], kr[:, b, k * P:(k + 1) * P], ident[:])
                    t.then_inc(k_turned, 1)

                def project(b, n, i):
                    hh, ww = [(h_hi, w_hi), (h_hi, w_lo), (h_lo, w_hi)][i]
                    if i == 0:
                        pe.wait_ge(hl_done, nth(b, n))
                    for k in range(KD):
                        mm = pe.matmul(proj[:, b, :], hh[:, b, k], ww[:, k, :],
                                       start=(i == 0 and k == 0), stop=(i == 2 and k == KD - 1))
                    if i == 2:
                        mm.then_inc(proj_full, 1)

                def out_rows(b, n):
                    pe.wait_ge(o_done, nth(b, n))
                    for k in range(KD):
                        mm = pe.matmul(turn[:, b, D:2 * D], o_t[:, b, k], wo[:, k, :], start=(k == 0), stop=(k == KD - 1))
                    mm.then_inc(rows_full, 1)

                for b in range(B):
                    for k in range(KD):
                        mm = pe.matmul(g_ps[:, b, k * P:(k + 1) * P], ident[:], ident_n[:], start=(k == 0), stop=False,
                                       skip_group_check=True)
                    mm.then_inc(g_full, 1)
                for b in range(B):
                    norm_turn(b, 1)
                for b in range(B):
                    for i in range(3):
                        project(b, 1, i)
                for b in range(B):
                    k_turn(b, 1)
                pe.wait_ge(self.small_in, 16 * 5)

                def step(c, prev, nxt, ahead):
                    def filler(n, end):
                        slot = 2 * n + end
                        if nxt:
                            if slot < 2:
                                norm_turn(slot, c + 2)
                            for b in range(B):
                                first = (2 * 2, 2 * 4)[b]
                                if first <= slot < first + 3:
                                    if slot == first:
                                        pe.wait_ge(v_kept, nth(b, c + 1))
                                    project(b, c + 2, slot - first)
                        if prev:
                            if slot == 7:
                                for b in range(B):
                                    if nxt:
                                        pe.wait_ge(h_done, nth(b, c + 2))
                                    out_turn(b, c)
                        if not nxt and slot == 6:
                            for b in range(B):
                                pe.wait_ge(v_kept, nth(b, NC))
                            self.turn_group(pe, 0, proj)
                        if prev:
                            if 11 <= slot < 13:
                                out_rows(slot - 11, c)
                        if nxt and 13 <= slot < 15:
                            if prev:
                                pe.wait_ge(dx_done, nth(slot - 13, c))
                            k_turn(slot - 13, c + 2)

                    for n in range(NMB):
                        for b in range(B):
                            pe.wait_ge(w_done, nth(b, c * NMB + (n + 1)))
                            if n == 0:
                                pe.wait_ge(k_diag_done, nth(b, c + 1))
                                if prev:
                                    pe.wait_ge(z_kept, nth(b, c))
                            for k in range(KD):
                                mm = pe.matmul(z_ps[:, b, k * P:(k + 1) * P], k_diag[:, b, k, n * P:(n + 1) * P],
                                               w[:, b, k], start=(n == 0 and k == 0), stop=(n == NMB - 1),
                                               skip_group_check=True)
                            mm.then_inc(z_full, 1)
                        filler(n, 0)
                        for b in range(B):
                            pe.wait_ge(u_done, nth(b, c * NMB + (n + 1)))
                            pe.wait_ge(k_rows_done, nth(b, c * NMB + (n + 1)))
                            for k in range(KD):
                                mm = pe.matmul(g_ps[:, b, k * P:(k + 1) * P], k_rows[:, b, n, k * P:(k + 1) * P],
                                               u[:, b, k * P:(k + 1) * P], start=False, stop=False, skip_group_check=True)
                            mm.then_inc(g_full, 1)
                        filler(n, 1)

                walk(pe, step)
                for b in range(B):
                    out_turn(b, NC)
                for b in range(B):
                    out_rows(b, NC)

    def turn_group(self, pe, g, turn):
        s = self.moe_s
        pe.wait_ge(s["xn_done"], GT * (g + 1))
        for k in range(KD):
            if g:
                pe.wait_ge(s["h_done"], KD * (g - 1) + k + 1)
            for i in range(GT):
                t = pe.transpose(turn[:, k, i * P:(i + 1) * P], self.g_xn[:, i, k * P:(k + 1) * P], self.ident[:])
            t.then_inc(s["turn_full"], 1)

    def drain_group_norm(self, act, g, turn):
        s, b = self.moe_s, g * GT // NC
        for k in range(KD):
            act.wait_ge(s["turn_full"], KD * g + k + 1)
            if g:
                act.wait_ge(s["hl_done"], g)
                act.wait_ge(s["logit_full"], g)
            act.activation(self.e_h[:, k, :], turn[:, k, :], ACT.Identity,
                           bias=self.mod_t[:, 1, SB_ * KD + k, b:b + 1],
                           scale=self.mod_t[:, 1, CB * KD + k, b:b + 1]).then_inc(s["h_done"], 1)

    def split_group(self, dve, g):
        s, h_hi = self.moe_s, self.e_h_hi[:, g % 2]
        dve.wait_ge(s["h_done"], KD * (g + 1))
        dve.tensor_copy(h_hi, self.e_h[:]).then_inc(s["hi_done"], 1)
        dve.wait_ge(s["hi_done"], g + 1)
        dve.tensor_tensor(self.e_h_lo[:, g % 2], self.e_h[:], h_hi.bitcast(F32), ALU.subtract
                          ).then_inc(s["hl_done"], 1)

    def moe_phase(self):
        nc = self.nc
        x, ident, gate_b = self.x, self.ident, self.gate_b
        TOK = GT * P
        NH = E + 2
        out = self.out.rearrange("b (c p) d -> p (b c) d", p=P)
        with ExitStack() as ctx:
            def sb(name, shape, dt=F32):
                return ctx.enter_context(nc.sbuf_tensor(name, shape, dt))

            def ps(name, shape, dt=F32):
                return ctx.enter_context(nc.psum_tensor(name, shape, dt))

            w_hi, w_lo = self.w_hi, self.w_lo
            w2, b1, b2, gw = self.moe_small
            h, h_hi, h_lo = self.e_h, self.e_h_hi, self.e_h_lo
            act_t = sb("m_act", [P, 2, NH, TOK])
            lg, top = sb("logits_sb", [P, GT, E]), sb("top", [P, GT, E])
            at_u, at_f = sb("top_at", [P, GT, E], U32), sb("top_at_f", [P, GT, 2])
            lane = sb("lane", [P, E])
            euler = sb("euler", [P, 1])
            diff, ratio = sb("logit_diff", [P, GT]), sb("gate_ratio", [P, GT])
            total, pair = sb("gate_total", [P, GT]), sb("gate_pair", [P, 2, GT])
            pick = sb("picked", [P, 2, GT, E])
            gates = sb("gates", [P, 2, GT, E + 1])
            gates_t = sb("gates_t", [E + 1, 2, GT, P])
            acc = sb("m_acc", [P, 2, D])
            dx = sb("m_dx", [P, 2, D])

            turn = ps("m_turn", [P, 2, 512])
            hid = ps("m_hid", [P, 2, 512])
            small = ps("m_small", [P, 512])
            shared = ps("m_shared", [P, 512])
            expert = ps("m_expert", [P, 2, 512])

            s = self.moe_s
            norms, rstd_of, centre = self.group_norm(s)
            block = ctx.enter_context(nc.Block())

            @block.sync
            def _(sp):
                for n in range(NT):
                    sp.wait_ge(s["x_done"], n + 1)
                    sp.dma_start(out[:, n, :], x[:, n, :]).then_inc(s["out_done"], 16)
                sp.wait_ge(s["out_done"], 16 * NT)

            @block.gpsimd
            def _(pool):
                pool.iota(lane[:], pattern=[[1, E]], base=0, channel_multiplier=0, allow_small_or_imprecise_dtypes=True)
                pool.memset(euler[:], float(np.e)).then_inc(s["const_made"], 1)

                def ratio_of(g):
                    pool.wait_ge(s["top_step"], 3 * g + 3)
                    pool.tensor_tensor(ratio[:], euler[:].broadcast_to([P, GT]), diff[:], ALU.pow).then_inc(s["ratio_done"], 1)

                def add_row(g, i):
                    n = g * GT + i
                    pool.wait_ge(s["dx_done"], n + 1)
                    pool.tensor_tensor(x[:, n, :], x[:, n, :], dx[:, n % 2], ALU.add).then_inc(s["x_done"], 1)

                pool.wait_ge(s["const_made"], 1)
                for g in range(-1, NG):
                    if g + 2 < NG:
                        rstd_of(pool, g + 2)
                    if g >= 0:
                        add_row(g, 0)
                    if g + 1 < NG:
                        ratio_of(g + 1)
                    for i in range(1, GT if g >= 0 else 0):
                        add_row(g, i)

            @block.scalar
            def _(act):
                def gates_turned(g):
                    act.wait_ge(s["gturn_full"], g + 1)
                    act.activation(gates_t[:, g % 2], small[0:E + 1, :].rearrange("p (i t) -> p i t", i=GT), ACT.Copy
                                   ).then_inc(s["gturn_done"], 1)

                def hidden(g, m):
                    n = g * NH + m
                    act.wait_ge(s["hid_full"], n + 1)
                    act.activation(act_t[:, g % 2, m], hid[:, n % 2, :], ACT.Gelu, bias=b1[:, m:m + 1]
                                   ).then_inc(s["act_done"], 1)

                def keep_shared(n):
                    act.wait_ge(s["shared_full"], n + 1)
                    if n >= 2:
                        act.wait_ge(s["dx_done"], n - 1)
                    act.activation(acc[:, n % 2], shared[:, 0:D], ACT.Copy).then_inc(s["shared_kept"], 1)

                act.wait_ge(self.moe_in, 16 * 4)
                for g in range(-1, NG):
                    for m in range(NH):
                        if g >= 0 and m % 2 == 1 and m // 2 < GT:
                            keep_shared(g * GT + m // 2)
                        if g + 1 < NG:
                            hidden(g + 1, m)
                        if m == 5 and g + 2 < NG:
                            self.drain_group_norm(act, g + 2, turn)
                    if g + 1 < NG:
                        gates_turned(g + 1)

            @block.vector
            def _(dve):
                def gating(g):
                    q = g % 2
                    dve.wait_ge(s["logit_full"], g + 1)
                    dve.tensor_copy(lg[:], small[:, 0:GT * E].rearrange("p (i e) -> p i e", e=E)).then_inc(s["logit_kept"], 1)
                    dve.wait_ge(s["logit_kept"], g + 1)
                    for i in range(GT):
                        t = dve.max(top[:, i], lg[:, i])
                    t.then_inc(s["top_step"], 1)
                    dve.wait_ge(s["top_step"], 3 * g + 1)
                    for i in range(GT):
                        t = dve.max_index(at_u[:, i], top[:, i], lg[:, i])
                    t.then_inc(s["top_step"], 1)
                    dve.tensor_tensor(diff[:], top[:, :, 1], top[:, :, 0], ALU.subtract).then_inc(s["top_step"], 1)
                    dve.wait_ge(s["top_step"], 3 * g + 3)
                    base = 6 * g
                    dve.tensor_copy(at_f[:], at_u[:, :, 0:2]).then_inc(s["gate_step"], 1)
                    dve.wait_ge(s["ratio_done"], g + 1)
                    dve.tensor_scalar(total[:], ratio[:], 1.0, None, ALU.add).then_inc(s["gate_step"], 1)
                    dve.wait_ge(s["gate_step"], base + 2)
                    dve.reciprocal(pair[:, 0], total[:]).then_inc(s["gate_step"], 1)
                    dve.wait_ge(s["gate_step"], base + 3)
                    dve.tensor_tensor(pair[:, 1], ratio[:], pair[:, 0], ALU.mult)
                    for k in range(2):
                        t = dve.tensor_tensor(pick[:, k], lane[:].unsqueeze(1).broadcast_to([P, GT, E]),
                                              at_f[:, :, k:k + 1].broadcast_to([P, GT, E]), ALU.is_equal)
                    t.then_inc(s["gate_step"], 1)
                    dve.wait_ge(s["gate_step"], base + 4)
                    for k in range(2):
                        t = dve.tensor_tensor(pick[:, k], pick[:, k], pair[:, k].unsqueeze(2).broadcast_to([P, GT, E]),
                                              ALU.mult)
                    t.then_inc(s["gate_step"], 1)
                    dve.wait_ge(s["gate_step"], base + 5)
                    dve.tensor_tensor(gates[:, q, :, 0:E], pick[:, 0], pick[:, 1], ALU.add).then_inc(s["gates_done"], 1)
                    dve.memset(total[:], 0.0).then_inc(s["gate_step"], 1)

                def weigh(g, i, k):
                    n = g * GT + i
                    dve.wait_ge(s["expert_full"], 4 * n + k + 1)
                    if k == 0:
                        dve.wait_ge(s["shared_kept"], n + 1)
                    for j in range(2):
                        e = 2 * k + j
                        if e:
                            dve.wait_ge(s["acc_step"], E * n + e)
                        ins = dve.scalar_tensor_tensor(acc[:, n % 2], expert[:, k % 2, j * D:(j + 1) * D],
                                                       gates[:, g % 2, i, e:e + 1], acc[:, n % 2], ALU.mult, ALU.add)
                        ins.then_inc(s["acc_step"], 1)

                def gate_rows(g, i):
                    n = g * GT + i
                    b = g * GT // NC
                    dve.wait_ge(s["acc_step"], E * (n + 1))
                    if n >= 2:
                        dve.wait_ge(s["x_done"], n - 1)
                    dve.tensor_tensor(dx[:, n % 2], acc[:, n % 2], gate_b[:, 1, 1, b, :], ALU.mult).then_inc(s["dx_done"], 1)

                dve.memset(gates[:], 1.0)
                dve.wait_ge(s["const_made"], 1)
                for g in range(-1, NG):
                    if g + 2 < NG:
                        norms(dve, g + 2)
                    for i in range(GT):
                        if g >= 0:
                            for k in range(E // 2):
                                weigh(g, i, k)
                            gate_rows(g, i)
                        if i == 0 and g + 1 < NG:
                            gating(g + 1)
                        if i == 1 and g + 2 < NG:
                            centre(dve, g + 2)
                    if g + 2 < NG:
                        self.split_group(dve, g + 2)

            @block.tensor
            def _(pe):
                def logits(g):
                    pe.wait_ge(s["h_done"], KD * (g + 1))
                    if g:
                        pe.wait_ge(s["gturn_done"], g)
                    for i in range(GT):
                        for k in range(KD):
                            mm = pe.matmul(small[:, i * E:(i + 1) * E], h[:, k, i * P:(i + 1) * P], gw[:, k, :],
                                           start=(k == 0), stop=(k == KD - 1))
                    mm.then_inc(s["logit_full"], 1)

                def gates_turn(g):
                    pe.wait_ge(s["gates_done"], g + 1)
                    for i in range(GT):
                        t = pe.transpose(small[0:E + 1, i * P:(i + 1) * P], gates[:, g % 2, i, :], ident[:])
                    t.then_inc(s["gturn_full"], 1)

                def hidden(g, m):
                    n = g * NH + m
                    if n >= 2:
                        pe.wait_ge(s["act_done"], n - 1)
                    cols = slice(m * P, (m + 1) * P)
                    for i, (ww, hh) in enumerate([(w_hi, h_hi), (w_lo, h_hi), (w_hi, h_lo)]):
                        for k in range(KD):
                            mm = pe.matmul(hid[:, n % 2, :], ww[:, k, cols], hh[:, g % 2, k, :],
                                           start=(i == 0 and k == 0), stop=(i == 2 and k == KD - 1))
                    mm.then_inc(s["hid_full"], 1)

                def shared_rows(g, i):
                    n = g * GT + i
                    if n:
                        pe.wait_ge(s["shared_kept"], n)
                    pe.wait_ge(s["gturn_done"], g + 1)
                    pe.wait_ge(s["act_done"], (g + 1) * NH)
                    pe.matmul(shared[:, 0:D], gates_t[:, g % 2, i, :], b2[:], start=True, stop=False)
                    for m in range(E, NH):
                        mm = pe.matmul(shared[:, 0:D], act_t[:, g % 2, m, i * P:(i + 1) * P], w2[:, m, :],
                                       start=False, stop=(m == NH - 1))
                    mm.then_inc(s["shared_full"], 1)

                def expert_rows(g, i, pairs):
                    n = g * GT + i
                    toks = slice(i * P, (i + 1) * P)
                    for k in pairs:
                        if 4 * n + k >= 2:
                            pe.wait_ge(s["acc_step"], 2 * (4 * n + k - 1))
                        for j in range(2):
                            e = 2 * k + j
                            mm = pe.matmul(expert[:, k % 2, j * D:(j + 1) * D], act_t[:, g % 2, e, toks], w2[:, e, :],
                                           start=True, stop=True)
                        mm.then_inc(s["expert_full"], 1)

                pe.wait_ge(self.moe_in, 16 * 4)
                pe.wait_ge(self.w_ready, self.chunks + 3)
                for g in range(-1, NG):
                    if g + 1 < NG:
                        pe.wait_ge(s["hl_done"], g + 2)
                    for m in range(NH):
                        i, part = (m - 1) // 2, (m - 1) % 2
                        if g >= 0 and 0 <= i < GT:
                            if part == 0:
                                shared_rows(g, i)
                            expert_rows(g, i, range(part * E // 4, (part + 1) * E // 4))
                        if g + 1 < NG:
                            hidden(g + 1, m)
                            if m == 0:
                                logits(g + 1)
                        if m == 5 and g + 2 < NG:
                            self.turn_group(pe, g + 2, turn)
                    if g + 1 < NG:
                        gates_turn(g + 1)


def rope_tables(length, dim):
    power = np.arange(0, dim, 2, dtype=np.float32) / np.float32(dim)
    inv_freq = np.float32(1.0) / np.power(10000.0, power.astype(np.float64)).astype(np.float32)
    angle = np.outer(np.arange(length, dtype=np.float32), inv_freq).astype(np.float32).astype(np.float64)
    sin = np.sin(angle)
    return np.cos(angle).astype(np.float32), np.concatenate([-sin, sin], axis=1).astype(np.float32)


def kernel(**inputs):
    import concourse.bacc as bacc
    from concourse.bass_utils import run_bass_kernel_spmd

    i = {k: np.asarray(v) for k, v in inputs.items()}
    cos, sin = rope_tables(S, HD)
    cos1, sin1 = rope_tables(S, TD)
    quads = np.arange(FI).reshape(FI // 512, P, 4).transpose(0, 2, 1).reshape(-1)
    arrays = {
        "x": i["L0_attn_x"],
        "cond": np.stack([i[f"L{n}_c"].T.reshape(KD, P, B).transpose(1, 0, 2) for n in range(2)], axis=1),
        "wmod": np.stack([i["L0_wmod"], i["L1_wmod"]]),
        "wqkv": np.concatenate([i["L0_attn_Wk"].T, i["L0_attn_Wv"].T, i["L0_attn_Wq"].T], axis=1),
        "wo": i["L0_attn_Wo"].T,
        "cos": cos, "sin": sin, "cos1": cos1, "sin1": sin1,
        "wgu": np.concatenate([i["L0_ffn_w_gate"][:, quads], i["L0_ffn_w_up"][:, quads]], axis=1),
        "wd": i["L0_ffn_w_down"][quads, :],
        "wkv1": np.concatenate([i["L1_attn_Wk"].T, i["L1_attn_Wv"].T], axis=1),
        "wo1": i["L1_attn_Wo"].T,
        "ln_g": i["L1_attn_ln_gamma"], "ln_b": i["L1_attn_ln_beta"],
        "gw": i["L1_ffn_gate_w"],
        "w1": np.concatenate([i["L1_ffn_w1"].transpose(1, 0, 2).reshape(D, E * EH), i["L1_ffn_shared_w1"]], axis=1),
        "b1": np.concatenate([i["L1_ffn_b1"], i["L1_ffn_shared_b1"].reshape(2, EH)], axis=0).T,
        "w2": np.concatenate([i["L1_ffn_w2"].reshape(E * EH, D), i["L1_ffn_shared_w2"]], axis=0),
        "b2": np.concatenate([i["L1_ffn_b2"], i["L1_ffn_shared_b2"][None]], axis=0),
    }
    arrays = {k: np.ascontiguousarray(v) for k, v in arrays.items()}
    nc = bacc.Bacc("TRN2", target_bir_lowering=False, num_devices=1)
    aps = {k: nc.dram_tensor(f"in_{k}", v.shape, mybir.dt.from_np(v.dtype), kind="ExternalInput").ap()
           for k, v in arrays.items()}
    out = nc.dram_tensor("out", (B, S, D), F32, kind="ExternalOutput").ap()
    build(nc, aps, out)
    r = run_bass_kernel_spmd(nc, [{f"in_{k}": v for k, v in arrays.items()}], core_ids=[0])
    return r.results[0]["out"]
```
